# Optimizing a Trainium2 kernel written in Bass

```python
import numpy as np
import jax
import jax.numpy as jnp

def _softmax(x, axis=-1):
    return jax.nn.softmax(x, axis=axis)

def _gelu(x):
    return jax.nn.gelu(x, approximate=True)

def _silu(x):
    return jax.nn.silu(x)

def _sigmoid(x):
    return jax.nn.sigmoid(x)

def _layernorm(x, axis=-1, eps=1e-05):
    m = jnp.mean(x, axis=axis, keepdims=True)
    v = jnp.var(x, axis=axis, keepdims=True)
    return (x - m) / jnp.sqrt(v + eps)

def _scatter_add(tgt, idx, src, axis=0):
    return tgt.at[idx].add(src)

def _segment_sum(src, seg, n):
    return jax.ops.segment_sum(src, seg, n)
kernel_name = 'mk_adj_ffn_d1_adj_r2_804fbf'

def setup_inputs(seed: int=0):
    np.random.seed(seed)
    _w = jnp.asarray

    def _rec_inputs():
        import jax
        import jax.numpy as jnp
        _gk = jax.random.key(seed)
        x = -0.0002928 + 1 * jax.random.normal(jax.random.fold_in(_gk, 1), (2048, 256), jnp.float32)
        _a = jax.random.bernoulli(jax.random.fold_in(_gk, 2), 0.000976562, (2048, 2048))
        adj = _a.astype(jnp.int32)
        return (x, adj)
    x, adj = _rec_inputs()

    def _L0_gnn_setup():
        import jax, jax.numpy as jnp
        import numpy as np
        N = 4096
        D_IN = 256
        D_OUT = 256
        key = jax.random.key(seed)
        k1, k2, k3, k4 = jax.random.split(key, 4)
        node_feats = jax.random.normal(k1, (N, D_IN), dtype=jnp.float32)
        adj_matrix = jax.random.randint(k2, (N, N), 0, 2, dtype=jnp.int32)
        w_self = jax.random.normal(k3, (D_OUT, D_IN), dtype=jnp.float32) * D_IN ** (-0.5)
        w_neigh = jax.random.normal(k4, (D_OUT, D_IN), dtype=jnp.float32) * D_IN ** (-0.5)
        return {'node_feats': node_feats, 'adj_matrix': adj_matrix, 'w_self': w_self, 'w_neigh': w_neigh}
    _L0_gnn_all = _L0_gnn_setup()
    _L0_gnn_in = {k: v for k, v in _L0_gnn_all.items() if k in ('w_self', 'w_neigh')}
    del _L0_gnn_all

    def _L0_ffn_setup():
        import jax, jax.numpy as jnp
        import numpy as np
        B, S, D, H, E = (4, 1024, 256, 8, 8)
        FF = 4 * D
        HD = D // H
        EPS = 1e-05

        def _layernorm(x, g, b):
            mu = jnp.mean(x, axis=-1, keepdims=True)
            var = jnp.mean((x - mu) ** 2, axis=-1, keepdims=True)
            return (x - mu) * jax.lax.rsqrt(var + EPS) * g + b
        key = jax.random.key(seed)
        ks = jax.random.split(key, 16)
        s = 0.02
        return {'x': jax.random.normal(ks[0], (B, S, D), dtype=jnp.float32), 'ln1_g': jnp.ones((D,), jnp.float32), 'ln1_b': jnp.zeros((D,), jnp.float32), 'Wq': jax.random.normal(ks[1], (D, D), jnp.float32) * s, 'bq': jnp.zeros((D,), jnp.float32), 'Wk': jax.random.normal(ks[2], (D, D), jnp.float32) * s, 'bk': jnp.zeros((D,), jnp.float32), 'Wv': jax.random.normal(ks[3], (D, D), jnp.float32) * s, 'bv': jnp.zeros((D,), jnp.float32), 'Wo': jax.random.normal(ks[4], (D, D), jnp.float32) * s, 'bo': jnp.zeros((D,), jnp.float32), 'gate_W': jax.random.normal(ks[5], (D, E), jnp.float32) * s, 'gate_b': jnp.zeros((E,), jnp.float32), 'W1': jax.random.normal(ks[6], (E, D, FF), jnp.float32) * s, 'b1': jnp.zeros((E, FF), jnp.float32), 'W2': jax.random.normal(ks[7], (E, FF, D), jnp.float32) * s, 'b2': jnp.zeros((E, D), jnp.float32)}
    _L0_ffn_all = _L0_ffn_setup()
    _L0_ffn_in = {k: v for k, v in _L0_ffn_all.items() if k in ('ln1_g', 'ln1_b', 'Wq', 'bq', 'Wk', 'bk', 'Wv', 'bv', 'Wo', 'bo', 'gate_W', 'gate_b', 'W1', 'b1', 'W2', 'b2')}
    del _L0_ffn_all
    return {'x': x, 'adj': adj, 'L0_gnn_w_self': _L0_gnn_in['w_self'], 'L0_gnn_w_neigh': _L0_gnn_in['w_neigh'], 'L0_ffn_ln1_g': _L0_ffn_in['ln1_g'], 'L0_ffn_ln1_b': _L0_ffn_in['ln1_b'], 'L0_ffn_Wq': _L0_ffn_in['Wq'], 'L0_ffn_bq': _L0_ffn_in['bq'], 'L0_ffn_Wk': _L0_ffn_in['Wk'], 'L0_ffn_bk': _L0_ffn_in['bk'], 'L0_ffn_Wv': _L0_ffn_in['Wv'], 'L0_ffn_bv': _L0_ffn_in['bv'], 'L0_ffn_Wo': _L0_ffn_in['Wo'], 'L0_ffn_bo': _L0_ffn_in['bo'], 'L0_ffn_gate_W': _L0_ffn_in['gate_W'], 'L0_ffn_gate_b': _L0_ffn_in['gate_b'], 'L0_ffn_W1': _L0_ffn_in['W1'], 'L0_ffn_b1': _L0_ffn_in['b1'], 'L0_ffn_W2': _L0_ffn_in['W2'], 'L0_ffn_b2': _L0_ffn_in['b2']}

def reference(x, adj, L0_gnn_w_self, L0_gnn_w_neigh, L0_ffn_ln1_g, L0_ffn_ln1_b, L0_ffn_Wq, L0_ffn_bq, L0_ffn_Wk, L0_ffn_bk, L0_ffn_Wv, L0_ffn_bv, L0_ffn_Wo, L0_ffn_bo, L0_ffn_gate_W, L0_ffn_gate_b, L0_ffn_W1, L0_ffn_b1, L0_ffn_W2, L0_ffn_b2):
    import jax
    import jax.numpy as jnp

    def _L0_gnn_ref(node_feats, adj_matrix, w_self, w_neigh):
        import jax, jax.numpy as jnp
        import numpy as np
        N = 4096
        D_IN = 256
        D_OUT = 256
        adj_f = adj_matrix.astype(node_feats.dtype)
        s = adj_f @ node_feats[:, 0]
        has_neigh = jnp.sum(adj_matrix, axis=1) > 0
        s = jnp.where(has_neigh, s, jnp.zeros_like(s))
        neigh_term = s[:, None] * jnp.sum(w_neigh, axis=1)[None, :]
        return jax.nn.relu(node_feats @ w_self.T + neigh_term)

    def _L0_ffn_ref(x, ln1_g, ln1_b, Wq, bq, Wk, bk, Wv, bv, Wo, bo, gate_W, gate_b, W1, b1, W2, b2):
        import jax, jax.numpy as jnp
        import numpy as np
        B, S, D, H, E = (4, 1024, 256, 8, 8)
        FF = 4 * D
        HD = D // H
        EPS = 1e-05

        def _layernorm(x, g, b):
            mu = jnp.mean(x, axis=-1, keepdims=True)
            var = jnp.mean((x - mu) ** 2, axis=-1, keepdims=True)
            return (x - mu) * jax.lax.rsqrt(var + EPS) * g + b
        b, s, d = x.shape
        q = (x @ Wq + bq).reshape(b, s, H, HD)
        k = (x @ Wk + bk).reshape(b, s, H, HD)
        v = (x @ Wv + bv).reshape(b, s, H, HD)
        scores = jnp.einsum('bqhd,bkhd->bhqk', q, k) / jnp.sqrt(jnp.float32(HD))
        attn = jax.nn.softmax(scores, axis=-1)
        o = jnp.einsum('bhqk,bkhd->bqhd', attn, v).reshape(b, s, d) @ Wo + bo
        h = _layernorm(x + o, ln1_g, ln1_b)
        t = h.reshape(b * s, d)
        probs = jax.nn.softmax(t @ gate_W + gate_b, axis=-1)
        idx = jnp.argmax(probs, axis=-1)
        gw = jnp.max(probs, axis=-1)
        hid = jax.nn.gelu(jnp.einsum('nd,edf->enf', t, W1) + b1[:, None, :])
        out_all = jnp.einsum('enf,efd->end', hid, W2) + b2[:, None, :]
        onehot = jax.nn.one_hot(idx, E, dtype=t.dtype)
        out = jnp.einsum('ne,end->nd', onehot, out_all)
        out = out * gw[:, None]
        return out.reshape(b, s, d)
    x = x + _L0_gnn_ref(_layernorm(x, axis=-1), adj, L0_gnn_w_self, L0_gnn_w_neigh)
    x = x + _L0_ffn_ref(_layernorm(x, axis=-1)[None], L0_ffn_ln1_g, L0_ffn_ln1_b, L0_ffn_Wq, L0_ffn_bq, L0_ffn_Wk, L0_ffn_bk, L0_ffn_Wv, L0_ffn_bv, L0_ffn_Wo, L0_ffn_bo, L0_ffn_gate_W, L0_ffn_gate_b, L0_ffn_W1, L0_ffn_b1, L0_ffn_W2, L0_ffn_b2)[0]
    return x

_drawn_inputs = setup_inputs


def setup_inputs(seed=0):
    import zlib

    import numpy as np

    out = dict(_drawn_inputs(seed))
    spreads = {'L0_ffn_ln1_g': (1.0, 0.6),
     'L0_ffn_ln1_b': (0.0, 0.8),
     'L0_ffn_bq': (0.0, 0.8),
     'L0_ffn_bk': (0.0, 0.8),
     'L0_ffn_bv': (0.0, 0.8),
     'L0_ffn_bo': (0.0, 0.8),
     'L0_ffn_gate_b': (0.0, 0.618),
     'L0_ffn_b1': (0.0, 0.8),
     'L0_ffn_b2': (0.0, 0.579)}
    factors = {'L0_ffn_Wq': 8.0,
     'L0_ffn_Wk': 8.0,
     'L0_ffn_Wv': 8.0,
     'L0_ffn_Wo': 8.0,
     'L0_ffn_gate_W': 2.848,
     'L0_ffn_W1': 3.525,
     'L0_ffn_W2': 3.368}
    for name, (base, spread) in spreads.items():
        noise = np.random.default_rng([zlib.crc32(name.encode()), seed]).standard_normal(out[name].shape)
        drawn = base * np.exp(spread * noise) if base else spread * noise
        out[name] = jnp.asarray(drawn.astype(out[name].dtype))
    for name, factor in factors.items():
        out[name] = (out[name] * factor).astype(out[name].dtype)
    return out
```

```python
import concourse.bass as bass
from concourse import mybir
from contextlib import ExitStack

F32 = mybir.dt.float32
F16 = mybir.dt.float16
I32 = mybir.dt.int32
U32 = mybir.dt.uint32
ALU = mybir.AluOpType
ACT = mybir.ActivationFunctionType
AX = mybir.AxisListType

P = 128
N = 2048
D = 256
H = 8
HD = D // H
E = 8
FF = 4 * D
NT = N // P
KC = D // P
FC = FF // P
GT = 4
NG = NT // GT
GW = GT * P
SLOTS = (N + E * (P - 1)) // P
EPS = 1e-5
QS = 16.0
MS = QS * QS
SCALE = float(HD) ** -0.5
TS = 16.0
WS = 64.0
HVW = HD + 1
PR = 8


class Link:

    def __init__(self, eng, sem):
        self.eng, self.sem, self.base, self.n, self.most = eng, sem, 0, 0, 0

    def at(self, base):
        self.base, self.n = base, 0

    def __call__(self, ins):
        self.n += 1
        ins.then_inc(self.sem, 1)
        self.eng.wait_ge(self.sem, self.base + self.n)


def from_zero(eng, body, end):
    body(0)
    with eng.Fori(1, end) as i:
        body(i)


def wait(eng, sem, value):
    if isinstance(value, int):
        if value > 0:
            eng.wait_ge(sem, value)
    else:
        eng.wait_ge(sem, value)


def phase_project(nc, T, dr):
    with ExitStack() as ctx:
        def sb(name, shape, dt=F32):
            return ctx.enter_context(nc.sbuf_tensor(name, shape, dt))

        def ps(name):
            return ctx.enter_context(nc.psum_tensor(name, [P, 512], F32))

        def sem(name):
            return ctx.enter_context(nc.semaphore(name))

        ident, v_all = T["ident"], T["v_all"]
        x_all = sb("x_all", [P, NT, D])
        adj_b = sb("adj_b", [P, GT, N], I32)
        xn0 = sb("xn0", [P, N])
        junk_v = sb("junk_v", [P, N])
        junk_a = sb("junk_a", [P, N])
        ones = sb("ones_a", [P, P])
        ws, wn = sb("ws", [P, KC, D]), sb("wn", [P, KC, D])
        wq, wk, wv = sb("wq", [P, KC, D]), sb("wk", [P, KC, D]), sb("wv", [P, KC, D])
        bqk = sb("bqk", [P, 2, KC])
        bqk_s = sb("bqk_s", [P, 2, KC])
        ws_t = sb("ws_t", [P, KC, D])
        wn_col = sb("wn_col", [P, KC])
        wn_diag = sb("wn_diag", [P, KC, P])
        wn_bc = sb("wn_bc", [P, D])
        stats = sb("stats", [P, NT, 6])
        mean, rstd, nmr = sb("mean", [P, NT]), sb("rstd", [P, NT]), sb("nmr", [P, NT])
        half, col0 = sb("half", [P, NT]), sb("col0", [P, NT])
        xn_b = sb("xn_b", [P, 2, D])
        xnt_b = sb("xnt_b", [P, 2, KC, P])
        s_col, r_col, sg_col = sb("s_col", [P, GT]), sb("r_col", [P, GT]), sb("sg_col", [P, GT])
        z_b = sb("z_b", [P, D])
        x1_b, xn2_b = sb("x1_b", [P, 2, D]), sb("xn2_b", [P, 2, D])
        st2, mv2, ve2, rs2, nm2 = sb("st2", [P, 6]), sb("mv2", [P, 2]), sb("ve2", [P, 1]), sb("rs2", [P, 1]), sb("nm2", [P, 1])
        xn2_t = sb("xn2_t", [P, KC, GW])
        qk32 = sb("qk32", [P, 2, GW])
        qk16 = sb("qk16", [P, 2, 2, GW], F16)
        zero_b = sb("zero_b", [P, D])
        diag = junk_v[:, :].rearrange("p (t q) -> p t q", t=NT)

        ps_t1, ps_t2, ps_v = ps("ps_t1"), ps("ps_t2"), ps("ps_v")
        ps_g = [ps("ps_g0"), ps("ps_g1")]
        ps_q = [ps("ps_q0"), ps("ps_q1")]
        ps_x = ps("ps_x")

        x_in, w_in, b_in = sem("x_in"), sem("w_in"), sem("b_in")
        adj_in = [sem(f"adj_in{j}") for j in range(GT)]
        row_stats = sem("row_stats_a")
        consts, dve_chain, zeroed = sem("consts_a"), sem("dve_chain_a"), sem("zeroed")
        xn0_diag, wn_diag_s = sem("xn0_diag"), sem("wn_diag_s")
        spread, spread_out = sem("spread"), sem("spread_out")
        var_ready, rstd_ready = sem("var_ready"), sem("rstd_ready")
        xn_ready, xn_turned, xnt_ready = sem("xn_ready"), sem("xn_turned"), sem("xnt_ready")
        self_done, z_done = sem("self_done"), sem("z_done")
        adj_summed, adj_counted = sem("adj_summed"), sem("adj_counted")
        x1_ready, xn2_ready, xn2_turned, xn2t_ready = sem("x1_ready"), sem("xn2_ready"), sem("xn2_turned"), sem("xn2t_ready")
        v_done, v_out = sem("v_done"), sem("v_out")
        qk_done, qk_hi, qk_split = sem("qk_done"), sem("qk_hi"), sem("qk_split")
        tile_stored = [sem("tile_stored0"), sem("tile_stored1")]
        qk_stored = [sem("qk_stored0"), sem("qk_stored1")]
        block = ctx.enter_context(nc.Block())

        N_WEIGHTS = 5
        N_SPREAD = NG + 2

        @block.sync
        def _(sp):
            sp.dma_start(x_all[:, :, :], dr["x"].rearrange("(t p) d -> p t d", p=P)).then_inc(x_in, 16)
            for j in range(GT):
                sp.dma_start(adj_b[:, j, :], dr["adj"][j * P:(j + 1) * P, :]).then_inc(adj_in[j], 16)
                if j == 0:
                    for w, src in ((ws, "w_self"), (wn, "w_neigh"), (wq, "Wq"), (wk, "Wk"), (wv, "Wv")):
                        sp.dma_start(w[:, :, :], dr[src].rearrange("(c p) d -> p c d", p=P)).then_inc(w_in, 16)
                    for n, src in enumerate(("bq", "bk")):
                        sp.dma_start(bqk[:, n, :], dr[src].rearrange("(c p) -> p c", p=P),
                                     allow_slow_non_contiguous=True).then_inc(b_in, 16)

            def store_tile(g, j):
                rows = bass.ds(g * GW + j * P, P)
                sp.wait_ge(x1_ready, g * GT + (j + 1))
                sp.dma_start(dr["x1"][rows, :], x1_b[:, j % 2, :]).then_inc(tile_stored[j % 2], 16)
                sp.wait_ge(xn2_ready, g * GT + (j + 1))
                sp.dma_start(dr["xn2"][rows, :], xn2_b[:, j % 2, :]).then_inc(tile_stored[j % 2], 16)

            def store_group(g):
                cols = bass.ds(g * GW if isinstance(g, int) else sp.snap(g * GW), GW)
                for c in range(2 * KC):
                    sp.wait_ge(qk_split, g * (2 * KC) + (c + 1))
                    dst = dr["qh"] if c < KC else dr["kh"]
                    for part in (1, 0):
                        sp.dma_start(dst[part, (c % KC) * P:(c % KC + 1) * P, cols],
                                     qk16[:, c % 2, part, :]).then_inc(qk_stored[c % 2], 16)

            with sp.Fori(1, NG) as g:
                for j in range(GT):
                    sp.wait_ge(adj_summed, g * GT + (j - GT + 1))
                    sp.wait_ge(adj_counted, g * GT + (j - GT + 1))
                    sp.dma_start(adj_b[:, j, :], dr["adj"][bass.ds(g * GW + j * P, P), :]).then_inc(adj_in[j], 16)
                    store_tile(g - 1, j)
                store_group(g - 1)
            for j in range(GT):
                store_tile(NG - 1, j)
            store_group(NG - 1)
            for n in range(2):
                sp.wait_ge(tile_stored[n], NT * 16)
                sp.wait_ge(qk_stored[n], NG * 4 * 16)

        @block.gpsimd
        def _(pool):
            nc.gpsimd.memset(ident[:, :], 0.0).then_inc(zeroed, 1)
            nc.gpsimd.memset(ones[:, :], 1.0).then_inc(consts, 1)
            nc.gpsimd.memset(v_all[:, :, :, HD:HVW], 1.0).then_inc(consts, 1)
            nc.gpsimd.memset(T["minus_half"][:, :], -0.5).then_inc(consts, 1)
            nc.gpsimd.memset(zero_b[:, :], 0.0).then_inc(zeroed, 1)
            pool.wait_ge(zeroed, 2)
            nc.gpsimd.affine_select(out=ident[:, :], in_=ident[:, :], compare_op=ALU.not_equal, fill=1.0,
                                    base=0, pattern=[[-1, P]], channel_multiplier=1).then_inc(consts, 1)
            pool.dma_start(dr["hs"].rearrange("(s p) d -> p s d", p=P),
                           zero_b[:, :].unsqueeze(1).to_broadcast([P, SLOTS, D])).then_inc(T["hs_cleared"], 16)
            pool.wait_ge(consts, 4)
            pool.wait_ge(var_ready, 1)
            nc.gpsimd.tensor_tensor(rstd[:, :], rstd[:, :], T["minus_half"][:, :], ALU.pow).then_inc(rstd_ready, 1)
            def body(g):
                for j in range(GT):
                    wait(pool, var_ready, g * GT + (j + 2))
                    nc.gpsimd.tensor_tensor(rs2[:, :], ve2[:, :], T["minus_half"][:, 0:1], ALU.pow).then_inc(rstd_ready, 1)
                for c in range(2 * KC):
                    wait(pool, qk_hi, g * (2 * KC) + (c + 1))
                    if c >= 2:
                        wait(pool, qk_stored[c % 2], g * (4 * 16) + 32)
                    else:
                        wait(pool, qk_stored[c % 2], g * (4 * 16))
                    nc.gpsimd.tensor_tensor(qk16[:, c % 2, 1, :], qk32[:, c % 2, :], qk16[:, c % 2, 0, :],
                                            ALU.subtract).then_inc(qk_split, 1)

            from_zero(pool, body, NG)
            pool.wait_ge(T["hs_cleared"], 16)

        @block.vector
        def _(dve):
            link = Link(dve, dve_chain)
            dve.wait_ge(x_in, 16)
            with dve.Fori(0, NT) as t:
                nc.vector.bn_stats(stats[:, bass.ds(t, 1), :].rearrange("p a s -> p (a s)"),
                                   x_all[:, bass.ds(t, 1), :].rearrange("p a d -> p (a d)")).then_inc(dve_chain, 1)
            link.at(NT)
            dve.wait_ge(dve_chain, NT)
            link(nc.vector.tensor_tensor(mean[:, :], stats[:, :, 1], stats[:, :, 4], ALU.add))
            link(nc.vector.tensor_scalar(mean[:, :], mean[:, :], 0.5, None, ALU.mult))
            link(nc.vector.tensor_tensor(half[:, :], stats[:, :, 1], mean[:, :], ALU.subtract))
            link(nc.vector.tensor_tensor(half[:, :], half[:, :], half[:, :], ALU.mult))
            link(nc.vector.tensor_tensor(rstd[:, :], stats[:, :, 2], stats[:, :, 5], ALU.add))
            link(nc.vector.scalar_tensor_tensor(rstd[:, :], rstd[:, :], 1.0 / D, half[:, :], ALU.mult, ALU.add))
            nc.vector.tensor_scalar(rstd[:, :], rstd[:, :], EPS, None, ALU.add).then_inc(var_ready, 1)
            dve.wait_ge(rstd_ready, 1)
            link(nc.vector.scalar_tensor_tensor(nmr[:, :], mean[:, :], -1.0, rstd[:, :], ALU.mult, ALU.mult))
            link(nc.vector.tensor_tensor(col0[:, :], x_all[:, :, 0], rstd[:, :], ALU.mult))
            link(nc.vector.tensor_tensor(col0[:, :], col0[:, :], nmr[:, :], ALU.add))
            dve.wait_ge(consts, 4)
            nc.vector.tensor_tensor(diag, ident[:, :].unsqueeze(1).to_broadcast([P, NT, P]),
                                    col0[:, :].unsqueeze(2).to_broadcast([P, NT, P]), ALU.mult).then_inc(xn0_diag, 1)
            dve.wait_ge(w_in, 16 * N_WEIGHTS)
            link(nc.vector.tensor_reduce(wn_col[:, :], wn[:, :, :], AX.X, ALU.add))
            nc.vector.tensor_tensor(wn_diag[:, :, :], ident[:, :].unsqueeze(1).to_broadcast([P, KC, P]),
                                    wn_col[:, :].unsqueeze(2).to_broadcast([P, KC, P]), ALU.mult).then_inc(wn_diag_s, 1)
            dve.wait_ge(spread_out, N_SPREAD)
            START, PER = link.base + link.n, 3
            def body(g):
                for j in range(GT):
                    link.at(g * (GT * PER) + (START + j * PER))
                    one = bass.ds(g * GT + j, 1)
                    x_t = x_all[:, one, :].rearrange("p a d -> p (a d)")
                    if j >= 2:
                        wait(dve, xn_turned, g * GT + (j - 1))
                    else:
                        wait(dve, xn_turned, g * GT)
                    nc.vector.tensor_scalar(xn_b[:, j % 2, :], x_t, rstd[:, one], nmr[:, one],
                                            ALU.mult, ALU.add).then_inc(xn_ready, 1)
                    wait(dve, adj_in[j], g * 16 + 16)
                    nc.vector.tensor_tensor_reduce(out=junk_v[:, :], in0=adj_b[:, j, :], in1=xn0[:, :], scale=1.0,
                                                   scalar=0.0, op0=ALU.mult, op1=ALU.add,
                                                   accum_out=s_col[:, j:j + 1]).then_inc(adj_summed, 1)
                    wait(dve, adj_summed, g * GT + (j + 1))
                    wait(dve, adj_counted, g * GT + (j + 1))
                    link(nc.vector.scalar_tensor_tensor(sg_col[:, j:j + 1], r_col[:, j:j + 1], 0.0,
                                                        s_col[:, j:j + 1], ALU.is_gt, ALU.mult))
                    wait(dve, self_done, g * GT + (j + 1))
                    nc.vector.scalar_tensor_tensor(z_b[:, :], wn_bc[:, :], sg_col[:, j:j + 1], ps_g[j % 2][:, 0:D],
                                                   ALU.mult, ALU.add).then_inc(z_done, 1)
                    wait(dve, z_done, g * GT + (j + 1))
                    if j >= 2:
                        wait(dve, tile_stored[j % 2], g * 64 + 32)
                    else:
                        wait(dve, tile_stored[j % 2], g * 64)
                    nc.vector.scalar_tensor_tensor(x1_b[:, j % 2, :], z_b[:, :], 0.0, x_t,
                                                   ALU.max, ALU.add).then_inc(x1_ready, 1)
                    wait(dve, x1_ready, g * GT + (j + 1))
                    nc.vector.bn_stats(st2[:, :], x1_b[:, j % 2, :]).then_inc(row_stats, 1)
                    dve.wait_ge(row_stats, 1)
                    dve.sem_clear(row_stats)
                    link(nc.vector.bn_aggr(mv2[:, :], st2[:, :]))
                    nc.vector.tensor_scalar(ve2[:, :], mv2[:, 1:2], EPS, None, ALU.add).then_inc(var_ready, 1)
                    wait(dve, rstd_ready, g * GT + (j + 2))
                    link(nc.vector.scalar_tensor_tensor(nm2[:, :], mv2[:, 0:1], -1.0, rs2[:, :], ALU.mult, ALU.mult))
                    if j >= 2:
                        wait(dve, xn2_turned, g * GT + (j - 1))
                    else:
                        wait(dve, xn2_turned, g * GT)
                    nc.vector.tensor_scalar(xn2_b[:, j % 2, :], x1_b[:, j % 2, :], rs2[:, :], nm2[:, :],
                                            ALU.mult, ALU.add).then_inc(xn2_ready, 1)
                    assert link.n == PER

            from_zero(dve, body, NG)

        @block.tensor
        def _(pe):
            pe.wait_ge(consts, 4)
            pe.wait_ge(w_in, 16 * N_WEIGHTS)
            for kc in range(KC):
                for dc in range(KC):
                    last = nc.tensor.transpose(ps_x[:, kc * D + dc * P:kc * D + (dc + 1) * P],
                                               ws[:, dc, kc * P:(kc + 1) * P], ident[:, :])
            last.then_inc(spread, 1)
            pe.wait_ge(xn0_diag, 1)
            for g, bank in enumerate((ps_t1, ps_t2, ps_g[0], ps_g[1])):
                nc.tensor.matmul(bank[:, :], ones[:, :], diag[:, g * GT:(g + 1) * GT, :], start=True,
                                 stop=True).then_inc(spread, 1)
            pe.wait_ge(wn_diag_s, 1)
            nc.tensor.matmul(ps_v[:, 0:D], ones[:, :], wn_diag[:, :, :], start=True, stop=True).then_inc(spread, 1)
            pe.wait_ge(spread_out, N_SPREAD)
            def body(g):
                for j in range(GT):
                    t1 = g * GT + (j + 1)
                    wait(pe, xn_ready, t1)
                    wait(pe, xnt_ready, g * GT + j)
                    for kc in range(KC):
                        last = nc.tensor.transpose(ps_t1[:, kc * P:(kc + 1) * P], xn_b[:, j % 2, kc * P:(kc + 1) * P],
                                                   ident[:, :])
                    last.then_inc(xn_turned, 1)
                    wait(pe, xnt_ready, t1)
                    if j >= 2:
                        wait(pe, z_done, g * GT + (j - 1))
                    else:
                        wait(pe, z_done, g * GT)
                    for kc in range(KC):
                        last = nc.tensor.matmul(ps_g[j % 2][:, 0:D], xnt_b[:, j % 2, kc, :], ws_t[:, kc, :],
                                                start=kc == 0, stop=kc == KC - 1)
                    last.then_inc(self_done, 1)
                    wait(pe, xn2_ready, t1)
                    wait(pe, xn2t_ready, g * GT + j)
                    for kc in range(KC):
                        last = nc.tensor.transpose(ps_t2[:, kc * P:(kc + 1) * P], xn2_b[:, j % 2, kc * P:(kc + 1) * P],
                                                   ident[:, :])
                    last.then_inc(xn2_turned, 1)
                    wait(pe, xn2t_ready, t1)
                    wait(pe, v_out, g * GT + j)
                    for kc in range(KC):
                        last = nc.tensor.matmul(ps_v[:, 0:D], xn2_t[:, kc, j * P:(j + 1) * P], wv[:, kc, :],
                                                start=kc == 0, stop=kc == KC - 1)
                    last.then_inc(v_done, 1)
                for c in range(2 * KC):
                    w = wq if c < KC else wk
                    if c >= 2:
                        wait(pe, qk_hi, g * (2 * KC) + (c - 1))
                    else:
                        wait(pe, qk_hi, g * (2 * KC))
                    for kc in range(KC):
                        last = nc.tensor.matmul(ps_q[c % 2][:, :], w[:, kc, (c % KC) * P:(c % KC + 1) * P],
                                                xn2_t[:, kc, :], start=kc == 0, stop=kc == KC - 1)
                    last.then_inc(qk_done, 1)

            from_zero(pe, body, NG)

        @block.scalar
        def _(act):
            act.wait_ge(spread, 1)
            nc.scalar.activation(ws_t[:, :, :].rearrange("p a b -> p (a b)"), ps_x[:, :], ACT.Copy).then_inc(spread_out, 1)
            for g, bank in enumerate((ps_t1, ps_t2, ps_g[0], ps_g[1])):
                act.wait_ge(spread, g + 2)
                nc.scalar.activation(xn0[:, g * GW:(g + 1) * GW], bank[:, :], ACT.Copy).then_inc(spread_out, 1)
            act.wait_ge(spread, NG + 2)
            nc.scalar.activation(wn_bc[:, :], ps_v[:, 0:D], ACT.Copy).then_inc(spread_out, 1)
            act.wait_ge(b_in, 32)
            nc.scalar.activation(bqk_s[:, :, :], bqk[:, :, :], ACT.Copy, scale=QS).then_inc(spread_out, 1)
            act.wait_ge(spread_out, N_SPREAD + 1)
            def body(g):
                for j in range(GT):
                    t1 = g * GT + (j + 1)
                    wait(act, xn_turned, t1)
                    if j >= 2:
                        wait(act, self_done, g * GT + (j - 1))
                    else:
                        wait(act, self_done, g * GT)
                    nc.scalar.activation(xnt_b[:, j % 2, :, :].rearrange("p a b -> p (a b)"), ps_t1[:, 0:D],
                                         ACT.Copy).then_inc(xnt_ready, 1)
                    wait(act, adj_in[j], g * 16 + 16)
                    nc.scalar.activation(junk_a[:, :], adj_b[:, j, :], ACT.Copy,
                                         accum_out=r_col[:, j:j + 1]).then_inc(adj_counted, 1)
                    wait(act, xn2_turned, t1)
                    if j == 0:
                        wait(act, qk_done, g * (2 * KC))
                    nc.scalar.activation(xn2_t[:, :, j * P:(j + 1) * P],
                                         ps_t2[:, 0:D].rearrange("p (c q) -> p c q", c=KC),
                                         ACT.Copy).then_inc(xn2t_ready, 1)
                    wait(act, v_done, t1)
                    nc.scalar.activation(v_all[:, bass.ds(g * GT + j, 1), :, 0:HD].rearrange("p a h d -> p (a h) d"),
                                         ps_v[:, 0:D].rearrange("p (h d) -> p h d", h=H), ACT.Copy).then_inc(v_out, 1)
                for c in range(2 * KC):
                    wait(act, qk_done, g * (2 * KC) + (c + 1))
                    if c >= 2:
                        wait(act, qk_split, g * (2 * KC) + (c - 1))
                        wait(act, qk_stored[c % 2], g * (4 * 16) + 32)
                    else:
                        wait(act, qk_split, g * (2 * KC))
                        wait(act, qk_stored[c % 2], g * (4 * 16))
                    b16 = bqk_s[:, c // KC, c % KC:c % KC + 1]
                    nc.scalar.activation(qk32[:, c % 2, :], ps_q[c % 2][:, :], ACT.Identity, bias=b16, scale=QS)
                    nc.scalar.activation(qk16[:, c % 2, 0, :], ps_q[c % 2][:, :], ACT.Identity, bias=b16,
                                         scale=QS).then_inc(qk_hi, 1)

            from_zero(act, body, NG)


def phase_attend(nc, T, dr):
    UNITS, LAST = H * NG, H * NG - 1
    QW = 3 * HD
    QM = QW + 2
    PIECES = 8
    LAG = 2

    with ExitStack() as ctx:
        def sb(name, shape, dt=F32):
            return ctx.enter_context(nc.sbuf_tensor(name, shape, dt))

        def sem(name):
            return ctx.enter_context(nc.semaphore(name))

        ident, v_all, o_all = T["ident"], T["v_all"], T["o_all"]
        q_st = sb("q_st", [P, NG, GW], F16)
        k_st = sb("k_st", [P, 2, N], F16)
        p_ring = sb("p_ring", [P, PR, GW])
        stage = sb("stage", [P, 2, FF])
        max_part = sb("max_part", [P, PIECES])
        max_col = sb("max_col", [P, GT])
        max_row = sb("max_row", [GT, 2, P], F16)
        o_raw = sb("o_raw", [P, GT, HVW])
        o_rec = sb("o_rec", [P, GT])
        ps_m = [ctx.enter_context(nc.psum_tensor(f"ps_m{n}", [P, 1024], F32)) for n in range(2)]
        ps_e = [ctx.enter_context(nc.psum_tensor(f"ps_e{n}", [P, 512], F32)) for n in range(2)]
        ps_o = ctx.enter_context(nc.psum_tensor("ps_o", [P, 512], F32))
        ps_r = ctx.enter_context(nc.psum_tensor("ps_r", [P, 512], F32))

        q_in = [sem(f"q_in{c}") for c in range(NG)]
        row_in = [sem(f"row_in{c}") for c in range(NG)]
        k_in, k_const = sem("k_in"), sem("k_const")
        piece_done, piece_max = sem("piece_done"), sem("piece_max")
        max_ready, max_turned, row_ready = sem("max_ready"), sem("max_turned"), sem("row_ready")
        scores_done, probs_ready, values_done = sem("scores_done"), sem("probs_ready"), sem("values_done")
        row_hi = sem("row_hi")
        o_copied, o_inv, o_normed = sem("o_copied"), sem("o_inv"), sem("o_normed")
        stage_in = [sem("stage_in0"), sem("stage_in1")]
        w_step, w_split = sem("w_step"), sem("w_split")
        block = ctx.enter_context(nc.Block())

        def ge(eng, s, b, n, per, extra):
            if isinstance(b, int):
                if per * (4 * b + n) + extra > 0:
                    eng.wait_ge(s, per * (4 * b + n) + extra)
            else:
                eng.wait_ge(s, b * (4 * per) + (per * n + extra))

        def head_ge(eng, s, b, n, per):
            eng.wait_ge(s, (b + n // NG) * per + per if isinstance(b, int) else b * per + (per * (n // NG + 1)))

        def over_units(eng, step):
            step(0, 0)
            with eng.Fori(0, H - 1) as b:
                for n in range(1, NG + 1):
                    step(b, n)
            for n in range(1, NG):
                step(H - 1, n)

        def exists(b, n):
            return not isinstance(b, int) or NG * b + n < UNITS

        w1 = dr["W1"].rearrange("e (c p) f -> c p e f", p=P)
        w2 = dr["W2"].rearrange("e (f p) d -> p e f d", p=P)

        @block.sync
        def _(sp):
            def load_q(b, n):
                c, head = n % NG, b + n // NG
                for part, row in ((0, 0), (1, HD), (0, 2 * HD)):
                    sp.dma_start(q_st[row:row + HD, c, :],
                                 dr["qh"][part, bass.ds(head * HD, HD), c * GW:(c + 1) * GW]).then_inc(q_in[c], 16)

            def load_k(head, parity):
                for part, row in ((0, 0), (0, HD), (1, 2 * HD)):
                    sp.dma_start(k_st[row:row + HD, parity, :],
                                 dr["kh"][part, bass.ds(head * HD, HD), :]).then_inc(k_in, 16)

            def store_row(b, n):
                c = n % NG
                for part in range(2):
                    sp.dma_start(q_st[QW + part:QW + part + 1, c, :], max_row[:, part, :]).then_inc(row_in[c], 16)

            def step(b, n):
                ge(sp, scores_done, b, n, NT, 0)
                if exists(b, n + 3):
                    load_q(b, n + 3)
                if n == 1 and exists(b, NG):
                    load_k(b + 1, bass.ds((b + 1) % 2, 1))
                if exists(b, n + 1):
                    ge(sp, row_ready, b, n, 1, 2)
                    store_row(b, n + 1)

            load_k(0, bass.ds(0, 1))
            for n in range(3):
                load_q(0, n)
            sp.wait_ge(row_ready, 1)
            store_row(0, 0)
            over_units(sp, step)

        @block.gpsimd
        def _(pool):
            nc.gpsimd.memset(k_st[QW:QM, :, :], -MS).then_inc(k_const, 1)
            pool.wait_ge(k_const, 1)
            with pool.Fori(0, E) as e:
                one = bass.ds(e, 1)
                for c in range(4):
                    pool.wait_ge(stage_in[c % 2], 16)
                    pool.sem_clear(stage_in[c % 2])
                    raw = stage[:, c % 2, :]
                    if c < KC:
                        hi, lo = (T[w][:, one, c, :].rearrange("p a f -> p (a f)") for w in ("w1h", "w1l"))
                    else:
                        hi, lo = (T[w][:, one, (c - KC) * 4:(c - KC + 1) * 4, :].rearrange("p a f d -> p (a f d)")
                                  for w in ("w2h", "w2l"))
                    nc.gpsimd.tensor_scalar(raw, raw, WS, None, ALU.mult).then_inc(w_step, 1)
                    pool.wait_ge(w_step, 1)
                    nc.gpsimd.tensor_copy(hi, raw).then_inc(w_step, 1)
                    pool.wait_ge(w_step, 2)
                    pool.sem_clear(w_step)
                    nc.gpsimd.tensor_tensor(lo, raw, hi, ALU.subtract).then_inc(w_split, 1)

        @block.tensor
        def _(pe):
            def piece_of_maxima(b, n, j):
                c = n % NG
                if j == 0:
                    head_ge(pe, q_in[c], b, n, 48)
                    head_ge(pe, k_in, b, n, 48)
                if j % 2 == 0:
                    ge(pe, piece_max, b, n, PIECES, j // 2 - 1)
                par = bass.ds((b + n // NG) % 2, 1)
                m = nc.tensor.matmul(ps_m[j // 2 % 2][:, (j % 2) * GW:(j % 2 + 1) * GW],
                                     q_st[0:QW, c, (j // NG) * P:(j // NG + 1) * P],
                                     k_st[0:QW, par, (j % NG) * GW:(j % NG + 1) * GW].rearrange("p a k -> p (a k)"),
                                     start=True, stop=True)
                if j % 2:
                    m.then_inc(piece_done, 1)

            def turn_maxima(b, n):
                ge(pe, max_ready, b, n, 1, 1)
                ge(pe, row_ready, b, n, 1, 0)
                nc.tensor.transpose(ps_r[0:GT, 0:P], max_col[:, :], ident[:, :]).then_inc(max_turned, 1)

            def values(b, n, j):
                ge(pe, probs_ready, b, n, NT, j + 1)
                if j == 0:
                    ge(pe, o_copied, b, n, 1, 0)
                head = b + n // NG
                for qs in range(GT):
                    m = nc.tensor.matmul(ps_o[:, qs * HVW:(qs + 1) * HVW], p_ring[:, j % PR, qs * P:(qs + 1) * P],
                                         v_all[:, j, bass.ds(head, 1), :].rearrange("p a d -> p (a d)"),
                                         start=j == 0 and qs == 0, stop=j == NT - 1, skip_group_check=True)
                m.then_inc(values_done, 1)

            def step(b, n):
                c = n % NG
                par = bass.ds((b + n // NG) % 2, 1)
                for j in range(NT):
                    if j == 0:
                        head_ge(pe, row_in[c], b, n, 32)
                    ge(pe, probs_ready, b, n, NT, j - 1)
                    nc.tensor.matmul(ps_e[j % 2][:, :],
                                     k_st[0:QM, par, j * P:(j + 1) * P].rearrange("p a k -> p (a k)"),
                                     q_st[0:QM, c, :], start=True, stop=True).then_inc(scores_done, 1)
                    if exists(b, n + 2):
                        piece_of_maxima(b, n + 2, j)
                    if j == 3 and exists(b, n + 1):
                        turn_maxima(b, n + 1)
                    if j >= LAG:
                        values(b, n, j - LAG)
                for j in range(NT - LAG, NT):
                    values(b, n, j)

            pe.wait_ge(k_const, 1)
            for j in range(NT):
                piece_of_maxima(0, 0, j)
            turn_maxima(0, 0)
            for j in range(NT):
                piece_of_maxima(0, 1, j)
            over_units(pe, step)

        @block.scalar
        def _(act):
            def load_weights(b, n):
                c, one = n % NG, bass.ds(b + n // NG, 1)
                ge(act, w_split, b, n, 1, 0 if n == 1 else -1)
                if c < KC:
                    dst, src = stage[:, c % 2, :], w1[c, :, one, :].rearrange("p a f -> p (a f)")
                else:
                    dst = stage[:, c % 2, :].rearrange("p (f d) -> p f d", d=D)
                    src = w2[:, one, (c - KC) * 4:(c - KC + 1) * 4, :].rearrange("p a f d -> p (a f) d")
                act.dma_start(dst, src).then_inc(stage_in[c % 2], 16)

            def step(b, n):
                for j in range(NT):
                    ge(act, scores_done, b, n, NT, j + 1)
                    ge(act, values_done, b, n, NT, j + 1 - PR)
                    nc.scalar.activation(p_ring[:, j % PR, :], ps_e[j % 2][:, :], ACT.Exp,
                                         scale=SCALE / MS).then_inc(probs_ready, 1)
                    if j == 8:
                        load_weights(b, n)
                ge(act, values_done, b, n, NT, NT)
                ge(act, o_normed, b, n, 1, 0)
                nc.scalar.activation(o_raw[:, :, :].rearrange("p a b -> p (a b)"), ps_o[:, 0:GT * HVW],
                                     ACT.Copy).then_inc(o_copied, 1)

            over_units(act, step)

        @block.vector
        def _(dve):
            def reduce_piece(b, n, i):
                if i == 0:
                    ge(dve, max_ready, b, n, 1, 0)
                ge(dve, piece_done, b, n, PIECES, i + 1)
                nc.vector.tensor_reduce(max_part[:, i:i + 1], ps_m[i % 2][:, :], AX.X, ALU.max).then_inc(piece_max, 1)

            def join_maxima(b, n):
                ge(dve, piece_max, b, n, PIECES, PIECES)
                ge(dve, max_turned, b, n, 1, 0)
                parts = max_part[:, :].rearrange("p (q a) -> p q a", a=2)
                nc.vector.tensor_tensor(max_col[:, :], parts[:, :, 0], parts[:, :, 1], ALU.max).then_inc(max_ready, 1)

            def make_row(b, n):
                ge(dve, max_turned, b, n, 1, 1)
                if not (isinstance(b, int) and NG * b + n == 0):
                    head_ge(dve, row_in[(n - 1) % NG], b, n - 1, 32)
                nc.vector.tensor_scalar(max_row[:, 0, :], ps_r[0:GT, 0:P], 1.0 / MS, None, ALU.mult).then_inc(row_hi, 1)
                ge(dve, row_hi, b, n, 1, 1)
                nc.vector.scalar_tensor_tensor(max_row[:, 1, :], ps_r[0:GT, 0:P], 1.0 / MS, max_row[:, 0, :],
                                               ALU.mult, ALU.subtract).then_inc(row_ready, 1)

            def normalise(b, n):
                c, head = n % NG, b + n // NG
                ge(dve, o_copied, b, n, 1, 1)
                nc.vector.reciprocal(o_rec[:, :], o_raw[:, :, HD]).then_inc(o_inv, 1)
                ge(dve, o_inv, b, n, 1, 1)
                nc.vector.tensor_tensor(o_all[:, c * GT:(c + 1) * GT, bass.ds(head * HD, HD)], o_raw[:, :, 0:HD],
                                        o_rec[:, :].unsqueeze(2).to_broadcast([P, GT, HD]),
                                        ALU.mult).then_inc(o_normed, 1)

            def step(b, n):
                for i in range(PIECES):
                    if exists(b, n + 2):
                        reduce_piece(b, n + 2, i)
                    if i == 2 and exists(b, n + 1):
                        make_row(b, n + 1)
                    if i == 4 and not (isinstance(b, int) and NG * b + n == 0):
                        normalise(b, n - 1)
                if exists(b, n + 2):
                    join_maxima(b, n + 2)

            for n in range(2):
                for i in range(PIECES):
                    reduce_piece(0, n, i)
                join_maxima(0, n)
                if n == 0:
                    make_row(0, 0)
            over_units(dve, step)
            normalise(H - 1, NG - 1)


def phase_route(nc, T, dr):
    with ExitStack() as ctx:
        def sb(name, shape, dt=F32):
            return ctx.enter_context(nc.sbuf_tensor(name, shape, dt))

        def ps(name):
            return ctx.enter_context(nc.psum_tensor(name, [P, 512], F32))

        def sem(name):
            return ctx.enter_context(nc.semaphore(name))

        ident, o_all = T["ident"], T["o_all"]
        h_all = T["v_all"][:, :, :, :].rearrange("p t h d -> p (t h d)")[:, 0:NT * D].rearrange("p (t d) -> p t d", d=D)
        wo = sb("wo", [P, KC, D])
        gate_w = sb("gate_w", [P, KC, E])
        rows = {n: sb("row_" + n, [P, D]) for n in ("bv", "bo", "ln_g", "ln_b")}
        gate_b = sb("gate_bb", [P, E])
        b1_rows = sb("b1_rows", [E * FC, P])
        ot_b, ott_b = sb("ot_b", [P, 2, D]), sb("ott_b", [P, 2, KC, P])
        xr_b, y_b, h_b, ht_b = sb("xr_b", [P, 2, D]), sb("y_b", [P, 2, D]), sb("h_b", [P, 2, D]), sb("ht_b", [P, 2, KC, P])
        st, mv, ve, rs, nm = sb("st_c", [P, 6]), sb("mv_c", [P, 2]), sb("ve_c", [P, 1]), sb("rs_c", [P, 1]), sb("nm_c", [P, 1])
        logits = sb("logits", [P, NT, E])
        lmax, den = sb("lmax", [P, NT]), sb("den", [P, NT])
        eq, onehot, ex = sb("eq", [P, NT, E]), sb("onehot", [P, NT, E]), sb("ex", [P, NT, E])
        first = sb("first", [P, NT])
        PAD = NT // 2
        cum = [sb(f"cum{n}", [P, PAD + NT, E]) for n in range(2)]
        many = sb("many", [P, E, NT])
        EPAD = E // 2
        tiles = [sb(f"tiles{n}", [P, EPAD + E]) for n in range(2)]
        base = sb("base", [P, E])
        place, pos_f = sb("place", [P, NT, E]), sb("pos_f", [P, NT])
        below = sb("below", [P, SLOTS, E])
        slot_f = sb("slot_f", [P, SLOTS])
        tri, ones = sb("tri", [P, P]), sb("ones_c", [P, P])
        iota_i = sb("iota_i", [P, E + NT + SLOTS], I32)
        iota_f = sb("iota_f", [P, E + NT + SLOTS])
        ps_ot, ps_ht, ps_b1 = ps("ps_ot"), ps("ps_ht"), ps("ps_b1")
        ps_gate = [ps("ps_gate0"), ps("ps_gate1")]
        ps_wo = [ps("ps_wo0"), ps("ps_wo1")]

        w_in, b1_in, b2_in = sem("wo_in"), sem("b1_in"), sem("b2_in")
        xr_in = [sem("xr_in0"), sem("xr_in1")]
        row_stats = sem("row_stats_c")
        consts, chain = sem("consts_c"), sem("dve_chain_c")
        ot_ready, ot_turned, ott_ready, wo_done = sem("ot_ready"), sem("ot_turned"), sem("ott_ready"), sem("wo_done")
        y_part, y_ready, var_ready, rstd_ready = sem("y_part"), sem("y_ready"), sem("var_ready_c"), sem("rstd_ready_c")
        h_ready, h_kept, h_turned, ht_ready = sem("h_ready"), sem("h_kept"), sem("h_turned"), sem("ht_ready")
        gate_done, gate_out = sem("gate_done"), sem("gate_out")
        b1_turned, b1_out = sem("b1_turned"), sem("b1_out")
        onehot_ready, counted, less_max, exps_ready = sem("onehot_ready"), sem("counted"), sem("less_max"), sem("exps_ready")
        pos_ready, scattered = sem("pos_ready"), [sem(f"scattered{n}") for n in range(4)]
        block = ctx.enter_context(nc.Block())
        N_W = 7

        @block.sync
        def _(sp):
            sp.dma_start(wo[:, :, :], dr["Wo"].rearrange("(c p) d -> p c d", p=P)).then_inc(w_in, 16)
            sp.dma_start(gate_w[:, :, :], dr["gate_W"].rearrange("(c p) e -> p c e", p=P)).then_inc(w_in, 16)
            for n, r in rows.items():
                sp.dma_start(r[:, :], dr[n].partition_broadcast(P)).then_inc(w_in, 16)
            sp.dma_start(gate_b[:, :], dr["gate_b"].partition_broadcast(P)).then_inc(w_in, 16)
            for j in range(2):
                sp.dma_start(xr_b[:, j, :], dr["xn2"][j * P:(j + 1) * P, :]).then_inc(xr_in[j], 16)
            sp.dma_start(b1_rows[:, :], dr["b1"].rearrange("e (f p) -> (e f) p", p=P)).then_inc(b1_in, 16)
            sp.dma_start(T["b2_bc"][:, :, :], dr["b2"].partition_broadcast(P)).then_inc(b2_in, 16)
            with sp.Fori(1, NT // 2) as b:
                for j in range(2):
                    wait(sp, y_ready, b * 2 + (j - 1))
                    sp.dma_start(xr_b[:, j, :], dr["xn2"][bass.ds(b * (2 * P) + j * P, P), :]).then_inc(xr_in[j], 16)
            sp.wait_ge(b2_in, 16)

        @block.gpsimd
        def _(pool):
            nc.gpsimd.memset(ones[:, :], 1.0).then_inc(consts, 1)
            nc.gpsimd.memset(tri[:, :], 1.0).then_inc(consts, 1)
            for t in (*cum, *tiles):
                nc.gpsimd.memset(t[:, ...] if len(t.shape) == 2 else t[:, :, :], 0.0).then_inc(consts, 1)
            nc.gpsimd.iota(iota_i[:, 0:E], [[1, E]], base=-E, channel_multiplier=0).then_inc(consts, 1)
            nc.gpsimd.iota(iota_i[:, E:E + NT], [[P, NT]], base=0, channel_multiplier=0).then_inc(consts, 1)
            nc.gpsimd.iota(iota_i[:, E + NT:], [[1, SLOTS]], base=0, channel_multiplier=0).then_inc(consts, 1)
            pool.wait_ge(consts, 9)
            nc.gpsimd.affine_select(out=tri[:, :], in_=tri[:, :], compare_op=ALU.is_gt, fill=0.0,
                                    base=0, pattern=[[1, P]], channel_multiplier=-1).then_inc(consts, 1)
            nc.gpsimd.tensor_copy(iota_f[:, :], iota_i[:, :]).then_inc(consts, 1)
            def body(b):
                for j in range(2):
                    wait(pool, var_ready, b * 2 + (j + 1))
                    nc.gpsimd.tensor_tensor(rs[:, :], ve[:, :], T["minus_half"][:, 0:1], ALU.pow).then_inc(rstd_ready, 1)

            from_zero(pool, body, NT // 2)
            pool.wait_ge(h_kept, NT)
            pool.wait_ge(pos_ready, 1)
            for t in range(NT):
                pool.indirect_dma_start(dr["hs"], bass.IndirectOffsetOnAxis(ap=T["pos"][:, t:t + 1], axis=0),
                                        h_all[:, t, :], None).then_inc(scattered[t % 4], 16)
            for n in range(4):
                pool.wait_ge(scattered[n], 16 * NT // 4)

        @block.vector
        def _(dve):
            link = Link(dve, chain)
            dve.wait_ge(w_in, 16 * N_W)
            PER = 4
            def body(b):
                for j in range(2):
                    wait(dve, ot_turned, b * 2)
                    nc.vector.tensor_tensor(ot_b[:, j, :], o_all[:, bass.ds(b * 2 + j, 1), :].rearrange("p a d -> p (a d)"),
                                            rows["bv"][:, :], ALU.add).then_inc(ot_ready, 1)
                for j in range(2):
                    link.at(b * (2 * PER) + j * PER)
                    wait(dve, wo_done, b * 2 + (j + 1))
                    nc.vector.tensor_tensor(y_b[:, j, :], ps_wo[j][:, 0:D], rows["bo"][:, :], ALU.add).then_inc(y_part, 1)
                    wait(dve, y_part, b * 2 + (j + 1))
                    wait(dve, xr_in[j], b * 16 + 16)
                    nc.vector.tensor_tensor(y_b[:, j, :], y_b[:, j, :], xr_b[:, j, :], ALU.add).then_inc(y_ready, 1)
                    wait(dve, y_ready, b * 2 + (j + 1))
                    nc.vector.bn_stats(st[:, :], y_b[:, j, :]).then_inc(row_stats, 1)
                    dve.wait_ge(row_stats, 1)
                    dve.sem_clear(row_stats)
                    link(nc.vector.bn_aggr(mv[:, :], st[:, :]))
                    nc.vector.tensor_scalar(ve[:, :], mv[:, 1:2], EPS, None, ALU.add).then_inc(var_ready, 1)
                    wait(dve, rstd_ready, b * 2 + (j + 1))
                    link(nc.vector.scalar_tensor_tensor(nm[:, :], mv[:, 0:1], -1.0, rs[:, :], ALU.mult, ALU.mult))
                    link(nc.vector.tensor_scalar(y_b[:, j, :], y_b[:, j, :], rs[:, :], nm[:, :], ALU.mult, ALU.add))
                    link(nc.vector.tensor_tensor(y_b[:, j, :], y_b[:, j, :], rows["ln_g"][:, :], ALU.mult))
                    assert link.n == PER
                    wait(dve, h_turned, b * 2)
                    nc.vector.tensor_tensor(h_b[:, j, :], y_b[:, j, :], rows["ln_b"][:, :], ALU.add).then_inc(h_ready, 1)
                    nc.vector.tensor_tensor(h_all[:, bass.ds(b * 2 + j, 1), :].rearrange("p a d -> p (a d)"),
                                            y_b[:, j, :], rows["ln_b"][:, :], ALU.add).then_inc(h_kept, 1)
                for j in range(2):
                    wait(dve, gate_done, b * 2 + (j + 1))
                    nc.vector.tensor_tensor(logits[:, bass.ds(b * 2 + j, 1), :].rearrange("p a e -> p (a e)"),
                                            ps_gate[j][:, 0:E], gate_b[:, :], ALU.add).then_inc(gate_out, 1)

            from_zero(dve, body, NT // 2)
            link.at(NT * PER)
            dve.wait_ge(gate_out, NT)
            dve.wait_ge(consts, 11)
            TE = [P, NT, E]
            ids = iota_f[:, 0:E].unsqueeze(1).to_broadcast(TE)
            link(nc.vector.tensor_reduce(lmax[:, :], logits[:, :, :], AX.X, ALU.max))
            hi = lmax[:, :].unsqueeze(2).to_broadcast(TE)
            nc.vector.tensor_tensor(ex[:, :, :], logits[:, :, :], hi, ALU.subtract).then_inc(less_max, 1)
            link(nc.vector.tensor_tensor(eq[:, :, :], logits[:, :, :], hi, ALU.is_equal))
            link(nc.vector.tensor_tensor(eq[:, :, :], eq[:, :, :], ids, ALU.mult))
            link(nc.vector.tensor_reduce(first[:, :], eq[:, :, :], AX.X, ALU.min))
            nc.vector.tensor_tensor(onehot[:, :, :], ids, first[:, :].unsqueeze(2).to_broadcast(TE),
                                    ALU.is_equal).then_inc(onehot_ready, 1)
            dve.wait_ge(exps_ready, 1)
            link(nc.vector.tensor_reduce(den[:, :], ex[:, :, :], AX.X, ALU.add))
            link(nc.vector.reciprocal(T["gw"][:, :], den[:, :]))
            dve.wait_ge(counted, 1)
            link(nc.vector.tensor_copy(cum[0][:, PAD:, :], ps_b1[:, P:2 * P].rearrange("p (t e) -> p t e", e=E)))
            at = 0
            for step in (1, 2, 4, 8):
                link(nc.vector.tensor_tensor(cum[1 - at][:, PAD:, :], cum[at][:, PAD:, :],
                                             cum[at][:, PAD - step:PAD + NT - step, :], ALU.add))
                at = 1 - at
            cum_t = cum[at]
            link(nc.vector.tensor_tensor(many[:, :, :], cum_t[:, PAD + NT - 1, :].unsqueeze(2).to_broadcast([P, E, NT]),
                                         iota_f[:, E:E + NT].unsqueeze(1).to_broadcast([P, E, NT]), ALU.is_gt))
            link(nc.vector.tensor_reduce(tiles[0][:, EPAD:], many[:, :, :], AX.X, ALU.add))
            link(nc.vector.tensor_scalar(base[:, :], tiles[0][:, EPAD:], -1.0, None, ALU.mult))
            at = 0
            for step in (1, 2, 4):
                link(nc.vector.tensor_tensor(tiles[1 - at][:, EPAD:], tiles[at][:, EPAD:],
                                             tiles[at][:, EPAD - step:EPAD + E - step], ALU.add))
                at = 1 - at
            ends = tiles[at][:, EPAD:]
            link(nc.vector.tensor_tensor(base[:, :], base[:, :], ends, ALU.add))
            link(nc.vector.tensor_scalar(base[:, :], base[:, :], float(P), None, ALU.mult))
            link(nc.vector.tensor_tensor(place[:, :, :], ps_b1[:, 0:P].rearrange("p (t e) -> p t e", e=E),
                                         cum_t[:, PAD - 1:PAD + NT - 1, :], ALU.add))
            link(nc.vector.tensor_tensor(place[:, :, :], place[:, :, :], base[:, :].unsqueeze(1).to_broadcast(TE), ALU.add))
            link(nc.vector.tensor_tensor(place[:, :, :], place[:, :, :], onehot[:, :, :], ALU.mult))
            link(nc.vector.tensor_reduce(pos_f[:, :], place[:, :, :], AX.X, ALU.add))
            nc.vector.tensor_copy(T["pos"][:, :], pos_f[:, :]).then_inc(pos_ready, 1)
            link(nc.vector.tensor_tensor(below[:, :, :], ends.unsqueeze(1).to_broadcast([P, SLOTS, E]),
                                         iota_f[:, E + NT:].unsqueeze(2).to_broadcast([P, SLOTS, E]), ALU.is_le))
            link(nc.vector.tensor_reduce(slot_f[:, :], below[:, :, :], AX.X, ALU.add))
            link(nc.vector.tensor_scalar(slot_f[:, :], slot_f[:, :], float(E - 1), None, ALU.min))
            link(nc.vector.tensor_copy(T["slot_e"][:, :], slot_f[:, :]))

        @block.tensor
        def _(pe):
            pe.wait_ge(w_in, 16 * N_W)
            def body(b):
                for j in range(2):
                    t1 = b * 2 + (j + 1)
                    wait(pe, ot_ready, t1)
                    wait(pe, ott_ready, b * 2 + j)
                    for kc in range(KC):
                        last = nc.tensor.transpose(ps_ot[:, kc * P:(kc + 1) * P], ot_b[:, j, kc * P:(kc + 1) * P], ident[:, :])
                    last.then_inc(ot_turned, 1)
                    wait(pe, ott_ready, t1)
                    wait(pe, y_part, b * 2)
                    for kc in range(KC):
                        last = nc.tensor.matmul(ps_wo[j][:, 0:D], ott_b[:, j, kc, :], wo[:, kc, :],
                                                start=kc == 0, stop=kc == KC - 1)
                    last.then_inc(wo_done, 1)
                wait(pe, gate_out, b * 2)
                for j in range(2):
                    t1 = b * 2 + (j + 1)
                    wait(pe, h_ready, t1)
                    wait(pe, ht_ready, b * 2 + j)
                    for kc in range(KC):
                        last = nc.tensor.transpose(ps_ht[:, kc * P:(kc + 1) * P], h_b[:, j, kc * P:(kc + 1) * P], ident[:, :])
                    last.then_inc(h_turned, 1)
                for j in range(2):
                    wait(pe, ht_ready, b * 2 + (j + 1))
                    for kc in range(KC):
                        last = nc.tensor.matmul(ps_gate[j][:, 0:E], ht_b[:, j, kc, :], gate_w[:, kc, :],
                                                start=kc == 0, stop=kc == KC - 1)
                    last.then_inc(gate_done, 1)

            from_zero(pe, body, NT // 2)
            pe.wait_ge(b1_in, 16)
            nc.tensor.transpose(ps_ot[:, 0:E * FC], b1_rows[:, :], ident[0:E * FC, 0:E * FC]).then_inc(b1_turned, 1)
            pe.wait_ge(onehot_ready, 1)
            pe.wait_ge(consts, 10)
            nc.tensor.matmul(ps_b1[:, 0:P], tri[:, :], onehot[:, :, :], start=True, stop=True)
            nc.tensor.matmul(ps_b1[:, P:2 * P], ones[:, :], onehot[:, :, :], start=True, stop=True).then_inc(counted, 1)

        @block.scalar
        def _(act):
            def body(b):
                for j in range(2):
                    wait(act, ot_turned, b * 2 + (j + 1))
                    wait(act, wo_done, b * 2)
                    nc.scalar.activation(ott_b[:, j, :, :].rearrange("p a b -> p (a b)"), ps_ot[:, 0:D],
                                         ACT.Copy).then_inc(ott_ready, 1)
                for j in range(2):
                    wait(act, h_turned, b * 2 + (j + 1))
                    wait(act, gate_done, b * 2)
                    nc.scalar.activation(ht_b[:, j, :, :].rearrange("p a b -> p (a b)"), ps_ht[:, 0:D],
                                         ACT.Copy).then_inc(ht_ready, 1)

            from_zero(act, body, NT // 2)
            act.wait_ge(b1_turned, 1)
            nc.scalar.activation(T["b1_t"][:, :, :].rearrange("p a b -> p (a b)"), ps_ot[:, 0:E * FC], ACT.Copy).then_inc(b1_out, 1)
            act.wait_ge(less_max, 1)
            nc.scalar.activation(ex[:, :, :], ex[:, :, :], ACT.Exp).then_inc(exps_ready, 1)


def phase_experts(nc, T, dr):
    HALF = FC // 2
    with ExitStack() as ctx:
        def sb(name, shape, dt=F32):
            return ctx.enter_context(nc.sbuf_tensor(name, shape, dt))

        def ps(name):
            return ctx.enter_context(nc.psum_tensor(name, [P, 512], F32))

        def sem(name):
            return ctx.enter_context(nc.semaphore(name))

        ident, slot_e = T["ident"], T["slot_e"]
        tok = sb("tok", [P, D])
        t32 = sb("t32", [P, KC * P])
        th, tl = sb("th", [P, KC * P], F16), sb("tl", [P, KC * P], F16)
        b1_b = sb("b1_b", [P, FC])
        hid = sb("hid", [P, FC, P])
        hid16 = [sb("hid_h", [P, 2, FC * P], F16), sb("hid_l", [P, 2, FC * P], F16)]
        y_b = sb("y_b_d", [P, D])
        ps_t, ps_y = ps("ps_t"), ps("ps_y")
        ps_h = [ps("ps_h0"), ps("ps_h1")]
        tok_in, y_stored = sem("tok_in"), sem("y_stored")
        turned, t32_ready, th_ready, t_split = sem("turned"), sem("t32_ready"), sem("th_ready"), sem("t_split")
        up_done, b1_ready, gelu_done = sem("up_done"), sem("b1_ready"), sem("gelu_done")
        hid_hi, hid_split, down_done, y_ready = sem("hid_hi"), sem("hid_split"), sem("down_done"), sem("y_ready")
        hid_scaled = sem("hid_scaled")
        block = ctx.enter_context(nc.Block())

        def expert(eng, s):
            slot = slot_e[0:1, s:s + 1] if isinstance(s, int) else slot_e[0:1, bass.ds(s, 1)]
            return eng.value_load(slot, min_val=0, max_val=E - 1)

        def over_slots(eng, step):
            step(0)
            step(1)
            with eng.Fori(2, SLOTS - 1) as s:
                step(s)
            step(SLOTS - 1)

        def first(s):
            return isinstance(s, int) and s == 0

        def final(s):
            return isinstance(s, int) and s == SLOTS - 1

        @block.sync
        def _(sp):
            def load(s):
                if not first(s):
                    sp.wait_ge(turned, s)
                sp.dma_start(tok[:, :], dr["hs"][bass.ds(s * P, P), :]).then_inc(tok_in, 16)

            def store(s):
                sp.wait_ge(y_ready, s + 1)
                sp.dma_start(dr["ys"][bass.ds(s * P, P), :], y_b[:, :]).then_inc(y_stored, 16)

            load(0)
            load(1)
            load(2)
            store(0)
            with sp.Fori(1, SLOTS - 2) as s:
                load(s + 2)
                store(s)
            store(SLOTS - 2)
            store(SLOTS - 1)
            sp.wait_ge(y_stored, 16 * SLOTS)

        @block.tensor
        def _(pe):
            def turn_tokens(s):
                pe.wait_ge(tok_in, s * 16 + 16)
                if not first(s):
                    pe.wait_ge(t32_ready, s)
                for kc in range(KC):
                    last = nc.tensor.transpose(ps_t[:, kc * P:(kc + 1) * P], tok[:, kc * P:(kc + 1) * P], ident[:, :])
                last.then_inc(turned, 1)

            def up(s, e, half):
                if not first(s):
                    pe.wait_ge(gelu_done, s * 2 + (half - 1))
                products = [(w, x, kc) for w, x in (("w1h", th), ("w1h", tl), ("w1l", th)) for kc in range(KC)]
                for f in range(half * HALF, (half + 1) * HALF):
                    for n, (w, x, kc) in enumerate(products):
                        last = nc.tensor.matmul(ps_h[half][:, (f % HALF) * P:(f % HALF + 1) * P],
                                                T[w][:, bass.ds(e, 1), kc, f * P:(f + 1) * P].rearrange("p a f -> p (a f)"),
                                                x[:, kc * P:(kc + 1) * P], start=n == 0, stop=n == len(products) - 1)
                last.then_inc(up_done, 1)

            def down(s, e):
                pe.wait_ge(hid_split, s * 2 + 2)
                if not first(s):
                    pe.wait_ge(y_ready, s)
                par = bass.ds(s % 2, 1)
                n = 0
                for f in range(FC):
                    for x, w in ((0, "w2h"), (0, "w2l"), (1, "w2h")):
                        last = nc.tensor.matmul(ps_y[:, 0:D], hid16[x][:, par, f * P:(f + 1) * P].rearrange("p a q -> p (a q)"),
                                                T[w][:, bass.ds(e, 1), f, :].rearrange("p a d -> p (a d)"),
                                                start=n == 0, stop=n == 3 * FC - 1)
                        n += 1
                last.then_inc(down_done, 1)

            def step(s):
                e = expert(pe, s)
                pe.wait_ge(t_split, s + 1)
                up(s, e, 0)
                if not final(s):
                    turn_tokens(s + 1)
                up(s, e, 1)
                if not first(s):
                    down(s - 1, expert(pe, s - 1))

            turn_tokens(0)
            over_slots(pe, step)
            down(SLOTS - 1, expert(pe, SLOTS - 1))

        @block.scalar
        def _(act):
            def tokens(s):
                act.wait_ge(turned, s + 1)
                if not first(s):
                    act.wait_ge(t_split, s)
                nc.scalar.activation(t32[:, :], ps_t[:, 0:D], ACT.Copy, scale=TS).then_inc(t32_ready, 1)

            def step(s):
                act.wait_ge(b1_ready, s + 1)
                for half in range(2):
                    act.wait_ge(up_done, s * 2 + (half + 1))
                    if not first(s):
                        act.wait_ge(hid_split, s * 2 + (half - 1))
                    for f in range(half * HALF, (half + 1) * HALF):
                        last = nc.scalar.activation(hid[:, f, :], ps_h[half][:, (f % HALF) * P:(f % HALF + 1) * P],
                                                    ACT.Gelu_apprx_tanh, bias=b1_b[:, f:f + 1], scale=1.0 / (TS * WS))
                    last.then_inc(gelu_done, 1)
                    if half == 0 and not final(s):
                        tokens(s + 1)

            tokens(0)
            over_slots(act, step)

        @block.vector
        def _(dve):
            def split_tokens(s):
                dve.wait_ge(t32_ready, s + 1)
                if not first(s):
                    dve.wait_ge(up_done, s * 2)
                nc.vector.tensor_copy(th[:, :], t32[:, :]).then_inc(th_ready, 1)
                dve.wait_ge(th_ready, s + 1)
                nc.vector.tensor_tensor(tl[:, :], t32[:, :], th[:, :], ALU.subtract).then_inc(t_split, 1)

            def bias(s, e):
                if not first(s):
                    dve.wait_ge(gelu_done, s * 2)
                nc.vector.tensor_copy(b1_b[:, :], T["b1_t"][:, bass.ds(e, 1), :].rearrange("p a f -> p (a f)")).then_inc(b1_ready, 1)

            def split_hidden(s, half):
                dve.wait_ge(gelu_done, s * 2 + (half + 1))
                if not (isinstance(s, int) and s < 2):
                    if half == 0:
                        dve.wait_ge(down_done, s - 1)
                raw = hid[:, half * HALF:(half + 1) * HALF, :].rearrange("p f q -> p (f q)")
                par = bass.ds(s % 2, 1)
                hi, lo = (x[:, par, half * HALF * P:(half + 1) * HALF * P].rearrange("p a q -> p (a q)") for x in hid16)
                nc.vector.tensor_scalar(raw, raw, TS, None, ALU.mult).then_inc(hid_scaled, 1)
                dve.wait_ge(hid_scaled, s * 2 + (half + 1))
                nc.vector.tensor_copy(hi, raw).then_inc(hid_hi, 1)
                dve.wait_ge(hid_hi, s * 2 + (half + 1))
                nc.vector.tensor_tensor(lo, raw, hi, ALU.subtract).then_inc(hid_split, 1)

            def output(s, e):
                dve.wait_ge(down_done, s + 1)
                if not first(s):
                    dve.wait_ge(y_stored, s * 16)
                nc.vector.scalar_tensor_tensor(y_b[:, :], ps_y[:, 0:D], 1.0 / (TS * WS),
                                               T["b2_bc"][:, bass.ds(e, 1), :].rearrange("p a d -> p (a d)"),
                                               ALU.mult, ALU.add).then_inc(y_ready, 1)

            def step(s):
                bias(s, expert(dve, s))
                split_hidden(s, 0)
                if not final(s):
                    split_tokens(s + 1)
                split_hidden(s, 1)
                if not first(s):
                    output(s - 1, expert(dve, s - 1))

            split_tokens(0)
            over_slots(dve, step)
            output(SLOTS - 1, expert(dve, SLOTS - 1))


def phase_return(nc, T, dr):
    with ExitStack() as ctx:
        def sb(name, shape, dt=F32):
            return ctx.enter_context(nc.sbuf_tensor(name, shape, dt))

        def sem(name):
            return ctx.enter_context(nc.semaphore(name))

        y_all, x1_all = sb("y_all", [P, NT, D]), sb("x1_all", [P, NT, D])
        x1_in, y_in, summed, stored = sem("x1_in"), [sem(f"y_in{g}") for g in range(NG)], sem("summed"), sem("stored")
        block = ctx.enter_context(nc.Block())

        @block.gpsimd
        def _(pool):
            for t in range(NT):
                pool.indirect_dma_start(y_all[:, t, :], None, dr["ys"],
                                        bass.IndirectOffsetOnAxis(ap=T["pos"][:, t:t + 1], axis=0)).then_inc(y_in[t // GT], 16)

        @block.vector
        def _(dve):
            dve.wait_ge(x1_in, 16)
            for t in range(NT):
                if t % GT == 0:
                    dve.wait_ge(y_in[t // GT], 16 * GT)
                last = nc.vector.scalar_tensor_tensor(y_all[:, t, :], y_all[:, t, :], T["gw"][:, t:t + 1], x1_all[:, t, :],
                                                      ALU.mult, ALU.add).then_inc(summed, 1)

        @block.sync
        def _(sp):
            sp.dma_start(x1_all[:, :, :], dr["x1"].rearrange("(t p) d -> p t d", p=P)).then_inc(x1_in, 16)
            for g in range(NG):
                sp.wait_ge(summed, GT * (g + 1))
                sp.dma_start(dr["out"][g * GW:(g + 1) * GW, :].rearrange("(t p) d -> p t d", p=P),
                             y_all[:, g * GT:(g + 1) * GT, :]).then_inc(stored, 16)
            sp.wait_ge(stored, 16 * NG)


def phase_rest(nc, T, dr, phases):
    with ExitStack() as ctx:
        def sb(name, shape, dt=F32):
            return ctx.enter_context(nc.sbuf_tensor(name, shape, dt))

        for w in ("w1h", "w1l"):
            T[w] = sb(w, [P, E, KC, FF], F16)
        for w in ("w2h", "w2l"):
            T[w] = sb(w, [P, E, FC, D], F16)
        T["pos"] = sb("pos", [P, NT], U32)
        T["gw"] = sb("gw", [P, NT])
        T["slot_e"] = sb("slot_e", [P, SLOTS], I32)
        T["b1_t"] = sb("b1_t", [P, E, FC])
        with ExitStack() as inner:
            T["o_all"] = inner.enter_context(nc.sbuf_tensor("o_all", [P, NT, D], F32))
            phase_attend(nc, T, dr)
            if "C" in phases:
                T["b2_bc"] = inner.enter_context(nc.sbuf_tensor("b2_bc", [P, E, D], F32))
                phase_route(nc, T, dr)
            if "D" in phases:
                phase_experts(nc, T, dr)
        if "E" in phases:
            phase_return(nc, T, dr)


def build(nc, a, out, phases="ABCDE"):
    with ExitStack() as ctx:
        def sb(name, shape, dt=F32):
            return ctx.enter_context(nc.sbuf_tensor(name, shape, dt))

        dr = dict(a)
        dr["out"] = out
        for name, shape, dt in (("x1", (N, D), F32), ("xn2", (N, D), F32), ("qh", (2, D, N), F16), ("kh", (2, D, N), F16),
                                ("hs", (SLOTS * P, D), F32), ("ys", (SLOTS * P, D), F32)):
            dr[name] = nc.dram_tensor(name + "_scratch", shape, dt).ap()
        T = {"ident": sb("ident", [P, P]), "v_all": sb("v_all", [P, NT, H, HVW]),
             "minus_half": sb("minus_half", [P, NT]),
             "hs_cleared": ctx.enter_context(nc.semaphore("hs_cleared"))}
        phase_project(nc, T, dr)
        if "B" in phases:
            phase_rest(nc, T, dr, phases)


_INS = {"x": "x", "adj": "adj", "L0_gnn_w_self": "w_self", "L0_gnn_w_neigh": "w_neigh", "L0_ffn_ln1_g": "ln_g",
        "L0_ffn_ln1_b": "ln_b", "L0_ffn_Wq": "Wq", "L0_ffn_bq": "bq", "L0_ffn_Wk": "Wk", "L0_ffn_bk": "bk",
        "L0_ffn_Wv": "Wv", "L0_ffn_bv": "bv", "L0_ffn_Wo": "Wo", "L0_ffn_bo": "bo", "L0_ffn_gate_W": "gate_W",
        "L0_ffn_gate_b": "gate_b", "L0_ffn_W1": "W1", "L0_ffn_b1": "b1", "L0_ffn_W2": "W2", "L0_ffn_b2": "b2"}


def kernel(**inputs):
    import numpy as np
    import concourse.bacc as bacc
    from concourse.bass_utils import run_bass_kernel_spmd

    nc = bacc.Bacc("TRN2", target_bir_lowering=False, num_devices=1)
    arrays, aps = {}, {}
    for name, short in _INS.items():
        arr = np.ascontiguousarray(inputs[name])
        arrays["in_" + short] = arr
        aps[short] = nc.dram_tensor("in_" + short, arr.shape, mybir.dt.from_np(arr.dtype), kind="ExternalInput").ap()
    out = nc.dram_tensor("out", (N, D), F32, kind="ExternalOutput").ap()
    build(nc, aps, out)
    r = run_bass_kernel_spmd(nc, [arrays], core_ids=[0])
    return r.results[0]["out"]
```

```python
import concourse.bass as bass
from concourse import mybir
from contextlib import ExitStack

F32 = mybir.dt.float32
F16 = mybir.dt.float16
I32 = mybir.dt.int32
U32 = mybir.dt.uint32
ALU = mybir.AluOpType
ACT = mybir.ActivationFunctionType
AX = mybir.AxisListType

P = 128
N = 2048
D = 256
H = 8
HD = D // H
E = 8
FF = 4 * D
NT = N // P
KC = D // P
FC = FF // P
GT = 4
NG = NT // GT
GW = GT * P
SLOTS = (N + E * (P - 1)) // P
EPS = 1e-5
QS = 16.0
MS = QS * QS
SCALE = float(HD) ** -0.5
TS = 16.0
WS = 64.0
PR = 8
KG = P // HD


class Link:

    def __init__(self, eng, sem):
        self.eng, self.sem, self.base, self.n, self.most = eng, sem, 0, 0, 0

    def at(self, base):
        self.base, self.n = base, 0

    def __call__(self, ins):
        self.n += 1
        ins.then_inc(self.sem, 1)
        self.eng.wait_ge(self.sem, self.base + self.n)


def from_zero(eng, body, end, apart=1):
    for i in range(apart):
        body(i)
    with eng.Fori(apart, end) as i:
        body(i)


def wait(eng, sem, value):
    if isinstance(value, int):
        if value > 0:
            eng.wait_ge(sem, value)
    else:
        eng.wait_ge(sem, value)


def phase_project(nc, T, dr):
    with ExitStack() as ctx:
        def sb(name, shape, dt=F32):
            return ctx.enter_context(nc.sbuf_tensor(name, shape, dt))

        def ps(name):
            return ctx.enter_context(nc.psum_tensor(name, [P, 512], F32))

        def sem(name):
            return ctx.enter_context(nc.semaphore(name))

        ident, v_all = T["ident"], T["v_all"]
        x_all = sb("x_all", [P, NT, D])
        adj_b = sb("adj_b", [P, GT, N], I32)
        xn0 = sb("xn0", [P, N])
        junk_v = sb("junk_v", [P, N])
        junk_a = sb("junk_a", [P, N])
        ones = sb("ones_a", [P, P])
        ws, wn = sb("ws", [P, KC, D]), sb("wn", [P, KC, D])
        wq, wk, wv = sb("wq", [P, KC, D]), sb("wk", [P, KC, D]), sb("wv", [P, KC, D])
        bqk = sb("bqk", [P, 2, KC])
        bqk_s = sb("bqk_s", [P, 2, KC])
        ws_t = sb("ws_t", [P, KC, D])
        wn_col = sb("wn_col", [P, KC])
        wn_diag = sb("wn_diag", [P, KC, P])
        wn_bc = sb("wn_bc", [P, D])
        stats = sb("stats", [P, NT, 6])
        mean, rstd, nmr = sb("mean", [P, NT]), sb("rstd", [P, NT]), sb("nmr", [P, NT])
        half, col0 = sb("half", [P, NT]), sb("col0", [P, NT])
        xn_b = sb("xn_b", [P, 2, D])
        xnt_b = sb("xnt_b", [P, 2, KC, P])
        s_col, r_col, sg_col = sb("s_col", [P, GT]), sb("r_col", [P, GT]), sb("sg_col", [P, GT])
        z_b = sb("z_b", [P, D])
        x1_b, xn2_b = sb("x1_b", [P, 2, D]), sb("xn2_b", [P, 2, D])
        st2, mv2, nm2 = sb("st2", [P, 6]), sb("mv2", [P, 2, 2]), sb("nm2", [P, 1])
        ve2, rs2 = sb("ve2", [P, 2]), sb("rs2", [P, 2])
        xn2_t = sb("xn2_t", [P, KC, GW])
        qk32 = sb("qk32", [P, 2, GW])
        qk16 = sb("qk16", [P, 2, 2, GW], F16)
        zero_b = sb("zero_b", [P, D])
        diag = junk_v[:, :].rearrange("p (t q) -> p t q", t=NT)

        ps_t1, ps_t2, ps_v = ps("ps_t1"), ps("ps_t2"), ps("ps_v")
        ps_g = [ps("ps_g0"), ps("ps_g1")]
        ps_q = [ps("ps_q0"), ps("ps_q1")]
        ps_x = ps("ps_x")

        x_in, w_in, b_in = sem("x_in"), sem("w_in"), sem("b_in")
        adj_in = [sem(f"adj_in{j}") for j in range(GT)]
        row_stats = sem("row_stats_a")
        consts, dve_chain, zeroed = sem("consts_a"), sem("dve_chain_a"), sem("zeroed")
        xn0_diag, wn_diag_s = sem("xn0_diag"), sem("wn_diag_s")
        spread, spread_out = sem("spread"), sem("spread_out")
        var_ready, rstd_ready = sem("var_ready"), sem("rstd_ready")
        xn_ready, xn_turned, xnt_ready = sem("xn_ready"), sem("xn_turned"), sem("xnt_ready")
        self_done, z_done = sem("self_done"), sem("z_done")
        adj_summed, adj_counted = sem("adj_summed"), sem("adj_counted")
        x1_ready, xn2_ready, xn2_turned, xn2t_ready = sem("x1_ready"), sem("xn2_ready"), sem("xn2_turned"), sem("xn2t_ready")
        v_done, v_out = sem("v_done"), sem("v_out")
        qk_done, qk_hi, qk_split = sem("qk_done"), sem("qk_hi"), sem("qk_split")
        tile_stored = [sem("tile_stored0"), sem("tile_stored1")]
        qk_stored = [sem("qk_stored0"), sem("qk_stored1")]
        block = ctx.enter_context(nc.Block())

        N_WEIGHTS = 5
        N_SPREAD = NG + 2

        def first(g, j):
            return isinstance(g, int) and g == 0 and j == 0

        @block.sync
        def _(sp):
            sp.dma_start(x_all[:, :, :], dr["x"].rearrange("(t p) d -> p t d", p=P)).then_inc(x_in, 16)
            for j in range(GT):
                sp.dma_start(adj_b[:, j, :], dr["adj"][j * P:(j + 1) * P, :]).then_inc(adj_in[j], 16)
                if j == 0:
                    for w, src in ((ws, "w_self"), (wn, "w_neigh"), (wq, "Wq"), (wk, "Wk"), (wv, "Wv")):
                        sp.dma_start(w[:, :, :], dr[src].rearrange("(c p) d -> p c d", p=P)).then_inc(w_in, 16)
                    for n, src in enumerate(("bq", "bk")):
                        sp.dma_start(bqk[:, n, :], dr[src].rearrange("(c p) -> p c", p=P),
                                     allow_slow_non_contiguous=True).then_inc(b_in, 16)

            def store_tile(g, j):
                rows = bass.ds(g * GW + j * P, P)
                sp.wait_ge(x1_ready, g * GT + (j + 1))
                sp.dma_start(dr["x1"][rows, :], x1_b[:, j % 2, :]).then_inc(tile_stored[j % 2], 16)
                sp.wait_ge(xn2_ready, g * GT + (j + 1))
                sp.dma_start(dr["xn2"][rows, :], xn2_b[:, j % 2, :]).then_inc(tile_stored[j % 2], 16)

            def store_group(g):
                cols = bass.ds(g * GW if isinstance(g, int) else sp.snap(g * GW), GW)
                for c in range(2 * KC):
                    sp.wait_ge(qk_split, g * (2 * KC) + (c + 1))
                    dst = dr["qh"] if c < KC else dr["kh"]
                    for part in (1, 0):
                        sp.dma_start(dst[part, (c % KC) * P:(c % KC + 1) * P, cols],
                                     qk16[:, c % 2, part, :]).then_inc(qk_stored[c % 2], 16)

            with sp.Fori(1, NG) as g:
                for j in range(GT):
                    sp.wait_ge(adj_summed, g * GT + (j - GT + 1))
                    sp.wait_ge(adj_counted, g * GT + (j - GT + 1))
                    sp.dma_start(adj_b[:, j, :], dr["adj"][bass.ds(g * GW + j * P, P), :]).then_inc(adj_in[j], 16)
                    store_tile(g - 1, j)
                store_group(g - 1)
            for j in range(GT):
                store_tile(NG - 1, j)
            store_group(NG - 1)
            for n in range(2):
                sp.wait_ge(tile_stored[n], NT * 16)
                sp.wait_ge(qk_stored[n], NG * 4 * 16)

        @block.gpsimd
        def _(pool):
            nc.gpsimd.memset(ident[:, :], 0.0).then_inc(zeroed, 1)
            nc.gpsimd.memset(ones[:, :], 1.0).then_inc(consts, 1)
            nc.gpsimd.memset(T["minus_half"][:, :], -0.5).then_inc(consts, 1)
            nc.gpsimd.memset(zero_b[:, :], 0.0).then_inc(zeroed, 1)
            pool.wait_ge(zeroed, 2)
            nc.gpsimd.affine_select(out=ident[:, :], in_=ident[:, :], compare_op=ALU.not_equal, fill=1.0,
                                    base=0, pattern=[[-1, P]], channel_multiplier=1).then_inc(consts, 1)
            pool.dma_start(dr["hs"].rearrange("(s p) d -> p s d", p=P),
                           zero_b[:, :].unsqueeze(1).to_broadcast([P, SLOTS, D])).then_inc(T["hs_cleared"], 16)
            pool.wait_ge(consts, 3)
            pool.wait_ge(var_ready, 1)
            nc.gpsimd.tensor_tensor(rstd[:, :], rstd[:, :], T["minus_half"][:, :], ALU.pow).then_inc(rstd_ready, 1)
            def body(g):
                for j in range(GT):
                    wait(pool, var_ready, g * GT + (j + 2))
                    nc.gpsimd.tensor_tensor(rs2[:, j % 2:j % 2 + 1], ve2[:, j % 2:j % 2 + 1],
                                            T["minus_half"][:, 0:1], ALU.pow).then_inc(rstd_ready, 1)
                    if j == 0 and not first(g, j):
                        split(g - 1)

            def split(g):
                for c in range(2 * KC):
                    wait(pool, qk_hi, g * (2 * KC) + (c + 1))
                    wait(pool, qk_stored[c % 2], g * (4 * 16) + c // 2 * 32)
                    nc.gpsimd.tensor_tensor(qk16[:, c % 2, 1, :], qk32[:, c % 2, :], qk16[:, c % 2, 0, :],
                                            ALU.subtract).then_inc(qk_split, 1)

            from_zero(pool, body, NG, apart=2)
            split(NG - 1)
            pool.wait_ge(T["hs_cleared"], 16)

        @block.vector
        def _(dve):
            link = Link(dve, dve_chain)
            dve.wait_ge(x_in, 16)
            with dve.Fori(0, NT) as t:
                nc.vector.bn_stats(stats[:, bass.ds(t, 1), :].rearrange("p a s -> p (a s)"),
                                   x_all[:, bass.ds(t, 1), :].rearrange("p a d -> p (a d)")).then_inc(dve_chain, 1)
            link.at(NT)
            dve.wait_ge(dve_chain, NT)
            link(nc.vector.tensor_tensor(mean[:, :], stats[:, :, 1], stats[:, :, 4], ALU.add))
            link(nc.vector.tensor_scalar(mean[:, :], mean[:, :], 0.5, None, ALU.mult))
            link(nc.vector.tensor_tensor(half[:, :], stats[:, :, 1], mean[:, :], ALU.subtract))
            link(nc.vector.tensor_tensor(half[:, :], half[:, :], half[:, :], ALU.mult))
            link(nc.vector.tensor_tensor(rstd[:, :], stats[:, :, 2], stats[:, :, 5], ALU.add))
            link(nc.vector.scalar_tensor_tensor(rstd[:, :], rstd[:, :], 1.0 / D, half[:, :], ALU.mult, ALU.add))
            nc.vector.tensor_scalar(rstd[:, :], rstd[:, :], EPS, None, ALU.add).then_inc(var_ready, 1)
            dve.wait_ge(rstd_ready, 1)
            link(nc.vector.scalar_tensor_tensor(nmr[:, :], mean[:, :], -1.0, rstd[:, :], ALU.mult, ALU.mult))
            link(nc.vector.tensor_tensor(col0[:, :], x_all[:, :, 0], rstd[:, :], ALU.mult))
            link(nc.vector.tensor_tensor(col0[:, :], col0[:, :], nmr[:, :], ALU.add))
            dve.wait_ge(consts, 3)
            nc.vector.tensor_tensor(diag, ident[:, :].unsqueeze(1).to_broadcast([P, NT, P]),
                                    col0[:, :].unsqueeze(2).to_broadcast([P, NT, P]), ALU.mult).then_inc(xn0_diag, 1)
            dve.wait_ge(w_in, 16 * N_WEIGHTS)
            link(nc.vector.tensor_reduce(wn_col[:, :], wn[:, :, :], AX.X, ALU.add))
            nc.vector.tensor_tensor(wn_diag[:, :, :], ident[:, :].unsqueeze(1).to_broadcast([P, KC, P]),
                                    wn_col[:, :].unsqueeze(2).to_broadcast([P, KC, P]), ALU.mult).then_inc(wn_diag_s, 1)
            dve.wait_ge(spread_out, N_SPREAD)
            START, PER = link.base + link.n, 3
            def second(g, j):
                par = slice(j % 2, j % 2 + 1)
                wait(dve, rstd_ready, g * GT + (j + 2))
                link(nc.vector.scalar_tensor_tensor(nm2[:, :], mv2[:, j % 2, 0:1], -1.0, rs2[:, par], ALU.mult, ALU.mult))
                wait(dve, xn2_turned, g * GT + (j - 1))
                nc.vector.tensor_scalar(xn2_b[:, j % 2, :], x1_b[:, j % 2, :], rs2[:, par], nm2[:, :],
                                    ALU.mult, ALU.add).then_inc(xn2_ready, 1)

            def body(g):
                for j in range(GT):
                    link.at(START if first(g, j) else g * (GT * PER) + (START + j * PER - 1))
                    one = bass.ds(g * GT + j, 1)
                    x_t = x_all[:, one, :].rearrange("p a d -> p (a d)")
                    wait(dve, xn_turned, g * GT + (j - 1))
                    nc.vector.tensor_scalar(xn_b[:, j % 2, :], x_t, rstd[:, one], nmr[:, one],
                                            ALU.mult, ALU.add).then_inc(xn_ready, 1)
                    wait(dve, adj_in[j], g * 16 + 16)
                    nc.vector.tensor_tensor_reduce(out=junk_v[:, :], in0=adj_b[:, j, :], in1=xn0[:, :], scale=1.0,
                                                   scalar=0.0, op0=ALU.mult, op1=ALU.add,
                                                   accum_out=s_col[:, j:j + 1]).then_inc(adj_summed, 1)
                    if not first(g, j):
                        second(g, j - 1)
                    wait(dve, adj_summed, g * GT + (j + 1))
                    wait(dve, adj_counted, g * GT + (j + 1))
                    link(nc.vector.scalar_tensor_tensor(sg_col[:, j:j + 1], r_col[:, j:j + 1], 0.0,
                                                        s_col[:, j:j + 1], ALU.is_gt, ALU.mult))
                    wait(dve, self_done, g * GT + (j + 1))
                    nc.vector.scalar_tensor_tensor(z_b[:, :], wn_bc[:, :], sg_col[:, j:j + 1], ps_g[j % 2][:, 0:D],
                                                   ALU.mult, ALU.add).then_inc(z_done, 1)
                    wait(dve, z_done, g * GT + (j + 1))
                    if j >= 2:
                        wait(dve, tile_stored[j % 2], g * 64 + 32)
                    else:
                        wait(dve, tile_stored[j % 2], g * 64)
                    nc.vector.scalar_tensor_tensor(x1_b[:, j % 2, :], z_b[:, :], 0.0, x_t,
                                                   ALU.max, ALU.add).then_inc(x1_ready, 1)
                    wait(dve, x1_ready, g * GT + (j + 1))
                    nc.vector.bn_stats(st2[:, :], x1_b[:, j % 2, :]).then_inc(row_stats, 1)
                    dve.wait_ge(row_stats, 1)
                    dve.sem_clear(row_stats)
                    link(nc.vector.bn_aggr(mv2[:, j % 2, :], st2[:, :]))
                    nc.vector.tensor_scalar(ve2[:, j % 2:j % 2 + 1], mv2[:, j % 2, 1:2], EPS, None,
                                            ALU.add).then_inc(var_ready, 1)
                    assert link.n == PER - first(g, j)

            from_zero(dve, body, NG, apart=2)
            link.at(START + NT * PER - 1)
            second(NG - 1, GT - 1)

        @block.tensor
        def _(pe):
            pe.wait_ge(consts, 3)
            pe.wait_ge(w_in, 16 * N_WEIGHTS)
            for kc in range(KC):
                for dc in range(KC):
                    last = nc.tensor.transpose(ps_x[:, kc * D + dc * P:kc * D + (dc + 1) * P],
                                               ws[:, dc, kc * P:(kc + 1) * P], ident[:, :])
            last.then_inc(spread, 1)
            pe.wait_ge(xn0_diag, 1)
            for g, bank in enumerate((ps_t1, ps_t2, ps_g[0], ps_g[1])):
                nc.tensor.matmul(bank[:, :], ones[:, :], diag[:, g * GT:(g + 1) * GT, :], start=True,
                                 stop=True).then_inc(spread, 1)
            pe.wait_ge(wn_diag_s, 1)
            nc.tensor.matmul(ps_v[:, 0:D], ones[:, :], wn_diag[:, :, :], start=True, stop=True).then_inc(spread, 1)
            pe.wait_ge(spread_out, N_SPREAD)
            def body(g):
                for j in range(GT):
                    t1 = g * GT + (j + 1)
                    wait(pe, xn_ready, t1)
                    wait(pe, xnt_ready, g * GT + j)
                    for kc in range(KC):
                        last = nc.tensor.transpose(ps_t1[:, kc * P:(kc + 1) * P], xn_b[:, j % 2, kc * P:(kc + 1) * P],
                                                   ident[:, :])
                    last.then_inc(xn_turned, 1)
                    wait(pe, xnt_ready, t1)
                    wait(pe, z_done, g * GT + (j - 1))
                    for kc in range(KC):
                        last = nc.tensor.matmul(ps_g[j % 2][:, 0:D], xnt_b[:, j % 2, kc, :], ws_t[:, kc, :],
                                                start=kc == 0, stop=kc == KC - 1)
                    last.then_inc(self_done, 1)
                    if not first(g, j):
                        second(g, j - 1)
                    if j == 0 and not first(g, j):
                        queries_keys(g - 1)

            def second(g, j):
                t1 = g * GT + (j + 1)
                wait(pe, xn2_ready, t1)
                wait(pe, xn2t_ready, g * GT + j)
                for kc in range(KC):
                    last = nc.tensor.transpose(ps_t2[:, kc * P:(kc + 1) * P], xn2_b[:, j % 2, kc * P:(kc + 1) * P],
                                               ident[:, :])
                last.then_inc(xn2_turned, 1)
                wait(pe, xn2t_ready, t1)
                wait(pe, v_out, g * GT + j)
                for kc in range(KC):
                    last = nc.tensor.matmul(ps_v[:, 0:D], xn2_t[:, kc, j % GT * P:(j % GT + 1) * P], wv[:, kc, :],
                                            start=kc == 0, stop=kc == KC - 1)
                last.then_inc(v_done, 1)

            def queries_keys(g):
                for c in range(2 * KC):
                    w = wq if c < KC else wk
                    wait(pe, qk_hi, g * (2 * KC) + (c - 1))
                    for kc in range(KC):
                        last = nc.tensor.matmul(ps_q[c % 2][:, :], w[:, kc, (c % KC) * P:(c % KC + 1) * P],
                                                xn2_t[:, kc, :], start=kc == 0, stop=kc == KC - 1)
                    last.then_inc(qk_done, 1)

            from_zero(pe, body, NG, apart=2)
            second(NG - 1, GT - 1)
            queries_keys(NG - 1)

        @block.scalar
        def _(act):
            act.wait_ge(spread, 1)
            nc.scalar.activation(ws_t[:, :, :].rearrange("p a b -> p (a b)"), ps_x[:, :], ACT.Copy).then_inc(spread_out, 1)
            for g, bank in enumerate((ps_t1, ps_t2, ps_g[0], ps_g[1])):
                act.wait_ge(spread, g + 2)
                nc.scalar.activation(xn0[:, g * GW:(g + 1) * GW], bank[:, :], ACT.Copy).then_inc(spread_out, 1)
            act.wait_ge(spread, NG + 2)
            nc.scalar.activation(wn_bc[:, :], ps_v[:, 0:D], ACT.Copy).then_inc(spread_out, 1)
            act.wait_ge(b_in, 32)
            nc.scalar.activation(bqk_s[:, :, :], bqk[:, :, :], ACT.Copy, scale=QS).then_inc(spread_out, 1)
            act.wait_ge(spread_out, N_SPREAD + 1)
            def body(g):
                for j in range(GT):
                    t1 = g * GT + (j + 1)
                    wait(act, xn_turned, t1)
                    wait(act, self_done, g * GT + (j - 1))
                    nc.scalar.activation(xnt_b[:, j % 2, :, :].rearrange("p a b -> p (a b)"), ps_t1[:, 0:D],
                                         ACT.Copy).then_inc(xnt_ready, 1)
                    wait(act, adj_in[j], g * 16 + 16)
                    nc.scalar.activation(junk_a[:, :], adj_b[:, j, :], ACT.Copy,
                                         accum_out=r_col[:, j:j + 1]).then_inc(adj_counted, 1)
                    if not first(g, j):
                        second(g, j - 1)
                    if j == 0 and not first(g, j):
                        queries_keys(g - 1)

            def second(g, j):
                t1 = g * GT + (j + 1)
                wait(act, xn2_turned, t1)
                if j == 0:
                    wait(act, qk_done, g * (2 * KC))
                nc.scalar.activation(xn2_t[:, :, j % GT * P:(j % GT + 1) * P],
                                     ps_t2[:, 0:D].rearrange("p (c q) -> p c q", c=KC),
                                     ACT.Copy).then_inc(xn2t_ready, 1)
                wait(act, v_done, t1)
                nc.scalar.activation(v_all[:, bass.ds(g * GT + j, 1), :, :].rearrange("p a h d -> p (a h) d"),
                                     ps_v[:, 0:D].rearrange("p (h d) -> p h d", h=H), ACT.Copy).then_inc(v_out, 1)

            def queries_keys(g):
                for c in range(2 * KC):
                    wait(act, qk_done, g * (2 * KC) + (c + 1))
                    wait(act, qk_split, g * (2 * KC) + (c - 1))
                    wait(act, qk_stored[c % 2], g * (4 * 16) + c // 2 * 32)
                    b16 = bqk_s[:, c // KC, c % KC:c % KC + 1]
                    nc.scalar.activation(qk32[:, c % 2, :], ps_q[c % 2][:, :], ACT.Identity, bias=b16, scale=QS)
                    nc.scalar.activation(qk16[:, c % 2, 0, :], ps_q[c % 2][:, :], ACT.Identity, bias=b16,
                                         scale=QS).then_inc(qk_hi, 1)

            from_zero(act, body, NG, apart=2)
            second(NG - 1, GT - 1)
            queries_keys(NG - 1)


def phase_attend(nc, T, dr):
    UNITS, LAST = H * NG, H * NG - 1
    QW = 3 * HD
    QM = QW + 2
    PIECES = NT
    GROUPS = NT // KG

    with ExitStack() as ctx:
        def sb(name, shape, dt=F32):
            return ctx.enter_context(nc.sbuf_tensor(name, shape, dt))

        def sem(name):
            return ctx.enter_context(nc.semaphore(name))

        ident, v_all = T["ident"], T["v_all"]
        q_st = sb("q_st", [P, NG, GW], F16)
        k_st = sb("k_st", [P, 2, N], F16)
        p_ring = sb("p_ring", [P, PR, GW])
        stage = sb("stage", [P, 2, FF])
        max_part = sb("max_part", [P, PIECES])
        max_col = sb("max_col", [P, GT])
        max_row = sb("max_row", [GT, 2, P], F16)
        v_head = sb("v_head", [P, 2, NT, HD])
        ones = sb("ones_b", [P, HD])
        add_up = sb("add_up", [P, HD])
        o_raw, d_raw = sb("o_raw", [P, GW]), sb("d_raw", [P, GW])
        inv, o_unit = sb("inv", [P, P]), sb("o_unit", [P, P])
        ps_m = [ctx.enter_context(nc.psum_tensor(f"ps_m{n}", [P, 512], F32)) for n in range(2)]
        ps_e = [ctx.enter_context(nc.psum_tensor(f"ps_e{n}", [P, 512], F32)) for n in range(2)]
        ps_o = ctx.enter_context(nc.psum_tensor("ps_o", [P, 512], F32))
        ps_d = ctx.enter_context(nc.psum_tensor("ps_d", [P, 512], F32))
        ps_s = ctx.enter_context(nc.psum_tensor("ps_s", [P, 512], F32))
        ps_r = ctx.enter_context(nc.psum_tensor("ps_r", [P, 512], F32))

        q_in = [sem(f"q_in{c}") for c in range(NG)]
        row_in = [sem(f"row_in{c}") for c in range(NG)]
        k_in, k_const = sem("k_in"), sem("k_const")
        piece_done, piece_max = sem("piece_done"), [sem(f"piece_max{n}") for n in range(2)]
        max_ready, max_turned, row_ready = sem("max_ready"), sem("max_turned"), sem("row_ready")
        scores_done, probs_ready = sem("scores_done"), sem("probs_ready")
        values_done, sums_done = sem("values_done"), sem("sums_done")
        row_hi, ones_ready, v_ready, add_ready = sem("row_hi"), sem("ones_ready"), sem("v_ready"), sem("add_ready")
        o_copied, d_copied, added_up = sem("o_copied"), sem("d_copied"), sem("added_up")
        inv_ready, o_normed, o_stored = sem("inv_ready"), sem("o_normed"), sem("o_stored")
        stage_in = [sem("stage_in0"), sem("stage_in1")]
        w_step, w_split = sem("w_step"), sem("w_split")
        block = ctx.enter_context(nc.Block())

        def ge(eng, s, b, n, per, extra):
            if isinstance(b, int):
                if per * (4 * b + n) + extra > 0:
                    eng.wait_ge(s, per * (4 * b + n) + extra)
            else:
                eng.wait_ge(s, b * (4 * per) + (per * n + extra))

        def head_ge(eng, s, b, n, per, extra=0):
            eng.wait_ge(s, (b + n // NG + 1) * per + extra if isinstance(b, int) else b * per + (per * (n // NG + 1) + extra))

        def over_units(eng, step):
            step(0, 0)
            with eng.Fori(0, H - 1) as b:
                for n in range(1, NG + 1):
                    step(b, n)
            for n in range(1, NG):
                step(H - 1, n)

        def exists(b, n):
            return not isinstance(b, int) or NG * b + n < UNITS

        def first(b, n):
            return isinstance(b, int) and NG * b + n == 0

        w1 = dr["W1"].rearrange("e (c p) f -> c p e f", p=P)
        w2 = dr["W2"].rearrange("e (f p) d -> p e f d", p=P)

        @block.sync
        def _(sp):
            def load_q(b, n):
                c, head = n % NG, b + n // NG
                for part, row in ((0, 0), (1, HD), (0, 2 * HD)):
                    sp.dma_start(q_st[row:row + HD, c, :],
                                 dr["qh"][part, bass.ds(head * HD, HD), c * GW:(c + 1) * GW]).then_inc(q_in[c], 16)

            def load_k(head, parity):
                for part, row in ((0, 0), (0, HD), (1, 2 * HD)):
                    sp.dma_start(k_st[row:row + HD, parity, :],
                                 dr["kh"][part, bass.ds(head * HD, HD), :]).then_inc(k_in, 16)

            def store_row(b, n):
                c = n % NG
                for part in range(2):
                    sp.dma_start(q_st[QW + part:QW + part + 1, c, :], max_row[:, part, :]).then_inc(row_in[c], 16)

            def store_output(b, n):
                c, head = (n - 1) % NG, b + (n - 1) // NG
                ge(sp, o_normed, b, n, 1, 0)
                sp.dma_start(dr["ot"][bass.ds(head, 1), c, :, :].rearrange("a p q -> p (a q)"),
                             o_unit[:, :]).then_inc(o_stored, 16)

            def step(b, n):
                ge(sp, scores_done, b, n, NT, 0)
                if exists(b, n + 3):
                    load_q(b, n + 3)
                if n == 1 and exists(b, NG):
                    load_k(b + 1, bass.ds((b + 1) % 2, 1))
                if exists(b, n + 1):
                    ge(sp, row_ready, b, n, 1, 2)
                    store_row(b, n + 1)
                if not first(b, n):
                    store_output(b, n)

            load_k(0, bass.ds(0, 1))
            for n in range(3):
                load_q(0, n)
            sp.wait_ge(row_ready, 1)
            store_row(0, 0)
            over_units(sp, step)
            store_output(H - 1, NG)
            sp.wait_ge(o_stored, 16 * UNITS)

        @block.gpsimd
        def _(pool):
            nc.gpsimd.memset(k_st[QW:QM, :, :], -MS).then_inc(k_const, 1)
            pool.wait_ge(k_const, 1)
            nc.gpsimd.memset(ones[:, :], 1.0).then_inc(ones_ready, 1)
            pool.wait_ge(ones_ready, 1)
            with pool.Fori(0, E) as e:
                one = bass.ds(e, 1)
                for c in range(4):
                    pool.wait_ge(stage_in[c % 2], 16)
                    pool.sem_clear(stage_in[c % 2])
                    raw = stage[:, c % 2, :]
                    if c < KC:
                        hi, lo = (T[w][:, one, c, :].rearrange("p a f -> p (a f)") for w in ("w1h", "w1l"))
                    else:
                        hi, lo = (T[w][:, one, (c - KC) * 4:(c - KC + 1) * 4, :].rearrange("p a f d -> p (a f d)")
                                  for w in ("w2h", "w2l"))
                    nc.gpsimd.tensor_scalar(raw, raw, WS, None, ALU.mult).then_inc(w_step, 1)
                    pool.wait_ge(w_step, 1)
                    nc.gpsimd.tensor_copy(hi, raw).then_inc(w_step, 1)
                    pool.wait_ge(w_step, 2)
                    pool.sem_clear(w_step)
                    nc.gpsimd.tensor_tensor(lo, raw, hi, ALU.subtract).then_inc(w_split, 1)

        @block.tensor
        def _(pe):
            def piece_of_maxima(b, n, j):
                c = n % NG
                if j == 0:
                    head_ge(pe, q_in[c], b, n, 48)
                    head_ge(pe, k_in, b, n, 48)
                ge(pe, piece_max[j % 2], b, n, PIECES // 2, j // 2)
                par = bass.ds((b + n // NG) % 2, 1)
                nc.tensor.matmul(ps_m[j % 2][:, :], q_st[0:QW, c, (j // NG) * P:(j // NG + 1) * P],
                                 k_st[0:QW, par, (j % NG) * GW:(j % NG + 1) * GW].rearrange("p a k -> p (a k)"),
                                 start=True, stop=True).then_inc(piece_done, 1)

            def turn_maxima(b, n):
                ge(pe, max_ready, b, n, 1, 1)
                ge(pe, row_ready, b, n, 1, 0)
                nc.tensor.transpose(ps_r[0:GT, 0:P], max_col[:, :], ident[:, :]).then_inc(max_turned, 1)

            def values(b, n, g):
                ge(pe, probs_ready, b, n, NT, KG * (g + 1))
                if g == 0:
                    ge(pe, o_copied, b, n, 1, 0)
                    if n % NG == 0:
                        head_ge(pe, v_ready, b, n, 2, -1)
                    else:
                        head_ge(pe, v_ready, b, n, 2, 0)
                for i in range(KG):
                    j = KG * g + i
                    m = nc.tensor.matmul(ps_o[i * HD:(i + 1) * HD, :], v_head[:, min(n % NG, 1), j, :], p_ring[:, j % PR, :],
                                         start=g == 0, stop=g == GROUPS - 1, skip_group_check=True)
                m.then_inc(values_done, 1)

            def sums(b, n, g):
                if g == 0:
                    ge(pe, d_copied, b, n, 1, 0)
                for i in range(KG):
                    m = nc.tensor.matmul(ps_d[i * HD:(i + 1) * HD, :], ones[:, :], p_ring[:, (KG * g + i) % PR, :],
                                         start=g == 0, stop=g == GROUPS - 1, skip_group_check=True)
                m.then_inc(sums_done, 1)

            def over_column_tiles(b, n):
                ge(pe, o_copied, b, n, 1, 1)
                ge(pe, d_copied, b, n, 1, 1)
                ge(pe, o_normed, b, n, 1, 0)
                for g in range(GT):
                    nc.tensor.matmul(ps_s[g * HD:(g + 1) * HD, 0:P], add_up[:, :], o_raw[:, g * P:(g + 1) * P],
                                     start=True, stop=True, skip_group_check=True)
                for g in range(GT):
                    m = nc.tensor.matmul(ps_s[g * HD:(g + 1) * HD, P:2 * P], add_up[:, :], d_raw[:, g * P:(g + 1) * P],
                                         start=True, stop=True, skip_group_check=True)
                m.then_inc(added_up, 1)

            def step(b, n):
                c = n % NG
                par = bass.ds((b + n // NG) % 2, 1)
                for j in range(NT):
                    if j == 0:
                        head_ge(pe, row_in[c], b, n, 32)
                    ge(pe, probs_ready, b, n, NT, j - 1)
                    nc.tensor.matmul(ps_e[j % 2][:, :],
                                     k_st[0:QM, par, j * P:(j + 1) * P].rearrange("p a k -> p (a k)"),
                                     q_st[0:QM, c, :], start=True, stop=True).then_inc(scores_done, 1)
                    if exists(b, n + 2):
                        piece_of_maxima(b, n + 2, j)
                    if j % KG in (1, 3) and not (first(b, n) and j < KG):
                        part = values if j % KG == 1 else sums
                        if j < KG:
                            part(b, n - 1, GROUPS - 1)
                        else:
                            part(b, n, j // KG - 1)
                    if j == 5 and exists(b, n + 1):
                        turn_maxima(b, n + 1)
                    if j == 8 and not first(b, n):
                        over_column_tiles(b, n - 1)

            pe.wait_ge(k_const, 1)
            for j in range(NT):
                piece_of_maxima(0, 0, j)
            turn_maxima(0, 0)
            for j in range(NT):
                piece_of_maxima(0, 1, j)
            pe.wait_ge(ones_ready, 1)
            pe.wait_ge(add_ready, 1)
            over_units(pe, step)
            values(H - 1, NG - 1, GROUPS - 1)
            sums(H - 1, NG - 1, GROUPS - 1)
            over_column_tiles(H - 1, NG - 1)

        @block.scalar
        def _(act):
            def load_weights(b, n):
                c, one = n % NG, bass.ds(b + n // NG, 1)
                ge(act, w_split, b, n, 1, 0 if n == 1 else -1)
                if c < KC:
                    dst, src = stage[:, c % 2, :], w1[c, :, one, :].rearrange("p a f -> p (a f)")
                else:
                    dst = stage[:, c % 2, :].rearrange("p (f d) -> p f d", d=D)
                    src = w2[:, one, (c - KC) * 4:(c - KC + 1) * 4, :].rearrange("p a f d -> p (a f) d")
                act.dma_start(dst, src).then_inc(stage_in[c % 2], 16)

            def copy_values(b, n):
                ge(act, values_done, b, n, GROUPS, GROUPS)
                ge(act, added_up, b, n, 1, 0)
                nc.scalar.activation(o_raw[:, :], ps_o[:, :], ACT.Copy).then_inc(o_copied, 1)

            def step(b, n):
                for j in range(NT):
                    ge(act, scores_done, b, n, NT, j + 1)
                    if j % KG == 0:
                        ge(act, sums_done, b, n, GROUPS, j // KG - 1)
                    nc.scalar.activation(p_ring[:, j % PR, :], ps_e[j % 2][:, :], ACT.Exp,
                                         scale=SCALE / MS).then_inc(probs_ready, 1)
                    if j == 1 and not first(b, n):
                        copy_values(b, n - 1)
                    if j == 8:
                        load_weights(b, n)

            over_units(act, step)
            copy_values(H - 1, NG - 1)

        @block.vector
        def _(dve):
            def reduce_piece(b, n, i):
                if i == 0:
                    ge(dve, max_ready, b, n, 1, 0)
                ge(dve, piece_done, b, n, PIECES, i + 1)
                nc.vector.tensor_reduce(max_part[:, i:i + 1], ps_m[i % 2][:, :], AX.X, ALU.max).then_inc(piece_max[i % 2], 1)

            def join_maxima(b, n):
                for s in piece_max:
                    ge(dve, s, b, n, PIECES // 2, PIECES // 2)
                ge(dve, max_turned, b, n, 1, 0)
                nc.vector.tensor_reduce(max_col[:, :], max_part[:, :].rearrange("p (q a) -> p q a", q=GT), AX.X,
                                        ALU.max).then_inc(max_ready, 1)

            def make_row(b, n):
                ge(dve, max_turned, b, n, 1, 1)
                if not (isinstance(b, int) and NG * b + n == 0):
                    head_ge(dve, row_in[(n - 1) % NG], b, n - 1, 32)
                nc.vector.tensor_scalar(max_row[:, 0, :], ps_r[0:GT, 0:P], 1.0 / MS, None, ALU.mult).then_inc(row_hi, 1)
                ge(dve, row_hi, b, n, 1, 1)
                nc.vector.scalar_tensor_tensor(max_row[:, 1, :], ps_r[0:GT, 0:P], 1.0 / MS, max_row[:, 0, :],
                                               ALU.mult, ALU.subtract).then_inc(row_ready, 1)

            def copy_sums(b, n):
                ge(dve, sums_done, b, n, GROUPS, GROUPS)
                ge(dve, added_up, b, n, 1, 0)
                nc.vector.tensor_copy(d_raw[:, :], ps_d[:, :]).then_inc(d_copied, 1)

            def normalise(b, n):
                ge(dve, added_up, b, n, 1, 1)
                nc.vector.reciprocal(inv[:, :], ps_s[:, P:2 * P]).then_inc(inv_ready, 1)
                ge(dve, inv_ready, b, n, 1, 1)
                ge(dve, o_stored, b, n, 16, 0)
                nc.vector.tensor_tensor(o_unit[:, :], ps_s[:, 0:P], inv[:, :], ALU.mult).then_inc(o_normed, 1)

            def copy_head(head, which):
                nc.vector.tensor_scalar(v_head[:, which, :, :],
                                        v_all[:, :, bass.ds(head, 1), :].rearrange("p t a d -> p t (a d)"),
                                        1.0, None, ALU.mult).then_inc(v_ready, 1)

            def step(b, n):
                for i in range(PIECES):
                    if exists(b, n + 2):
                        reduce_piece(b, n + 2, i)
                    if i == 5 and exists(b, n + 1):
                        make_row(b, n + 1)
                    if i == 3 and not first(b, n):
                        copy_sums(b, n - 1)
                    if i == 10 and not first(b, n):
                        normalise(b, n - 1)
                    if i == 12 and n == 2 and exists(b, NG):
                        ge(dve, values_done, b, 1, GROUPS, 0)
                        copy_head(b + 1, 0)
                    if i == 12 and n == NG:
                        ge(dve, values_done, b, NG, GROUPS, 0)
                        copy_head(b + 1, 1)
                if exists(b, n + 2):
                    join_maxima(b, n + 2)

            nc.vector.tensor_reduce(add_up[:, :], ident[:, :].rearrange("p (g d) -> p d g", d=HD), AX.X,
                                    ALU.add).then_inc(add_ready, 1)
            copy_head(0, 0)
            copy_head(0, 1)
            for n in range(2):
                for i in range(PIECES):
                    reduce_piece(0, n, i)
                join_maxima(0, n)
                if n == 0:
                    make_row(0, 0)
            over_units(dve, step)
            copy_sums(H - 1, NG - 1)
            normalise(H - 1, NG - 1)


def phase_route(nc, T, dr):
    with ExitStack() as ctx:
        def sb(name, shape, dt=F32):
            return ctx.enter_context(nc.sbuf_tensor(name, shape, dt))

        def ps(name):
            return ctx.enter_context(nc.psum_tensor(name, [P, 512], F32))

        def sem(name):
            return ctx.enter_context(nc.semaphore(name))

        ident = T["ident"]
        h_all = T["v_all"][:, :, :, :].rearrange("p t h d -> p t (h d)")
        ot_all = sb("ot_all", [P, KC, N])
        bv_col = sb("bv_col", [P, KC])
        wo = sb("wo", [P, KC, D])
        gate_w = sb("gate_w", [P, KC, E])
        rows = {n: sb("row_" + n, [P, D]) for n in ("bo", "ln_g", "ln_b")}
        gate_b = sb("gate_bb", [P, E])
        b1_rows = sb("b1_rows", [E * FC, P])
        ot_b = sb("ot_b", [P, 2, KC, P])
        xr_b, y_b, h_b, ht_b = sb("xr_b", [P, 2, D]), sb("y_b", [P, 2, D]), sb("h_b", [P, 2, D]), sb("ht_b", [P, 2, KC, P])
        st, mv, ve, rs, nm = sb("st_c", [P, 6]), sb("mv_c", [P, 2]), sb("ve_c", [P, 1]), sb("rs_c", [P, 1]), sb("nm_c", [P, 1])
        logits = sb("logits", [P, NT, E])
        lmax, den = sb("lmax", [P, NT]), sb("den", [P, NT])
        eq, onehot, ex = sb("eq", [P, NT, E]), sb("onehot", [P, NT, E]), sb("ex", [P, NT, E])
        first = sb("first", [P, NT])
        PAD = NT // 2
        cum = [sb(f"cum{n}", [P, PAD + NT, E]) for n in range(2)]
        many = sb("many", [P, E, NT])
        EPAD = E // 2
        tiles = [sb(f"tiles{n}", [P, EPAD + E]) for n in range(2)]
        base = sb("base", [P, E])
        place, pos_f = sb("place", [P, NT, E]), sb("pos_f", [P, NT])
        below = sb("below", [P, SLOTS, E])
        slot_f = sb("slot_f", [P, SLOTS])
        tri, ones = sb("tri", [P, P]), sb("ones_c", [P, P])
        iota_i = sb("iota_i", [P, E + NT + SLOTS], I32)
        iota_f = sb("iota_f", [P, E + NT + SLOTS])
        ps_b, ps_ht, ps_b1 = ps("ps_b"), ps("ps_ht"), ps("ps_b1")
        ps_gate = [ps("ps_gate0"), ps("ps_gate1")]
        ps_wo = [ps("ps_wo0"), ps("ps_wo1")]

        w_in, b1_in, b2_in = sem("wo_in"), sem("b1_in"), sem("b2_in")
        xr_in = [sem("xr_in0"), sem("xr_in1")]
        row_stats = sem("row_stats_c")
        consts, chain = sem("consts_c"), sem("dve_chain_c")
        ot_in, ot_ready, wo_done = sem("ot_in"), sem("ot_ready"), sem("wo_done")
        y_part, y_ready, var_ready, rstd_ready = sem("y_part"), sem("y_ready"), sem("var_ready_c"), sem("rstd_ready_c")
        h_ready, h_kept, h_turned, ht_ready = sem("h_ready"), sem("h_kept"), sem("h_turned"), sem("ht_ready")
        gate_done, gate_out = sem("gate_done"), sem("gate_out")
        b1_turned, b1_out = sem("b1_turned"), sem("b1_out")
        onehot_ready, counted, less_max, exps_ready = sem("onehot_ready"), sem("counted"), sem("less_max"), sem("exps_ready")
        pos_ready, scattered = sem("pos_ready"), [sem(f"scattered{n}") for n in range(4)]
        block = ctx.enter_context(nc.Block())
        N_W = 7

        @block.sync
        def _(sp):
            sp.dma_start(bv_col[:, :], dr["bv"].rearrange("(c p) -> p c", p=P),
                         allow_slow_non_contiguous=True).then_inc(w_in, 16)
            sp.dma_start(wo[:, :, :], dr["Wo"].rearrange("(c p) d -> p c d", p=P)).then_inc(w_in, 16)
            for head in range(H):
                rows_h = slice(head * HD % P, head * HD % P + HD)
                sp.dma_start(ot_all[rows_h, head * HD // P, :].rearrange("d (t q) -> d t q", q=P),
                             dr["ot"][head, :, :, :].rearrange("c (g d) q -> d (c g) q", d=HD)).then_inc(ot_in, 16)
            sp.dma_start(gate_w[:, :, :], dr["gate_W"].rearrange("(c p) e -> p c e", p=P)).then_inc(w_in, 16)
            for n, r in rows.items():
                sp.dma_start(r[:, :], dr[n].partition_broadcast(P)).then_inc(w_in, 16)
            sp.dma_start(gate_b[:, :], dr["gate_b"].partition_broadcast(P)).then_inc(w_in, 16)
            for j in range(2):
                sp.dma_start(xr_b[:, j, :], dr["xn2"][j * P:(j + 1) * P, :]).then_inc(xr_in[j], 16)
            sp.dma_start(b1_rows[:, :], dr["b1"].rearrange("e (f p) -> (e f) p", p=P)).then_inc(b1_in, 16)
            sp.dma_start(T["b2_bc"][:, :, :], dr["b2"].partition_broadcast(P)).then_inc(b2_in, 16)
            with sp.Fori(1, NT // 2) as b:
                for j in range(2):
                    wait(sp, y_ready, b * 2 + (j - 1))
                    sp.dma_start(xr_b[:, j, :], dr["xn2"][bass.ds(b * (2 * P) + j * P, P), :]).then_inc(xr_in[j], 16)
            sp.wait_ge(b2_in, 16)

        @block.gpsimd
        def _(pool):
            nc.gpsimd.memset(ones[:, :], 1.0).then_inc(consts, 1)
            nc.gpsimd.memset(tri[:, :], 1.0).then_inc(consts, 1)
            for t in (*cum, *tiles):
                nc.gpsimd.memset(t[:, ...] if len(t.shape) == 2 else t[:, :, :], 0.0).then_inc(consts, 1)
            nc.gpsimd.iota(iota_i[:, 0:E], [[1, E]], base=-E, channel_multiplier=0).then_inc(consts, 1)
            nc.gpsimd.iota(iota_i[:, E:E + NT], [[P, NT]], base=0, channel_multiplier=0).then_inc(consts, 1)
            nc.gpsimd.iota(iota_i[:, E + NT:], [[1, SLOTS]], base=0, channel_multiplier=0).then_inc(consts, 1)
            pool.wait_ge(consts, 9)
            nc.gpsimd.affine_select(out=tri[:, :], in_=tri[:, :], compare_op=ALU.is_gt, fill=0.0,
                                    base=0, pattern=[[1, P]], channel_multiplier=-1).then_inc(consts, 1)
            nc.gpsimd.tensor_copy(iota_f[:, :], iota_i[:, :]).then_inc(consts, 1)
            def body(b):
                for j in range(2):
                    wait(pool, var_ready, b * 2 + (j + 1))
                    nc.gpsimd.tensor_tensor(rs[:, :], ve[:, :], T["minus_half"][:, 0:1], ALU.pow).then_inc(rstd_ready, 1)

            from_zero(pool, body, NT // 2)
            pool.wait_ge(h_kept, NT)
            pool.wait_ge(pos_ready, 1)
            for t in range(NT):
                pool.indirect_dma_start(dr["hs"], bass.IndirectOffsetOnAxis(ap=T["pos"][:, t:t + 1], axis=0),
                                        h_all[:, t, :], None).then_inc(scattered[t % 4], 16)
            for n in range(4):
                pool.wait_ge(scattered[n], 16 * NT // 4)

        @block.vector
        def _(dve):
            link = Link(dve, chain)
            dve.wait_ge(w_in, 16 * N_W)
            PER = 4
            def body(b):
                for j in range(2):
                    link.at(b * (2 * PER) + j * PER)
                    wait(dve, wo_done, b * 2 + (j + 1))
                    nc.vector.tensor_tensor(y_b[:, j, :], ps_wo[j][:, 0:D], rows["bo"][:, :], ALU.add).then_inc(y_part, 1)
                    wait(dve, y_part, b * 2 + (j + 1))
                    wait(dve, xr_in[j], b * 16 + 16)
                    nc.vector.tensor_tensor(y_b[:, j, :], y_b[:, j, :], xr_b[:, j, :], ALU.add).then_inc(y_ready, 1)
                    wait(dve, y_ready, b * 2 + (j + 1))
                    nc.vector.bn_stats(st[:, :], y_b[:, j, :]).then_inc(row_stats, 1)
                    dve.wait_ge(row_stats, 1)
                    dve.sem_clear(row_stats)
                    link(nc.vector.bn_aggr(mv[:, :], st[:, :]))
                    nc.vector.tensor_scalar(ve[:, :], mv[:, 1:2], EPS, None, ALU.add).then_inc(var_ready, 1)
                    wait(dve, rstd_ready, b * 2 + (j + 1))
                    link(nc.vector.scalar_tensor_tensor(nm[:, :], mv[:, 0:1], -1.0, rs[:, :], ALU.mult, ALU.mult))
                    link(nc.vector.tensor_scalar(y_b[:, j, :], y_b[:, j, :], rs[:, :], nm[:, :], ALU.mult, ALU.add))
                    link(nc.vector.tensor_tensor(y_b[:, j, :], y_b[:, j, :], rows["ln_g"][:, :], ALU.mult))
                    assert link.n == PER
                    wait(dve, h_turned, b * 2)
                    nc.vector.tensor_tensor(h_b[:, j, :], y_b[:, j, :], rows["ln_b"][:, :], ALU.add).then_inc(h_ready, 1)
                    nc.vector.tensor_tensor(h_all[:, bass.ds(b * 2 + j, 1), :].rearrange("p a d -> p (a d)"),
                                            y_b[:, j, :], rows["ln_b"][:, :], ALU.add).then_inc(h_kept, 1)
                for j in range(2):
                    wait(dve, gate_done, b * 2 + (j + 1))
                    nc.vector.tensor_tensor(logits[:, bass.ds(b * 2 + j, 1), :].rearrange("p a e -> p (a e)"),
                                            ps_gate[j][:, 0:E], gate_b[:, :], ALU.add).then_inc(gate_out, 1)

            from_zero(dve, body, NT // 2)
            link.at(NT * PER)
            dve.wait_ge(gate_out, NT)
            dve.wait_ge(consts, 11)
            TE = [P, NT, E]
            ids = iota_f[:, 0:E].unsqueeze(1).to_broadcast(TE)
            link(nc.vector.tensor_reduce(lmax[:, :], logits[:, :, :], AX.X, ALU.max))
            hi = lmax[:, :].unsqueeze(2).to_broadcast(TE)
            nc.vector.tensor_tensor(ex[:, :, :], logits[:, :, :], hi, ALU.subtract).then_inc(less_max, 1)
            link(nc.vector.tensor_tensor(eq[:, :, :], logits[:, :, :], hi, ALU.is_equal))
            link(nc.vector.tensor_tensor(eq[:, :, :], eq[:, :, :], ids, ALU.mult))
            link(nc.vector.tensor_reduce(first[:, :], eq[:, :, :], AX.X, ALU.min))
            nc.vector.tensor_tensor(onehot[:, :, :], ids, first[:, :].unsqueeze(2).to_broadcast(TE),
                                    ALU.is_equal).then_inc(onehot_ready, 1)
            dve.wait_ge(exps_ready, 1)
            link(nc.vector.tensor_reduce(den[:, :], ex[:, :, :], AX.X, ALU.add))
            link(nc.vector.reciprocal(T["gw"][:, :], den[:, :]))
            dve.wait_ge(counted, 1)
            link(nc.vector.tensor_copy(cum[0][:, PAD:, :], ps_b1[:, P:2 * P].rearrange("p (t e) -> p t e", e=E)))
            at = 0
            for step in (1, 2, 4, 8):
                link(nc.vector.tensor_tensor(cum[1 - at][:, PAD:, :], cum[at][:, PAD:, :],
                                             cum[at][:, PAD - step:PAD + NT - step, :], ALU.add))
                at = 1 - at
            cum_t = cum[at]
            link(nc.vector.tensor_tensor(many[:, :, :], cum_t[:, PAD + NT - 1, :].unsqueeze(2).to_broadcast([P, E, NT]),
                                         iota_f[:, E:E + NT].unsqueeze(1).to_broadcast([P, E, NT]), ALU.is_gt))
            link(nc.vector.tensor_reduce(tiles[0][:, EPAD:], many[:, :, :], AX.X, ALU.add))
            link(nc.vector.tensor_scalar(base[:, :], tiles[0][:, EPAD:], -1.0, None, ALU.mult))
            at = 0
            for step in (1, 2, 4):
                link(nc.vector.tensor_tensor(tiles[1 - at][:, EPAD:], tiles[at][:, EPAD:],
                                             tiles[at][:, EPAD - step:EPAD + E - step], ALU.add))
                at = 1 - at
            ends = tiles[at][:, EPAD:]
            link(nc.vector.tensor_tensor(base[:, :], base[:, :], ends, ALU.add))
            link(nc.vector.tensor_scalar(base[:, :], base[:, :], float(P), None, ALU.mult))
            link(nc.vector.tensor_tensor(place[:, :, :], ps_b1[:, 0:P].rearrange("p (t e) -> p t e", e=E),
                                         cum_t[:, PAD - 1:PAD + NT - 1, :], ALU.add))
            link(nc.vector.tensor_tensor(place[:, :, :], place[:, :, :], base[:, :].unsqueeze(1).to_broadcast(TE), ALU.add))
            link(nc.vector.tensor_tensor(place[:, :, :], place[:, :, :], onehot[:, :, :], ALU.mult))
            link(nc.vector.tensor_reduce(pos_f[:, :], place[:, :, :], AX.X, ALU.add))
            nc.vector.tensor_copy(T["pos"][:, :], pos_f[:, :]).then_inc(pos_ready, 1)
            link(nc.vector.tensor_tensor(below[:, :, :], ends.unsqueeze(1).to_broadcast([P, SLOTS, E]),
                                         iota_f[:, E + NT:].unsqueeze(2).to_broadcast([P, SLOTS, E]), ALU.is_le))
            link(nc.vector.tensor_reduce(slot_f[:, :], below[:, :, :], AX.X, ALU.add))
            link(nc.vector.tensor_scalar(slot_f[:, :], slot_f[:, :], float(E - 1), None, ALU.min))
            link(nc.vector.tensor_copy(T["slot_e"][:, :], slot_f[:, :]))

        @block.tensor
        def _(pe):
            pe.wait_ge(w_in, 16 * N_W)
            def body(b):
                for j in range(2):
                    t1 = b * 2 + (j + 1)
                    wait(pe, ot_ready, t1)
                    wait(pe, y_part, b * 2)
                    for kc in range(KC):
                        last = nc.tensor.matmul(ps_wo[j][:, 0:D], ot_b[:, j, kc, :], wo[:, kc, :],
                                                start=kc == 0, stop=kc == KC - 1)
                    last.then_inc(wo_done, 1)
                wait(pe, gate_out, b * 2)
                for j in range(2):
                    t1 = b * 2 + (j + 1)
                    wait(pe, h_ready, t1)
                    wait(pe, ht_ready, b * 2 + j)
                    for kc in range(KC):
                        last = nc.tensor.transpose(ps_ht[:, kc * P:(kc + 1) * P], h_b[:, j, kc * P:(kc + 1) * P], ident[:, :])
                    last.then_inc(h_turned, 1)
                for j in range(2):
                    wait(pe, ht_ready, b * 2 + (j + 1))
                    for kc in range(KC):
                        last = nc.tensor.matmul(ps_gate[j][:, 0:E], ht_b[:, j, kc, :], gate_w[:, kc, :],
                                                start=kc == 0, stop=kc == KC - 1)
                    last.then_inc(gate_done, 1)

            from_zero(pe, body, NT // 2)
            pe.wait_ge(b1_in, 16)
            nc.tensor.transpose(ps_b[:, 0:E * FC], b1_rows[:, :], ident[0:E * FC, 0:E * FC]).then_inc(b1_turned, 1)
            pe.wait_ge(onehot_ready, 1)
            pe.wait_ge(consts, 10)
            nc.tensor.matmul(ps_b1[:, 0:P], tri[:, :], onehot[:, :, :], start=True, stop=True)
            nc.tensor.matmul(ps_b1[:, P:2 * P], ones[:, :], onehot[:, :, :], start=True, stop=True).then_inc(counted, 1)

        @block.scalar
        def _(act):
            act.wait_ge(w_in, 16 * N_W)
            act.wait_ge(ot_in, 16 * H)

            def body(b):
                for j in range(2):
                    wait(act, wo_done, b * 2)
                    for kc in range(KC):
                        last = nc.scalar.activation(ot_b[:, j, kc, :], ot_all[:, kc, bass.ds(b * (2 * P) + j * P, P)],
                                                    ACT.Identity, bias=bv_col[:, kc:kc + 1])
                    last.then_inc(ot_ready, 1)
                for j in range(2):
                    wait(act, h_turned, b * 2 + (j + 1))
                    wait(act, gate_done, b * 2)
                    nc.scalar.activation(ht_b[:, j, :, :].rearrange("p a b -> p (a b)"), ps_ht[:, 0:D],
                                         ACT.Copy).then_inc(ht_ready, 1)

            from_zero(act, body, NT // 2)
            act.wait_ge(b1_turned, 1)
            nc.scalar.activation(T["b1_t"][:, :, :].rearrange("p a b -> p (a b)"), ps_b[:, 0:E * FC], ACT.Copy).then_inc(b1_out, 1)
            act.wait_ge(less_max, 1)
            nc.scalar.activation(ex[:, :, :], ex[:, :, :], ACT.Exp).then_inc(exps_ready, 1)


def phase_experts(nc, T, dr):
    HALF = FC // 2
    with ExitStack() as ctx:
        def sb(name, shape, dt=F32):
            return ctx.enter_context(nc.sbuf_tensor(name, shape, dt))

        def ps(name):
            return ctx.enter_context(nc.psum_tensor(name, [P, 512], F32))

        def sem(name):
            return ctx.enter_context(nc.semaphore(name))

        ident, slot_e = T["ident"], T["slot_e"]
        tok = sb("tok", [P, D])
        t32 = sb("t32", [P, KC * P])
        th, tl = sb("th", [P, KC * P], F16), sb("tl", [P, KC * P], F16)
        b1_b = sb("b1_b", [P, FC])
        hid = sb("hid", [P, FC, P])
        hid16 = [sb("hid_h", [P, 2, FC * P], F16), sb("hid_l", [P, 2, FC * P], F16)]
        y_b = sb("y_b_d", [P, D])
        ps_t, ps_y = ps("ps_t"), ps("ps_y")
        ps_h = [ps("ps_h0"), ps("ps_h1")]
        tok_in, y_stored = sem("tok_in"), sem("y_stored")
        turned, t32_ready, th_ready, t_split = sem("turned"), sem("t32_ready"), sem("th_ready"), sem("t_split")
        up_done, b1_ready, gelu_done = sem("up_done"), sem("b1_ready"), sem("gelu_done")
        hid_hi, hid_split, down_done, y_ready = sem("hid_hi"), sem("hid_split"), sem("down_done"), sem("y_ready")
        hid_scaled = sem("hid_scaled")
        block = ctx.enter_context(nc.Block())

        def expert(eng, s):
            slot = slot_e[0:1, s:s + 1] if isinstance(s, int) else slot_e[0:1, bass.ds(s, 1)]
            return eng.value_load(slot, min_val=0, max_val=E - 1)

        def over_slots(eng, step):
            step(0)
            step(1)
            with eng.Fori(2, SLOTS - 1) as s:
                step(s)
            step(SLOTS - 1)

        def first(s):
            return isinstance(s, int) and s == 0

        def final(s):
            return isinstance(s, int) and s == SLOTS - 1

        @block.sync
        def _(sp):
            def load(s):
                if not first(s):
                    sp.wait_ge(turned, s)
                sp.dma_start(tok[:, :], dr["hs"][bass.ds(s * P, P), :]).then_inc(tok_in, 16)

            def store(s):
                sp.wait_ge(y_ready, s + 1)
                sp.dma_start(dr["ys"][bass.ds(s * P, P), :], y_b[:, :]).then_inc(y_stored, 16)

            load(0)
            load(1)
            load(2)
            store(0)
            with sp.Fori(1, SLOTS - 2) as s:
                load(s + 2)
                store(s)
            store(SLOTS - 2)
            store(SLOTS - 1)
            sp.wait_ge(y_stored, 16 * SLOTS)

        @block.tensor
        def _(pe):
            def turn_tokens(s):
                pe.wait_ge(tok_in, s * 16 + 16)
                if not first(s):
                    pe.wait_ge(t32_ready, s)
                for kc in range(KC):
                    last = nc.tensor.transpose(ps_t[:, kc * P:(kc + 1) * P], tok[:, kc * P:(kc + 1) * P], ident[:, :])
                last.then_inc(turned, 1)

            def up(s, e, half):
                if not first(s):
                    pe.wait_ge(gelu_done, s * 2 + (half - 1))
                products = [(w, x, kc) for w, x in (("w1h", th), ("w1h", tl), ("w1l", th)) for kc in range(KC)]
                for f in range(half * HALF, (half + 1) * HALF):
                    for n, (w, x, kc) in enumerate(products):
                        last = nc.tensor.matmul(ps_h[half][:, (f % HALF) * P:(f % HALF + 1) * P],
                                                T[w][:, bass.ds(e, 1), kc, f * P:(f + 1) * P].rearrange("p a f -> p (a f)"),
                                                x[:, kc * P:(kc + 1) * P], start=n == 0, stop=n == len(products) - 1)
                last.then_inc(up_done, 1)

            def down(s, e):
                pe.wait_ge(hid_split, s * 2 + 2)
                if not first(s):
                    pe.wait_ge(y_ready, s)
                par = bass.ds(s % 2, 1)
                n = 0
                for f in range(FC):
                    for x, w in ((0, "w2h"), (0, "w2l"), (1, "w2h")):
                        last = nc.tensor.matmul(ps_y[:, 0:D], hid16[x][:, par, f * P:(f + 1) * P].rearrange("p a q -> p (a q)"),
                                                T[w][:, bass.ds(e, 1), f, :].rearrange("p a d -> p (a d)"),
                                                start=n == 0, stop=n == 3 * FC - 1)
                        n += 1
                last.then_inc(down_done, 1)

            def step(s):
                e = expert(pe, s)
                pe.wait_ge(t_split, s + 1)
                up(s, e, 0)
                if not final(s):
                    turn_tokens(s + 1)
                up(s, e, 1)
                if not first(s):
                    down(s - 1, expert(pe, s - 1))

            turn_tokens(0)
            over_slots(pe, step)
            down(SLOTS - 1, expert(pe, SLOTS - 1))

        @block.scalar
        def _(act):
            def tokens(s):
                act.wait_ge(turned, s + 1)
                if not first(s):
                    act.wait_ge(t_split, s)
                nc.scalar.activation(t32[:, :], ps_t[:, 0:D], ACT.Copy, scale=TS).then_inc(t32_ready, 1)

            def step(s):
                act.wait_ge(b1_ready, s + 1)
                for half in range(2):
                    act.wait_ge(up_done, s * 2 + (half + 1))
                    if not first(s):
                        act.wait_ge(hid_split, s * 2 + (half - 1))
                    for f in range(half * HALF, (half + 1) * HALF):
                        last = nc.scalar.activation(hid[:, f, :], ps_h[half][:, (f % HALF) * P:(f % HALF + 1) * P],
                                                    ACT.Gelu_apprx_tanh, bias=b1_b[:, f:f + 1], scale=1.0 / (TS * WS))
                    last.then_inc(gelu_done, 1)
                    if half == 0 and not final(s):
                        tokens(s + 1)

            tokens(0)
            over_slots(act, step)

        @block.vector
        def _(dve):
            def split_tokens(s):
                dve.wait_ge(t32_ready, s + 1)
                if not first(s):
                    dve.wait_ge(up_done, s * 2)
                nc.vector.tensor_copy(th[:, :], t32[:, :]).then_inc(th_ready, 1)
                dve.wait_ge(th_ready, s + 1)
                nc.vector.tensor_tensor(tl[:, :], t32[:, :], th[:, :], ALU.subtract).then_inc(t_split, 1)

            def bias(s, e):
                if not first(s):
                    dve.wait_ge(gelu_done, s * 2)
                nc.vector.tensor_copy(b1_b[:, :], T["b1_t"][:, bass.ds(e, 1), :].rearrange("p a f -> p (a f)")).then_inc(b1_ready, 1)

            def split_hidden(s, half):
                dve.wait_ge(gelu_done, s * 2 + (half + 1))
                if not (isinstance(s, int) and s < 2):
                    if half == 0:
                        dve.wait_ge(down_done, s - 1)
                raw = hid[:, half * HALF:(half + 1) * HALF, :].rearrange("p f q -> p (f q)")
                par = bass.ds(s % 2, 1)
                hi, lo = (x[:, par, half * HALF * P:(half + 1) * HALF * P].rearrange("p a q -> p (a q)") for x in hid16)
                nc.vector.tensor_scalar(raw, raw, TS, None, ALU.mult).then_inc(hid_scaled, 1)
                dve.wait_ge(hid_scaled, s * 2 + (half + 1))
                nc.vector.tensor_copy(hi, raw).then_inc(hid_hi, 1)
                dve.wait_ge(hid_hi, s * 2 + (half + 1))
                nc.vector.tensor_tensor(lo, raw, hi, ALU.subtract).then_inc(hid_split, 1)

            def output(s, e):
                dve.wait_ge(down_done, s + 1)
                if not first(s):
                    dve.wait_ge(y_stored, s * 16)
                nc.vector.scalar_tensor_tensor(y_b[:, :], ps_y[:, 0:D], 1.0 / (TS * WS),
                                               T["b2_bc"][:, bass.ds(e, 1), :].rearrange("p a d -> p (a d)"),
                                               ALU.mult, ALU.add).then_inc(y_ready, 1)

            def step(s):
                bias(s, expert(dve, s))
                split_hidden(s, 0)
                if not final(s):
                    split_tokens(s + 1)
                split_hidden(s, 1)
                if not first(s):
                    output(s - 1, expert(dve, s - 1))

            split_tokens(0)
            over_slots(dve, step)
            output(SLOTS - 1, expert(dve, SLOTS - 1))


def phase_return(nc, T, dr):
    with ExitStack() as ctx:
        def sb(name, shape, dt=F32):
            return ctx.enter_context(nc.sbuf_tensor(name, shape, dt))

        def sem(name):
            return ctx.enter_context(nc.semaphore(name))

        y_all, x1_all = sb("y_all", [P, NT, D]), sb("x1_all", [P, NT, D])
        x1_in, y_in, summed, stored = sem("x1_in"), [sem(f"y_in{g}") for g in range(NG)], sem("summed"), sem("stored")
        block = ctx.enter_context(nc.Block())

        @block.gpsimd
        def _(pool):
            for t in range(NT):
                pool.indirect_dma_start(y_all[:, t, :], None, dr["ys"],
                                        bass.IndirectOffsetOnAxis(ap=T["pos"][:, t:t + 1], axis=0)).then_inc(y_in[t // GT], 16)

        @block.vector
        def _(dve):
            dve.wait_ge(x1_in, 16)
            for t in range(NT):
                if t % GT == 0:
                    dve.wait_ge(y_in[t // GT], 16 * GT)
                last = nc.vector.scalar_tensor_tensor(y_all[:, t, :], y_all[:, t, :], T["gw"][:, t:t + 1], x1_all[:, t, :],
                                                      ALU.mult, ALU.add).then_inc(summed, 1)

        @block.sync
        def _(sp):
            sp.dma_start(x1_all[:, :, :], dr["x1"].rearrange("(t p) d -> p t d", p=P)).then_inc(x1_in, 16)
            for g in range(NG):
                sp.wait_ge(summed, GT * (g + 1))
                sp.dma_start(dr["out"][g * GW:(g + 1) * GW, :].rearrange("(t p) d -> p t d", p=P),
                             y_all[:, g * GT:(g + 1) * GT, :]).then_inc(stored, 16)
            sp.wait_ge(stored, 16 * NG)


def phase_rest(nc, T, dr, phases):
    with ExitStack() as ctx:
        def sb(name, shape, dt=F32):
            return ctx.enter_context(nc.sbuf_tensor(name, shape, dt))

        for w in ("w1h", "w1l"):
            T[w] = sb(w, [P, E, KC, FF], F16)
        for w in ("w2h", "w2l"):
            T[w] = sb(w, [P, E, FC, D], F16)
        T["pos"] = sb("pos", [P, NT], U32)
        T["gw"] = sb("gw", [P, NT])
        T["slot_e"] = sb("slot_e", [P, SLOTS], I32)
        T["b1_t"] = sb("b1_t", [P, E, FC])
        with ExitStack() as inner:
            phase_attend(nc, T, dr)
            if "C" in phases:
                T["b2_bc"] = inner.enter_context(nc.sbuf_tensor("b2_bc", [P, E, D], F32))
                phase_route(nc, T, dr)
            if "D" in phases:
                phase_experts(nc, T, dr)
        if "E" in phases:
            phase_return(nc, T, dr)


def build(nc, a, out, phases="ABCDE"):
    with ExitStack() as ctx:
        def sb(name, shape, dt=F32):
            return ctx.enter_context(nc.sbuf_tensor(name, shape, dt))

        dr = dict(a)
        dr["out"] = out
        for name, shape, dt in (("x1", (N, D), F32), ("xn2", (N, D), F32), ("qh", (2, D, N), F16), ("kh", (2, D, N), F16), ("ot", (H, NG, P, P), F32),
                                ("hs", (SLOTS * P, D), F32), ("ys", (SLOTS * P, D), F32)):
            dr[name] = nc.dram_tensor(name + "_scratch", shape, dt).ap()
        T = {"ident": sb("ident", [P, P]), "v_all": sb("v_all", [P, NT, H, HD]),
             "minus_half": sb("minus_half", [P, NT]),
             "hs_cleared": ctx.enter_context(nc.semaphore("hs_cleared"))}
        phase_project(nc, T, dr)
        if "B" in phases:
            phase_rest(nc, T, dr, phases)


_INS = {"x": "x", "adj": "adj", "L0_gnn_w_self": "w_self", "L0_gnn_w_neigh": "w_neigh", "L0_ffn_ln1_g": "ln_g",
        "L0_ffn_ln1_b": "ln_b", "L0_ffn_Wq": "Wq", "L0_ffn_bq": "bq", "L0_ffn_Wk": "Wk", "L0_ffn_bk": "bk",
        "L0_ffn_Wv": "Wv", "L0_ffn_bv": "bv", "L0_ffn_Wo": "Wo", "L0_ffn_bo": "bo", "L0_ffn_gate_W": "gate_W",
        "L0_ffn_gate_b": "gate_b", "L0_ffn_W1": "W1", "L0_ffn_b1": "b1", "L0_ffn_W2": "W2", "L0_ffn_b2": "b2"}


def kernel(**inputs):
    import numpy as np
    import concourse.bacc as bacc
    from concourse.bass_utils import run_bass_kernel_spmd

    nc = bacc.Bacc("TRN2", target_bir_lowering=False, num_devices=1)
    arrays, aps = {}, {}
    for name, short in _INS.items():
        arr = np.ascontiguousarray(inputs[name])
        arrays["in_" + short] = arr
        aps[short] = nc.dram_tensor("in_" + short, arr.shape, mybir.dt.from_np(arr.dtype), kind="ExternalInput").ap()
    out = nc.dram_tensor("out", (N, D), F32, kind="ExternalOutput").ap()
    build(nc, aps, out)
    r = run_bass_kernel_spmd(nc, [arrays], core_ids=[0])
    return r.results[0]["out"]
```

```python
import concourse.bass as bass
from concourse import mybir
from contextlib import ExitStack

F32 = mybir.dt.float32
F16 = mybir.dt.float16
I32 = mybir.dt.int32
U32 = mybir.dt.uint32
ALU = mybir.AluOpType
ACT = mybir.ActivationFunctionType
AX = mybir.AxisListType

P = 128
N = 2048
D = 256
H = 8
HD = D // H
E = 8
FF = 4 * D
NT = N // P
KC = D // P
FC = FF // P
GT = 4
NG = NT // GT
GW = GT * P
SLOTS = (N + E * (P - 1)) // P
EPS = 1e-5
QS = 16.0
MS = QS * QS
SCALE = float(HD) ** -0.5
TS = 16.0
WS = 64.0
PR = 8
KG = P // HD


class Link:

    def __init__(self, eng, sem):
        self.eng, self.sem, self.base, self.n, self.most = eng, sem, 0, 0, 0

    def at(self, base):
        self.base, self.n = base, 0

    def __call__(self, ins):
        self.n += 1
        ins.then_inc(self.sem, 1)
        self.eng.wait_ge(self.sem, self.base + self.n)


def from_zero(eng, body, end, apart=1):
    for i in range(apart):
        body(i)
    with eng.Fori(apart, end) as i:
        body(i)


def wait(eng, sem, value):
    if isinstance(value, int):
        if value > 0:
            eng.wait_ge(sem, value)
    else:
        eng.wait_ge(sem, value)


def phase_project(nc, T, dr):
    with ExitStack() as ctx:
        def sb(name, shape, dt=F32):
            return ctx.enter_context(nc.sbuf_tensor(name, shape, dt))

        def ps(name):
            return ctx.enter_context(nc.psum_tensor(name, [P, 512], F32))

        def sem(name):
            return ctx.enter_context(nc.semaphore(name))

        ident, v_all = T["ident"], T["v_all"]
        x_all = sb("x_all", [P, NT, D])
        adj_b = sb("adj_b", [P, GT, N], I32)
        xn0 = sb("xn0", [P, N])
        junk_v = sb("junk_v", [P, N])
        junk_a = sb("junk_a", [P, N])
        ones = sb("ones_a", [P, P])
        ws, wn = sb("ws", [P, KC, D]), sb("wn", [P, KC, D])
        wq, wk, wv = sb("wq", [P, KC, D]), sb("wk", [P, KC, D]), sb("wv", [P, KC, D])
        bqk = sb("bqk", [P, 2, KC])
        bqk_s = sb("bqk_s", [P, 2, KC])
        ws_t = sb("ws_t", [P, KC, D])
        wn_col = sb("wn_col", [P, KC])
        wn_diag = sb("wn_diag", [P, KC, P])
        wn_bc = sb("wn_bc", [P, D])
        stats = sb("stats", [P, NT, 6])
        mean, rstd, nmr = sb("mean", [P, NT]), sb("rstd", [P, NT]), sb("nmr", [P, NT])
        half, col0 = sb("half", [P, NT]), sb("col0", [P, NT])
        xn_b = sb("xn_b", [P, 2, D])
        xnt_b = sb("xnt_b", [P, 2, KC, P])
        s_col, r_col, sg_col = sb("s_col", [P, GT]), sb("r_col", [P, GT]), sb("sg_col", [P, GT])
        z_b = sb("z_b", [P, D])
        x1_b, xn2_b = sb("x1_b", [P, 2, D]), sb("xn2_b", [P, 2, D])
        st2, mv2, nm2 = sb("st2", [P, 6]), sb("mv2", [P, 2, 2]), sb("nm2", [P, 1])
        ve2, rs2 = sb("ve2", [P, 2]), sb("rs2", [P, 2])
        xn2_t = sb("xn2_t", [P, 2, KC, GW])
        xn2t_b = sb("xn2t_b", [P, 2, KC, P])
        qk32 = sb("qk32", [P, 2, GW])
        qk16 = sb("qk16", [P, 2, 2, GW], F16)
        zero_b = sb("zero_b", [P, D])
        diag = junk_v[:, :].rearrange("p (t q) -> p t q", t=NT)

        ps_t1, ps_t2, ps_v = ps("ps_t1"), ps("ps_t2"), ps("ps_v")
        ps_g = [ps("ps_g0"), ps("ps_g1")]
        ps_q = [ps("ps_q0"), ps("ps_q1")]
        ps_x = ps("ps_x")

        x_in, w_in, b_in = [sem(f"x_in{g}") for g in range(NG)], sem("w_in_a"), sem("b_in")
        qkv_in = sem("qkv_in")
        adj_in = [sem(f"adj_in{j}") for j in range(GT)]
        row_stats = sem("row_stats_a")
        consts, dve_chain, zeroed = sem("consts_a"), sem("dve_chain_a"), sem("zeroed")
        xn0_diag, wn_diag_s = sem("xn0_diag"), sem("wn_diag_s")
        spread, spread_out = sem("spread"), sem("spread_out")
        var_ready, rstd_ready = sem("var_ready"), sem("rstd_ready")
        xn_ready, xn_turned, xnt_ready = sem("xn_ready"), sem("xn_turned"), sem("xnt_ready")
        self_done, z_done = sem("self_done"), sem("z_done")
        adj_summed, adj_counted = sem("adj_summed"), sem("adj_counted")
        x1_ready, xn2_ready, xn2_turned, xn2t_ready = sem("x1_ready"), sem("xn2_ready"), sem("xn2_turned"), sem("xn2t_ready")
        xn2t_kept = sem("xn2t_kept")
        v_done, v_out = sem("v_done"), sem("v_out")
        qk_done, qk_hi, qk_split = sem("qk_done"), sem("qk_hi"), sem("qk_split")
        tile_stored = [sem("tile_stored0"), sem("tile_stored1")]
        qk_stored = [sem("qk_stored0"), sem("qk_stored1")]
        block = ctx.enter_context(nc.Block())

        N_WEIGHTS = 2
        N_SPREAD = NG + 2

        def first_group(g):
            return isinstance(g, int) and g == 0

        def first(g, j):
            return first_group(g) and j == 0

        @block.sync
        def _(sp):
            for g in range(NG):
                sp.dma_start(x_all[:, g * GT:(g + 1) * GT, :],
                             dr["x"][g * GW:(g + 1) * GW, :].rearrange("(t p) d -> p t d", p=P)).then_inc(x_in[g], 16)
            for w, src in ((ws, "w_self"), (wn, "w_neigh")):
                sp.dma_start(w[:, :, :], dr[src].rearrange("(c p) d -> p c d", p=P)).then_inc(w_in, 16)
            for j in range(GT):
                sp.dma_start(adj_b[:, j, :], dr["adj"][j * P:(j + 1) * P, :]).then_inc(adj_in[j], 16)
                if j == 0:
                    for w, src in ((wq, "Wq"), (wk, "Wk"), (wv, "Wv")):
                        sp.dma_start(w[:, :, :], dr[src].rearrange("(c p) d -> p c d", p=P)).then_inc(qkv_in, 16)
                    for n, src in enumerate(("bq", "bk")):
                        sp.dma_start(bqk[:, n, :], dr[src].rearrange("(c p) -> p c", p=P),
                                     allow_slow_non_contiguous=True).then_inc(b_in, 16)

            def store_tile(g, j):
                rows = bass.ds(g * GW + j * P, P)
                sp.wait_ge(x1_ready, g * GT + (j + 1))
                sp.dma_start(dr["x1"][rows, :], x1_b[:, j % 2, :]).then_inc(tile_stored[j % 2], 16)
                sp.wait_ge(xn2_ready, g * GT + (j + 1))
                sp.dma_start(dr["xn2"][rows, :], xn2_b[:, j % 2, :]).then_inc(tile_stored[j % 2], 16)

            def store_chunk(g, c):
                cols = bass.ds(g * GW if isinstance(g, int) else sp.snap(g * GW), GW)
                sp.wait_ge(qk_split, g * (2 * KC) + (c + 1))
                dst = dr["qh"] if c < KC else dr["kh"]
                for part in (1, 0):
                    sp.dma_start(dst[part, (c % KC) * P:(c % KC + 1) * P, cols],
                                 qk16[:, c % 2, part, :]).then_inc(qk_stored[c % 2], 16)

            def body(g):
                for j in range(GT):
                    sp.wait_ge(adj_summed, g * GT + (j - GT + 1))
                    sp.wait_ge(adj_counted, g * GT + (j - GT + 1))
                    sp.dma_start(adj_b[:, j, :], dr["adj"][bass.ds(g * GW + j * P, P), :]).then_inc(adj_in[j], 16)
                    store_tile(g - 1, j)
                    if not (isinstance(g, int) and g < 2):
                        store_chunk(g - 2, j)

            body(1)
            with sp.Fori(2, NG) as g:
                body(g)
            for j in range(GT):
                store_tile(NG - 1, j)
                store_chunk(NG - 2, j)
            for c in range(2 * KC):
                store_chunk(NG - 1, c)
            for n in range(2):
                sp.wait_ge(tile_stored[n], NT * 16)
                sp.wait_ge(qk_stored[n], NG * 4 * 16)

        @block.gpsimd
        def _(pool):
            nc.gpsimd.memset(ident[:, :], 0.0).then_inc(zeroed, 1)
            nc.gpsimd.memset(ones[:, :], 1.0).then_inc(consts, 1)
            nc.gpsimd.memset(T["minus_half"][:, :], -0.5).then_inc(consts, 1)
            nc.gpsimd.memset(zero_b[:, :], 0.0).then_inc(zeroed, 1)
            pool.wait_ge(zeroed, 2)
            nc.gpsimd.affine_select(out=ident[:, :], in_=ident[:, :], compare_op=ALU.not_equal, fill=1.0,
                                    base=0, pattern=[[-1, P]], channel_multiplier=1).then_inc(consts, 1)
            pool.dma_start(dr["hs"].rearrange("(s p) d -> p s d", p=P),
                           zero_b[:, :].unsqueeze(1).to_broadcast([P, SLOTS, D])).then_inc(T["hs_cleared"], 16)
            pool.wait_ge(consts, 3)
            pool.wait_ge(var_ready, 1)
            nc.gpsimd.tensor_tensor(rstd[:, :], rstd[:, :], T["minus_half"][:, :], ALU.pow).then_inc(rstd_ready, 1)
            def body(g):
                for j in range(GT):
                    wait(pool, var_ready, g * GT + (j + 2))
                    nc.gpsimd.tensor_tensor(rs2[:, j % 2:j % 2 + 1], ve2[:, j % 2:j % 2 + 1],
                                            T["minus_half"][:, 0:1], ALU.pow).then_inc(rstd_ready, 1)
                    if not first_group(g):
                        split(g - 1, j)

            def split(g, c):
                wait(pool, qk_hi, g * (2 * KC) + (c + 1))
                wait(pool, qk_stored[c % 2], g * (4 * 16) + c // 2 * 32)
                nc.gpsimd.tensor_tensor(qk16[:, c % 2, 1, :], qk32[:, c % 2, :], qk16[:, c % 2, 0, :],
                                        ALU.subtract).then_inc(qk_split, 1)

            from_zero(pool, body, NG, apart=2)
            for c in range(2 * KC):
                split(NG - 1, c)
            pool.wait_ge(T["hs_cleared"], 16)

        @block.vector
        def _(dve):
            link = Link(dve, dve_chain)
            for t in range(NT):
                if t % GT == 0:
                    dve.wait_ge(x_in[t // GT], 16)
                nc.vector.bn_stats(stats[:, t, :], x_all[:, t, :]).then_inc(dve_chain, 1)
            link.at(NT)
            dve.wait_ge(dve_chain, NT)
            link(nc.vector.tensor_tensor(mean[:, :], stats[:, :, 1], stats[:, :, 4], ALU.add))
            link(nc.vector.tensor_scalar(mean[:, :], mean[:, :], 0.5, None, ALU.mult))
            link(nc.vector.tensor_tensor(half[:, :], stats[:, :, 1], mean[:, :], ALU.subtract))
            link(nc.vector.tensor_tensor(half[:, :], half[:, :], half[:, :], ALU.mult))
            link(nc.vector.tensor_tensor(rstd[:, :], stats[:, :, 2], stats[:, :, 5], ALU.add))
            link(nc.vector.scalar_tensor_tensor(rstd[:, :], rstd[:, :], 1.0 / D, half[:, :], ALU.mult, ALU.add))
            nc.vector.tensor_scalar(rstd[:, :], rstd[:, :], EPS, None, ALU.add).then_inc(var_ready, 1)
            dve.wait_ge(rstd_ready, 1)
            link(nc.vector.scalar_tensor_tensor(nmr[:, :], mean[:, :], -1.0, rstd[:, :], ALU.mult, ALU.mult))
            link(nc.vector.tensor_tensor(col0[:, :], x_all[:, :, 0], rstd[:, :], ALU.mult))
            link(nc.vector.tensor_tensor(col0[:, :], col0[:, :], nmr[:, :], ALU.add))
            dve.wait_ge(consts, 3)
            nc.vector.tensor_tensor(diag, ident[:, :].unsqueeze(1).to_broadcast([P, NT, P]),
                                    col0[:, :].unsqueeze(2).to_broadcast([P, NT, P]), ALU.mult).then_inc(xn0_diag, 1)
            dve.wait_ge(w_in, 16 * N_WEIGHTS)
            link(nc.vector.tensor_reduce(wn_col[:, :], wn[:, :, :], AX.X, ALU.add))
            nc.vector.tensor_tensor(wn_diag[:, :, :], ident[:, :].unsqueeze(1).to_broadcast([P, KC, P]),
                                    wn_col[:, :].unsqueeze(2).to_broadcast([P, KC, P]), ALU.mult).then_inc(wn_diag_s, 1)
            dve.wait_ge(spread_out, N_SPREAD)
            START, PER = link.base + link.n, 3
            def second(g, j):
                par = slice(j % 2, j % 2 + 1)
                wait(dve, rstd_ready, g * GT + (j + 2))
                link(nc.vector.scalar_tensor_tensor(nm2[:, :], mv2[:, j % 2, 0:1], -1.0, rs2[:, par], ALU.mult, ALU.mult))
                wait(dve, xn2_turned, g * GT + (j - 1))
                nc.vector.tensor_scalar(xn2_b[:, j % 2, :], x1_b[:, j % 2, :], rs2[:, par], nm2[:, :],
                                    ALU.mult, ALU.add).then_inc(xn2_ready, 1)

            def body(g):
                for j in range(GT):
                    link.at(START if first(g, j) else g * (GT * PER) + (START + j * PER - 1))
                    one = bass.ds(g * GT + j, 1)
                    x_t = x_all[:, one, :].rearrange("p a d -> p (a d)")
                    wait(dve, xn_turned, g * GT + (j - 1))
                    nc.vector.tensor_scalar(xn_b[:, j % 2, :], x_t, rstd[:, one], nmr[:, one],
                                            ALU.mult, ALU.add).then_inc(xn_ready, 1)
                    wait(dve, adj_in[j], g * 16 + 16)
                    nc.vector.tensor_tensor_reduce(out=junk_v[:, :], in0=adj_b[:, j, :], in1=xn0[:, :], scale=1.0,
                                                   scalar=0.0, op0=ALU.mult, op1=ALU.add,
                                                   accum_out=s_col[:, j:j + 1]).then_inc(adj_summed, 1)
                    if not first(g, j):
                        second(g, j - 1)
                    wait(dve, adj_summed, g * GT + (j + 1))
                    wait(dve, adj_counted, g * GT + (j + 1))
                    link(nc.vector.scalar_tensor_tensor(sg_col[:, j:j + 1], r_col[:, j:j + 1], 0.0,
                                                        s_col[:, j:j + 1], ALU.is_gt, ALU.mult))
                    wait(dve, self_done, g * GT + (j + 1))
                    nc.vector.scalar_tensor_tensor(z_b[:, :], wn_bc[:, :], sg_col[:, j:j + 1], ps_g[j % 2][:, 0:D],
                                                   ALU.mult, ALU.add).then_inc(z_done, 1)
                    wait(dve, z_done, g * GT + (j + 1))
                    if j >= 2:
                        wait(dve, tile_stored[j % 2], g * 64 + 32)
                    else:
                        wait(dve, tile_stored[j % 2], g * 64)
                    nc.vector.scalar_tensor_tensor(x1_b[:, j % 2, :], z_b[:, :], 0.0, x_t,
                                                   ALU.max, ALU.add).then_inc(x1_ready, 1)
                    wait(dve, x1_ready, g * GT + (j + 1))
                    nc.vector.bn_stats(st2[:, :], x1_b[:, j % 2, :]).then_inc(row_stats, 1)
                    dve.wait_ge(row_stats, 1)
                    dve.sem_clear(row_stats)
                    link(nc.vector.bn_aggr(mv2[:, j % 2, :], st2[:, :]))
                    nc.vector.tensor_scalar(ve2[:, j % 2:j % 2 + 1], mv2[:, j % 2, 1:2], EPS, None,
                                            ALU.add).then_inc(var_ready, 1)
                    assert link.n == PER - first(g, j)

            from_zero(dve, body, NG, apart=2)
            link.at(START + NT * PER - 1)
            second(NG - 1, GT - 1)

        @block.tensor
        def _(pe):
            pe.wait_ge(consts, 3)
            pe.wait_ge(w_in, 16 * N_WEIGHTS)
            for kc in range(KC):
                for dc in range(KC):
                    last = nc.tensor.transpose(ps_x[:, kc * D + dc * P:kc * D + (dc + 1) * P],
                                               ws[:, dc, kc * P:(kc + 1) * P], ident[:, :])
            last.then_inc(spread, 1)
            pe.wait_ge(xn0_diag, 1)
            for g, bank in enumerate((ps_t1, ps_t2, ps_g[0], ps_g[1])):
                nc.tensor.matmul(bank[:, :], ones[:, :], diag[:, g * GT:(g + 1) * GT, :], start=True,
                                 stop=True).then_inc(spread, 1)
            pe.wait_ge(wn_diag_s, 1)
            nc.tensor.matmul(ps_v[:, 0:D], ones[:, :], wn_diag[:, :, :], start=True, stop=True).then_inc(spread, 1)
            pe.wait_ge(spread_out, N_SPREAD)
            pe.wait_ge(qkv_in, 16 * 3)
            def body(g):
                for j in range(GT):
                    t1 = g * GT + (j + 1)
                    wait(pe, xn_ready, t1)
                    wait(pe, xnt_ready, g * GT + j)
                    for kc in range(KC):
                        last = nc.tensor.transpose(ps_t1[:, kc * P:(kc + 1) * P], xn_b[:, j % 2, kc * P:(kc + 1) * P],
                                                   ident[:, :])
                    last.then_inc(xn_turned, 1)
                    wait(pe, xnt_ready, t1)
                    wait(pe, z_done, g * GT + (j - 1))
                    for kc in range(KC):
                        last = nc.tensor.matmul(ps_g[j % 2][:, 0:D], xnt_b[:, j % 2, kc, :], ws_t[:, kc, :],
                                                start=kc == 0, stop=kc == KC - 1)
                    last.then_inc(self_done, 1)
                    if not first(g, j):
                        second(g, j - 1)
                    if not first_group(g):
                        queries_keys(g - 1, j)

            def second(g, j):
                t1 = g * GT + (j + 1)
                wait(pe, xn2_ready, t1)
                wait(pe, xn2t_kept, g * GT + j)
                for kc in range(KC):
                    last = nc.tensor.transpose(ps_t2[:, kc * P:(kc + 1) * P], xn2_b[:, j % 2, kc * P:(kc + 1) * P],
                                               ident[:, :])
                last.then_inc(xn2_turned, 1)
                wait(pe, xn2t_ready, t1)
                wait(pe, v_out, g * GT + j)
                for kc in range(KC):
                    last = nc.tensor.matmul(ps_v[:, 0:D], xn2t_b[:, j % 2, kc, :], wv[:, kc, :],
                                            start=kc == 0, stop=kc == KC - 1)
                last.then_inc(v_done, 1)

            def queries_keys(g, c):
                w = wq if c < KC else wk
                wait(pe, xn2t_kept, g * GT + GT)
                wait(pe, qk_hi, g * (2 * KC) + (c - 1))
                for kc in range(KC):
                    last = nc.tensor.matmul(ps_q[c % 2][:, :], w[:, kc, (c % KC) * P:(c % KC + 1) * P],
                                            xn2_t[:, bass.ds(g % 2, 1), kc, :].rearrange("p a q -> p (a q)"), start=kc == 0, stop=kc == KC - 1)
                last.then_inc(qk_done, 1)

            from_zero(pe, body, NG, apart=2)
            second(NG - 1, GT - 1)
            for c in range(2 * KC):
                queries_keys(NG - 1, c)

        @block.scalar
        def _(act):
            act.wait_ge(spread, 1)
            nc.scalar.activation(ws_t[:, :, :].rearrange("p a b -> p (a b)"), ps_x[:, :], ACT.Copy).then_inc(spread_out, 1)
            for g, bank in enumerate((ps_t1, ps_t2, ps_g[0], ps_g[1])):
                act.wait_ge(spread, g + 2)
                nc.scalar.activation(xn0[:, g * GW:(g + 1) * GW], bank[:, :], ACT.Copy).then_inc(spread_out, 1)
            act.wait_ge(spread, NG + 2)
            nc.scalar.activation(wn_bc[:, :], ps_v[:, 0:D], ACT.Copy).then_inc(spread_out, 1)
            act.wait_ge(b_in, 32)
            nc.scalar.activation(bqk_s[:, :, :], bqk[:, :, :], ACT.Copy, scale=QS).then_inc(spread_out, 1)
            act.wait_ge(spread_out, N_SPREAD + 1)
            def body(g):
                for j in range(GT):
                    t1 = g * GT + (j + 1)
                    wait(act, adj_counted, g * GT + j)
                    wait(act, adj_in[j], g * 16 + 16)
                    nc.scalar.activation(junk_a[:, :], adj_b[:, j, :], ACT.Copy,
                                         accum_out=r_col[:, j:j + 1]).then_inc(adj_counted, 1)
                    wait(act, xn_turned, t1)
                    wait(act, self_done, g * GT + (j - 1))
                    nc.scalar.activation(xnt_b[:, j % 2, :, :].rearrange("p a b -> p (a b)"), ps_t1[:, 0:D],
                                         ACT.Copy).then_inc(xnt_ready, 1)
                    if not first_group(g) and j > 0:
                        queries_keys(g - 1, j - 1)
                    elif j == 0 and not (isinstance(g, int) and g < 2):
                        queries_keys(g - 2, GT - 1)
                    if not first(g, j):
                        second(g, j - 1)

            def second(g, j):
                t1 = g * GT + (j + 1)
                wait(act, xn2_turned, t1)
                nc.scalar.activation(xn2t_b[:, j % 2, :, :].rearrange("p a b -> p (a b)"), ps_t2[:, 0:D],
                                     ACT.Copy).then_inc(xn2t_ready, 1)
                if j == 0:
                    wait(act, qk_done, g * (2 * KC) - 2 * KC)
                nc.scalar.activation(xn2_t[:, bass.ds((g + j // GT) % 2, 1), :, j % GT * P:(j % GT + 1) * P].rearrange(
                                         "p a c q -> p (a c) q"),
                                     ps_t2[:, 0:D].rearrange("p (c q) -> p c q", c=KC), ACT.Copy).then_inc(xn2t_kept, 1)
                wait(act, v_done, t1)
                nc.scalar.activation(v_all[:, bass.ds(g * GT + j, 1), :, :].rearrange("p a h d -> p (a h) d"),
                                     ps_v[:, 0:D].rearrange("p (h d) -> p h d", h=H), ACT.Copy).then_inc(v_out, 1)

            def queries_keys(g, c):
                wait(act, qk_done, g * (2 * KC) + (c + 1))
                wait(act, qk_split, g * (2 * KC) + (c - 1))
                wait(act, qk_stored[c % 2], g * (4 * 16) + c // 2 * 32)
                b16 = bqk_s[:, c // KC, c % KC:c % KC + 1]
                nc.scalar.activation(qk32[:, c % 2, :], ps_q[c % 2][:, :], ACT.Identity, bias=b16, scale=QS)
                nc.scalar.activation(qk16[:, c % 2, 0, :], ps_q[c % 2][:, :], ACT.Identity, bias=b16,
                                     scale=QS).then_inc(qk_hi, 1)

            from_zero(act, body, NG, apart=2)
            queries_keys(NG - 2, GT - 1)
            second(NG - 1, GT - 1)
            for c in range(2 * KC):
                queries_keys(NG - 1, c)


def phase_attend(nc, T, dr):
    UNITS, LAST = H * NG, H * NG - 1
    QW = 3 * HD
    QM = QW + 2
    PIECES = NT
    GROUPS = NT // KG

    with ExitStack() as ctx:
        def sb(name, shape, dt=F32):
            return ctx.enter_context(nc.sbuf_tensor(name, shape, dt))

        def sem(name):
            return ctx.enter_context(nc.semaphore(name))

        ident, v_all = T["ident"], T["v_all"]
        q_st = sb("q_st", [P, NG, GW], F16)
        k_st = sb("k_st", [P, 2, N], F16)
        p_ring = sb("p_ring", [P, PR, GW])
        stage = sb("stage", [P, 2, FF])
        max_part = sb("max_part", [P, PIECES])
        max_col = sb("max_col", [P, GT])
        max_row = sb("max_row", [GT, 2, P], F16)
        v_head = sb("v_head", [P, 2, NT, HD])
        ones = sb("ones_b", [P, HD])
        add_up = sb("add_up", [P, HD])
        o_raw, d_raw = sb("o_raw", [P, GW]), sb("d_raw", [P, GW])
        inv, o_unit = sb("inv", [P, P]), T["o_unit"]
        ps_m = [ctx.enter_context(nc.psum_tensor(f"ps_m{n}", [P, 512], F32)) for n in range(2)]
        ps_e = [ctx.enter_context(nc.psum_tensor(f"ps_e{n}", [P, 512], F32)) for n in range(2)]
        ps_o = ctx.enter_context(nc.psum_tensor("ps_o", [P, 512], F32))
        ps_d = ctx.enter_context(nc.psum_tensor("ps_d", [P, 512], F32))
        ps_s = ctx.enter_context(nc.psum_tensor("ps_s", [P, 512], F32))
        ps_r = ctx.enter_context(nc.psum_tensor("ps_r", [P, 512], F32))

        q_in = [sem(f"q_in{c}") for c in range(NG)]
        row_in = [sem(f"row_in{c}") for c in range(NG)]
        k_in, k_const = sem("k_in"), sem("k_const")
        piece_done, piece_max = sem("piece_done"), [sem(f"piece_max{n}") for n in range(2)]
        max_ready, max_turned, row_ready = sem("max_ready"), sem("max_turned"), sem("row_ready")
        scores_done, probs_ready = sem("scores_done"), sem("probs_ready")
        values_done, sums_done = sem("values_done"), sem("sums_done")
        row_hi, ones_ready, v_ready, add_ready = sem("row_hi"), sem("ones_ready"), sem("v_ready"), sem("add_ready")
        o_copied, d_copied, added_up = sem("o_copied"), sem("d_copied"), sem("added_up")
        inv_ready, o_normed, o_stored = sem("inv_ready"), sem("o_normed"), T["o_stored"]
        stage_in = [sem("stage_in0"), sem("stage_in1")]
        w_step, w_split = sem("w_step"), sem("w_split")
        block = ctx.enter_context(nc.Block())

        def ge(eng, s, b, n, per, extra):
            if isinstance(b, int):
                if per * (4 * b + n) + extra > 0:
                    eng.wait_ge(s, per * (4 * b + n) + extra)
            else:
                eng.wait_ge(s, b * (4 * per) + (per * n + extra))

        def head_ge(eng, s, b, n, per, extra=0):
            eng.wait_ge(s, (b + n // NG + 1) * per + extra if isinstance(b, int) else b * per + (per * (n // NG + 1) + extra))

        def over_units(eng, step):
            step(0, 0)
            with eng.Fori(0, H - 1) as b:
                for n in range(1, NG + 1):
                    step(b, n)
            for n in range(1, NG):
                step(H - 1, n)

        def exists(b, n):
            return not isinstance(b, int) or NG * b + n < UNITS

        def first(b, n):
            return isinstance(b, int) and NG * b + n == 0

        w1 = dr["W1"].rearrange("e (c p) f -> c p e f", p=P)
        w2 = dr["W2"].rearrange("e (f p) d -> p e f d", p=P)

        @block.sync
        def _(sp):
            def load_q(b, n):
                c, head = n % NG, b + n // NG
                for part, row in ((0, 0), (1, HD), (0, 2 * HD)):
                    sp.dma_start(q_st[row:row + HD, c, :],
                                 dr["qh"][part, bass.ds(head * HD, HD), c * GW:(c + 1) * GW]).then_inc(q_in[c], 16)

            def load_k(head, parity):
                for part, row in ((0, 0), (0, HD), (1, 2 * HD)):
                    sp.dma_start(k_st[row:row + HD, parity, :],
                                 dr["kh"][part, bass.ds(head * HD, HD), :]).then_inc(k_in, 16)

            def store_row(b, n):
                c = n % NG
                for part in range(2):
                    sp.dma_start(q_st[QW + part:QW + part + 1, c, :], max_row[:, part, :]).then_inc(row_in[c], 16)

            def store_output(b, n):
                c, head = (n - 1) % NG, b + (n - 1) // NG
                ge(sp, o_normed, b, n, 1, 0)
                for g in range(GT):
                    sp.dma_start(dr["ot"][c, g, bass.ds(head * HD, HD), :], o_unit[g * HD:(g + 1) * HD, :]).then_inc(o_stored, 16)

            def step(b, n):
                ge(sp, scores_done, b, n, NT, 0)
                if exists(b, n + 3):
                    load_q(b, n + 3)
                if n == 1 and exists(b, NG):
                    load_k(b + 1, bass.ds((b + 1) % 2, 1))
                if exists(b, n + 1):
                    ge(sp, row_ready, b, n, 1, 2)
                    store_row(b, n + 1)
                if not first(b, n):
                    store_output(b, n)

            load_k(0, bass.ds(0, 1))
            for n in range(3):
                load_q(0, n)
            sp.wait_ge(row_ready, 1)
            store_row(0, 0)
            load_route_weights(sp, T, dr)
            over_units(sp, step)
            store_output(H - 1, NG)

        @block.gpsimd
        def _(pool):
            nc.gpsimd.memset(k_st[QW:QM, :, :], -MS).then_inc(k_const, 1)
            pool.wait_ge(k_const, 1)
            nc.gpsimd.memset(ones[:, :], 1.0).then_inc(ones_ready, 1)
            pool.wait_ge(ones_ready, 1)
            with pool.Fori(0, E) as e:
                one = bass.ds(e, 1)
                for c in range(4):
                    pool.wait_ge(stage_in[c % 2], 16)
                    pool.sem_clear(stage_in[c % 2])
                    raw = stage[:, c % 2, :]
                    if c < KC:
                        hi, lo = (T[w][:, one, c, :].rearrange("p a f -> p (a f)") for w in ("w1h", "w1l"))
                    else:
                        hi, lo = (T[w][:, one, (c - KC) * 4:(c - KC + 1) * 4, :].rearrange("p a f d -> p (a f d)")
                                  for w in ("w2h", "w2l"))
                    nc.gpsimd.tensor_scalar(raw, raw, WS, None, ALU.mult).then_inc(w_step, 1)
                    pool.wait_ge(w_step, 1)
                    nc.gpsimd.tensor_copy(hi, raw).then_inc(w_step, 1)
                    pool.wait_ge(w_step, 2)
                    pool.sem_clear(w_step)
                    nc.gpsimd.tensor_tensor(lo, raw, hi, ALU.subtract).then_inc(w_split, 1)

        @block.tensor
        def _(pe):
            def piece_of_maxima(b, n, j):
                c = n % NG
                if j == 0:
                    head_ge(pe, q_in[c], b, n, 48)
                    head_ge(pe, k_in, b, n, 48)
                ge(pe, piece_max[j % 2], b, n, PIECES // 2, j // 2)
                par = bass.ds((b + n // NG) % 2, 1)
                nc.tensor.matmul(ps_m[j % 2][:, :], q_st[0:QW, c, (j // NG) * P:(j // NG + 1) * P],
                                 k_st[0:QW, par, (j % NG) * GW:(j % NG + 1) * GW].rearrange("p a k -> p (a k)"),
                                 start=True, stop=True).then_inc(piece_done, 1)

            def turn_maxima(b, n):
                ge(pe, max_ready, b, n, 1, 1)
                ge(pe, row_ready, b, n, 1, 0)
                nc.tensor.transpose(ps_r[0:GT, 0:P], max_col[:, :], ident[:, :]).then_inc(max_turned, 1)

            def values(b, n, g):
                ge(pe, probs_ready, b, n, NT, KG * (g + 1))
                if g == 0:
                    ge(pe, o_copied, b, n, 1, 0)
                    if n % NG == 0:
                        head_ge(pe, v_ready, b, n, 2, -1)
                    else:
                        head_ge(pe, v_ready, b, n, 2, 0)
                for i in range(KG):
                    j = KG * g + i
                    m = nc.tensor.matmul(ps_o[i * HD:(i + 1) * HD, :], v_head[:, min(n % NG, 1), j, :], p_ring[:, j % PR, :],
                                         start=g == 0, stop=g == GROUPS - 1, skip_group_check=True)
                m.then_inc(values_done, 1)

            def sums(b, n, g):
                if g == 0:
                    ge(pe, d_copied, b, n, 1, 0)
                for i in range(KG):
                    m = nc.tensor.matmul(ps_d[i * HD:(i + 1) * HD, :], ones[:, :], p_ring[:, (KG * g + i) % PR, :],
                                         start=g == 0, stop=g == GROUPS - 1, skip_group_check=True)
                m.then_inc(sums_done, 1)

            def over_column_tiles(b, n):
                ge(pe, o_copied, b, n, 1, 1)
                ge(pe, d_copied, b, n, 1, 1)
                ge(pe, o_normed, b, n, 1, 0)
                for g in range(GT):
                    nc.tensor.matmul(ps_s[g * HD:(g + 1) * HD, 0:P], add_up[:, :], o_raw[:, g * P:(g + 1) * P],
                                     start=True, stop=True, skip_group_check=True)
                for g in range(GT):
                    m = nc.tensor.matmul(ps_s[g * HD:(g + 1) * HD, P:2 * P], add_up[:, :], d_raw[:, g * P:(g + 1) * P],
                                         start=True, stop=True, skip_group_check=True)
                m.then_inc(added_up, 1)

            def step(b, n):
                c = n % NG
                par = bass.ds((b + n // NG) % 2, 1)
                for j in range(NT):
                    if j == 0:
                        head_ge(pe, row_in[c], b, n, 32)
                    ge(pe, probs_ready, b, n, NT, j - 1)
                    nc.tensor.matmul(ps_e[j % 2][:, :],
                                     k_st[0:QM, par, j * P:(j + 1) * P].rearrange("p a k -> p (a k)"),
                                     q_st[0:QM, c, :], start=True, stop=True).then_inc(scores_done, 1)
                    if exists(b, n + 2):
                        piece_of_maxima(b, n + 2, j)
                    if j % KG in (1, 3) and not (first(b, n) and j < KG):
                        part = values if j % KG == 1 else sums
                        if j < KG:
                            part(b, n - 1, GROUPS - 1)
                        else:
                            part(b, n, j // KG - 1)
                    if j == 5 and exists(b, n + 1):
                        turn_maxima(b, n + 1)
                    if j == 8 and not first(b, n):
                        over_column_tiles(b, n - 1)

            pe.wait_ge(k_const, 1)
            for j in range(NT):
                piece_of_maxima(0, 0, j)
            turn_maxima(0, 0)
            for j in range(NT):
                piece_of_maxima(0, 1, j)
            pe.wait_ge(ones_ready, 1)
            pe.wait_ge(add_ready, 1)
            over_units(pe, step)
            values(H - 1, NG - 1, GROUPS - 1)
            sums(H - 1, NG - 1, GROUPS - 1)
            over_column_tiles(H - 1, NG - 1)

        @block.scalar
        def _(act):
            def load_weights(b, n):
                c, one = n % NG, bass.ds(b + n // NG, 1)
                ge(act, w_split, b, n, 1, -1)
                if c < KC:
                    dst, src = stage[:, c % 2, :], w1[c, :, one, :].rearrange("p a f -> p (a f)")
                else:
                    dst = stage[:, c % 2, :].rearrange("p (f d) -> p f d", d=D)
                    src = w2[:, one, (c - KC) * 4:(c - KC + 1) * 4, :].rearrange("p a f d -> p (a f) d")
                act.dma_start(dst, src).then_inc(stage_in[c % 2], 16)

            def copy_values(b, n):
                ge(act, values_done, b, n, GROUPS, GROUPS)
                ge(act, added_up, b, n, 1, 0)
                nc.scalar.activation(o_raw[:, :], ps_o[:, :], ACT.Copy).then_inc(o_copied, 1)

            def step(b, n):
                for j in range(NT):
                    ge(act, scores_done, b, n, NT, j + 1)
                    if j % KG == 0:
                        ge(act, sums_done, b, n, GROUPS, j // KG - 1)
                    nc.scalar.activation(p_ring[:, j % PR, :], ps_e[j % 2][:, :], ACT.Exp,
                                         scale=SCALE / MS).then_inc(probs_ready, 1)
                    if j == 1 and not first(b, n):
                        copy_values(b, n - 1)
                    if j == 8 and exists(b, n + 1):
                        load_weights(b, n + 1)

            load_weights(0, 0)
            over_units(act, step)
            copy_values(H - 1, NG - 1)

        @block.vector
        def _(dve):
            def reduce_piece(b, n, i):
                if i == 0:
                    ge(dve, max_ready, b, n, 1, 0)
                ge(dve, piece_done, b, n, PIECES, i + 1)
                nc.vector.tensor_reduce(max_part[:, i:i + 1], ps_m[i % 2][:, :], AX.X, ALU.max).then_inc(piece_max[i % 2], 1)

            def join_maxima(b, n):
                for s in piece_max:
                    ge(dve, s, b, n, PIECES // 2, PIECES // 2)
                ge(dve, max_turned, b, n, 1, 0)
                nc.vector.tensor_reduce(max_col[:, :], max_part[:, :].rearrange("p (q a) -> p q a", q=GT), AX.X,
                                        ALU.max).then_inc(max_ready, 1)

            def make_row(b, n):
                ge(dve, max_turned, b, n, 1, 1)
                if not (isinstance(b, int) and NG * b + n == 0):
                    head_ge(dve, row_in[(n - 1) % NG], b, n - 1, 32)
                nc.vector.tensor_scalar(max_row[:, 0, :], ps_r[0:GT, 0:P], 1.0 / MS, None, ALU.mult).then_inc(row_hi, 1)
                ge(dve, row_hi, b, n, 1, 1)
                nc.vector.scalar_tensor_tensor(max_row[:, 1, :], ps_r[0:GT, 0:P], 1.0 / MS, max_row[:, 0, :],
                                               ALU.mult, ALU.subtract).then_inc(row_ready, 1)

            def copy_sums(b, n):
                ge(dve, sums_done, b, n, GROUPS, GROUPS)
                ge(dve, added_up, b, n, 1, 0)
                nc.vector.tensor_copy(d_raw[:, :], ps_d[:, :]).then_inc(d_copied, 1)

            def normalise(b, n):
                ge(dve, added_up, b, n, 1, 1)
                nc.vector.reciprocal(inv[:, :], ps_s[:, P:2 * P]).then_inc(inv_ready, 1)
                ge(dve, inv_ready, b, n, 1, 1)
                ge(dve, o_stored, b, n, 16 * GT, 0)
                nc.vector.tensor_tensor(o_unit[:, :], ps_s[:, 0:P], inv[:, :], ALU.mult).then_inc(o_normed, 1)

            def copy_head(head, which):
                nc.vector.tensor_scalar(v_head[:, which, :, :],
                                        v_all[:, :, bass.ds(head, 1), :].rearrange("p t a d -> p t (a d)"),
                                        1.0, None, ALU.mult).then_inc(v_ready, 1)

            def step(b, n):
                for i in range(PIECES):
                    if exists(b, n + 2):
                        reduce_piece(b, n + 2, i)
                    if i == 5 and exists(b, n + 1):
                        make_row(b, n + 1)
                    if i == 3 and not first(b, n):
                        copy_sums(b, n - 1)
                    if i == 10 and not first(b, n):
                        normalise(b, n - 1)
                    if i == 12 and n == 2 and exists(b, NG):
                        ge(dve, values_done, b, 1, GROUPS, 0)
                        copy_head(b + 1, 0)
                    if i == 12 and n == NG:
                        ge(dve, values_done, b, NG, GROUPS, 0)
                        copy_head(b + 1, 1)
                if exists(b, n + 2):
                    join_maxima(b, n + 2)

            nc.vector.tensor_reduce(add_up[:, :], ident[:, :].rearrange("p (g d) -> p d g", d=HD), AX.X,
                                    ALU.add).then_inc(add_ready, 1)
            copy_head(0, 0)
            copy_head(0, 1)
            for n in range(2):
                for i in range(PIECES):
                    reduce_piece(0, n, i)
                join_maxima(0, n)
                if n == 0:
                    make_row(0, 0)
            over_units(dve, step)
            copy_sums(H - 1, NG - 1)
            normalise(H - 1, NG - 1)


ROUTE_WEIGHTS = ("bv_col", "wo", "gate_w", "rows", "gate_b", "b1_rows", "w_in")
N_ROUTE = 8


def load_route_weights(sp, T, dr):
    w_in = T["w_in"]
    sp.dma_start(T["bv_col"][:, :], dr["bv"].rearrange("(c p) -> p c", p=P),
                 allow_slow_non_contiguous=True).then_inc(w_in, 16)
    sp.dma_start(T["wo"][:, :, :], dr["Wo"].rearrange("(c p) d -> p c d", p=P)).then_inc(w_in, 16)
    sp.dma_start(T["gate_w"][:, :, :], dr["gate_W"].rearrange("(c p) e -> p c e", p=P)).then_inc(w_in, 16)
    for n, row in T["rows"].items():
        sp.dma_start(row[:, :], dr[n].partition_broadcast(P)).then_inc(w_in, 16)
    sp.dma_start(T["gate_b"][:, :], dr["gate_b"].partition_broadcast(P)).then_inc(w_in, 16)
    sp.dma_start(T["b1_rows"][:, :], dr["b1"].rearrange("e (f p) -> (e f) p", p=P)).then_inc(w_in, 16)


def phase_route(nc, T, dr):
    with ExitStack() as ctx:
        def sb(name, shape, dt=F32):
            return ctx.enter_context(nc.sbuf_tensor(name, shape, dt))

        def ps(name):
            return ctx.enter_context(nc.psum_tensor(name, [P, 512], F32))

        def sem(name):
            return ctx.enter_context(nc.semaphore(name))

        ident = T["ident"]
        h_all = T["v_all"][:, :, :, :].rearrange("p t h d -> p t (h d)")
        ot_all = sb("ot_all", [P, KC, N])
        b2_bc = T["b2_bc"]
        b2_in, ot_in = sem("b2_in"), [sem(f"ot_in{g}") for g in range(NG)]
        bv_col, wo, gate_w, rows, gate_b, b1_rows, w_in = (T[n] for n in ROUTE_WEIGHTS)
        xr_all = sb("xr_all", [P, NT, D])
        ht_b = sb("ht_b", [P, 2, GT, KC, P])
        EW = P // GT
        gate_pad = sb("gate_pad", [P, KC, EW])
        lt_b = sb("lt_b", [P, P])
        stats = sb("stats_c", [P, NT, 6])
        mean, var, half = sb("mean_c", [P, NT]), sb("var_c", [P, NT]), sb("half_c", [P, NT])
        rstd, nmr = sb("rstd_c", [P, NT]), sb("nmr_c", [P, NT])
        logits = sb("logits", [P, NT, E])
        lmax, den = sb("lmax", [P, NT]), sb("den", [P, NT])
        eq, onehot, ex = sb("eq", [P, NT, E]), sb("onehot", [P, NT, E]), sb("ex", [P, NT, E])
        first = sb("first", [P, NT])
        PAD = NT // 2
        cum = [sb(f"cum{n}", [P, PAD + NT, E]) for n in range(2)]
        many = sb("many", [P, E, NT])
        EPAD = E // 2
        tiles = [sb(f"tiles{n}", [P, EPAD + E]) for n in range(2)]
        base = sb("base", [P, E])
        place, pos_f = sb("place", [P, NT, E]), sb("pos_f", [P, NT])
        below = sb("below", [P, SLOTS, E])
        slot_f = sb("slot_f", [P, SLOTS])
        tri, ones = sb("tri", [P, P]), sb("ones_c", [P, P])
        iota_i = sb("iota_i", [P, E + NT + SLOTS], I32)
        iota_f = sb("iota_f", [P, E + NT + SLOTS])
        ps_b, ps_b1, ps_lt, ps_gate = ps("ps_b"), ps("ps_b1"), ps("ps_lt"), ps("ps_gate")
        ps_ht = [ps("ps_ht0"), ps("ps_ht1")]
        ps_wo = [ps("ps_wo0"), ps("ps_wo1")]

        xr_in, xr_ready = [sem(f"xr_in{g}") for g in range(NG)], sem("xr_ready")
        consts, chain = sem("consts_c"), sem("dve_chain_c")
        ot_ready, wo_done, y_ready = sem("ot_ready"), sem("wo_done"), sem("y_ready")
        row_stats, var_ready, rstd_ready = sem("row_stats_c"), sem("var_ready_c"), sem("rstd_ready_c")
        nmr_ready, normed, h_ready = sem("nmr_ready"), sem("normed"), sem("h_ready")
        h_turned, ht_ready = sem("h_turned"), sem("ht_ready")
        gated, lt_ready, gate_done = sem("gated"), sem("lt_ready"), sem("gate_done")
        b1_turned, b1_out = sem("b1_turned"), sem("b1_out")
        onehot_ready, counted, less_max, exps_ready = sem("onehot_ready"), sem("counted"), sem("less_max"), sem("exps_ready")
        pos_ready, scattered = sem("pos_ready"), [sem(f"scattered{n}") for n in range(4)]
        block = ctx.enter_context(nc.Block())

        @block.sync
        def _(sp):
            for g in range(NG):
                if g == NG - 1:
                    sp.wait_ge(T["o_stored"], 16 * GT * H * NG)
                for kc in range(KC):
                    sp.dma_start(ot_all[:, kc, g * GW:(g + 1) * GW].rearrange("p (t q) -> p t q", q=P),
                                 dr["ot"][g, :, kc * P:(kc + 1) * P, :].rearrange("t p q -> p t q")).then_inc(ot_in[g], 16)
                sp.dma_start(xr_all[:, g * GT:(g + 1) * GT, :],
                             dr["xn2"][g * GW:(g + 1) * GW, :].rearrange("(t p) d -> p t d", p=P)).then_inc(xr_in[g], 16)
            sp.dma_start(b2_bc[:, :, :], dr["b2"].partition_broadcast(P)).then_inc(b2_in, 16)
            sp.wait_ge(b2_in, 16)

        @block.gpsimd
        def _(pool):
            nc.gpsimd.memset(ones[:, :], 1.0).then_inc(consts, 1)
            nc.gpsimd.memset(tri[:, :], 1.0).then_inc(consts, 1)

            def rstd_of(g):
                tiles_g = slice(g * GT, (g + 1) * GT)
                pool.wait_ge(var_ready, g + 1)
                nc.gpsimd.tensor_tensor(rstd[:, tiles_g], var[:, tiles_g], T["minus_half"][:, 0:GT],
                                        ALU.pow).then_inc(rstd_ready, 1)
                pool.wait_ge(rstd_ready, g + 1)

            for t in (*cum, *tiles, gate_pad):
                nc.gpsimd.memset(t[:, ...] if len(t.shape) == 2 else t[:, :, :], 0.0).then_inc(consts, 1)
            nc.gpsimd.iota(iota_i[:, 0:E], [[1, E]], base=-E, channel_multiplier=0).then_inc(consts, 1)
            nc.gpsimd.iota(iota_i[:, E:E + NT], [[P, NT]], base=0, channel_multiplier=0).then_inc(consts, 1)
            nc.gpsimd.iota(iota_i[:, E + NT:], [[1, SLOTS]], base=0, channel_multiplier=0).then_inc(consts, 1)
            pool.wait_ge(consts, 10)
            nc.gpsimd.affine_select(out=tri[:, :], in_=tri[:, :], compare_op=ALU.is_gt, fill=0.0,
                                    base=0, pattern=[[1, P]], channel_multiplier=-1).then_inc(consts, 1)
            nc.gpsimd.tensor_copy(iota_f[:, :], iota_i[:, :]).then_inc(consts, 1)
            pool.wait_ge(w_in, 16 * N_ROUTE)
            nc.gpsimd.tensor_copy(gate_pad[:, :, 0:E], gate_w[:, :, :]).then_inc(consts, 1)
            pool.wait_ge(consts, 13)
            for g in range(NG):
                tiles_g = slice(g * GT, (g + 1) * GT)
                pool.wait_ge(xr_in[g], 16)
                nc.gpsimd.tensor_tensor(xr_all[:, tiles_g, :], xr_all[:, tiles_g, :],
                                        rows["bo"][:, :].unsqueeze(1).to_broadcast([P, GT, D]), ALU.add).then_inc(xr_ready, 1)
                pool.wait_ge(xr_ready, g + 1)
                if g:
                    rstd_of(g - 1)
            rstd_of(NG - 1)
            pool.wait_ge(pos_ready, 1)
            for t in range(NT):
                pool.indirect_dma_start(dr["hs"], bass.IndirectOffsetOnAxis(ap=T["pos"][:, t:t + 1], axis=0),
                                        h_all[:, t, :], None).then_inc(scattered[t % 4], 16)
            for n in range(4):
                pool.wait_ge(scattered[n], 16 * NT // 4)

        @block.vector
        def _(dve):
            link = Link(dve, chain)
            dve.wait_ge(w_in, 16 * N_ROUTE)

            def statistics(t):
                dve.wait_ge(y_ready, t + 1)
                nc.vector.bn_stats(stats[:, t, :], h_all[:, t, :]).then_inc(row_stats, 1)

            def sum_rows(g):
                for t in range(g * GT, (g + 1) * GT):
                    dve.wait_ge(xr_ready, g + 1)
                    dve.wait_ge(wo_done, t + 1)
                    nc.vector.tensor_tensor(h_all[:, t, :], ps_wo[t % 2][:, 0:D], xr_all[:, t, :], ALU.add).then_inc(y_ready, 1)
                    if t > g * GT:
                        statistics(t - 1)
                statistics((g + 1) * GT - 1)

            def variance(g):
                q = slice(g * GT, (g + 1) * GT)
                dve.wait_ge(row_stats, (g + 1) * GT)
                link(nc.vector.tensor_tensor(mean[:, q], stats[:, q, 1], stats[:, q, 4], ALU.add))
                link(nc.vector.tensor_scalar(mean[:, q], mean[:, q], 0.5, None, ALU.mult))
                link(nc.vector.tensor_tensor(half[:, q], stats[:, q, 1], mean[:, q], ALU.subtract))
                link(nc.vector.tensor_tensor(half[:, q], half[:, q], half[:, q], ALU.mult))
                link(nc.vector.tensor_tensor(var[:, q], stats[:, q, 2], stats[:, q, 5], ALU.add))
                link(nc.vector.scalar_tensor_tensor(var[:, q], var[:, q], 1.0 / D, half[:, q], ALU.mult, ALU.add))
                nc.vector.tensor_scalar(var[:, q], var[:, q], EPS, None, ALU.add).then_inc(var_ready, 1)

            def minus_mean(g):
                q = slice(g * GT, (g + 1) * GT)
                dve.wait_ge(rstd_ready, g + 1)
                nc.vector.scalar_tensor_tensor(nmr[:, q], mean[:, q], -1.0, rstd[:, q], ALU.mult,
                                               ALU.mult).then_inc(nmr_ready, 1)

            def scale_shift(g):
                q = slice(g * GT, (g + 1) * GT)
                dve.wait_ge(normed, (g + 1) * GT)
                link(nc.vector.tensor_tensor(h_all[:, q, :], h_all[:, q, :],
                                             rows["ln_g"][:, :].unsqueeze(1).to_broadcast([P, GT, D]), ALU.mult))
                nc.vector.tensor_tensor(h_all[:, q, :], h_all[:, q, :],
                                        rows["ln_b"][:, :].unsqueeze(1).to_broadcast([P, GT, D]), ALU.add).then_inc(h_ready, 1)

            for g in range(NG + 2):
                if g < NG:
                    sum_rows(g)
                if 1 <= g <= NG:
                    minus_mean(g - 1)
                if g < NG:
                    variance(g)
                if 2 <= g:
                    scale_shift(g - 2)
            dve.wait_ge(gate_done, NG)
            link(nc.vector.tensor_tensor(logits[:, :, :], ps_gate[:, :].rearrange("p (t e) -> p t e", e=EW)[:, :, 0:E],
                                         gate_b[:, :].unsqueeze(1).to_broadcast([P, NT, E]), ALU.add))
            dve.wait_ge(consts, 13)
            TE = [P, NT, E]
            ids = iota_f[:, 0:E].unsqueeze(1).to_broadcast(TE)
            link(nc.vector.tensor_reduce(lmax[:, :], logits[:, :, :], AX.X, ALU.max))
            hi = lmax[:, :].unsqueeze(2).to_broadcast(TE)
            nc.vector.tensor_tensor(ex[:, :, :], logits[:, :, :], hi, ALU.subtract).then_inc(less_max, 1)
            link(nc.vector.tensor_tensor(eq[:, :, :], logits[:, :, :], hi, ALU.is_equal))
            link(nc.vector.tensor_tensor(eq[:, :, :], eq[:, :, :], ids, ALU.mult))
            link(nc.vector.tensor_reduce(first[:, :], eq[:, :, :], AX.X, ALU.min))
            nc.vector.tensor_tensor(onehot[:, :, :], ids, first[:, :].unsqueeze(2).to_broadcast(TE),
                                    ALU.is_equal).then_inc(onehot_ready, 1)
            dve.wait_ge(exps_ready, 1)
            link(nc.vector.tensor_reduce(den[:, :], ex[:, :, :], AX.X, ALU.add))
            link(nc.vector.reciprocal(T["gw"][:, :], den[:, :]))
            dve.wait_ge(counted, 1)
            link(nc.vector.tensor_copy(cum[0][:, PAD:, :], ps_b1[:, P:2 * P].rearrange("p (t e) -> p t e", e=E)))
            at = 0
            for step in (1, 2, 4, 8):
                link(nc.vector.tensor_tensor(cum[1 - at][:, PAD:, :], cum[at][:, PAD:, :],
                                             cum[at][:, PAD - step:PAD + NT - step, :], ALU.add))
                at = 1 - at
            cum_t = cum[at]
            link(nc.vector.tensor_tensor(many[:, :, :], cum_t[:, PAD + NT - 1, :].unsqueeze(2).to_broadcast([P, E, NT]),
                                         iota_f[:, E:E + NT].unsqueeze(1).to_broadcast([P, E, NT]), ALU.is_gt))
            link(nc.vector.tensor_reduce(tiles[0][:, EPAD:], many[:, :, :], AX.X, ALU.add))
            link(nc.vector.tensor_scalar(base[:, :], tiles[0][:, EPAD:], -1.0, None, ALU.mult))
            at = 0
            for step in (1, 2, 4):
                link(nc.vector.tensor_tensor(tiles[1 - at][:, EPAD:], tiles[at][:, EPAD:],
                                             tiles[at][:, EPAD - step:EPAD + E - step], ALU.add))
                at = 1 - at
            ends = tiles[at][:, EPAD:]
            link(nc.vector.tensor_tensor(base[:, :], base[:, :], ends, ALU.add))
            link(nc.vector.tensor_scalar(base[:, :], base[:, :], float(P), None, ALU.mult))
            link(nc.vector.tensor_tensor(place[:, :, :], ps_b1[:, 0:P].rearrange("p (t e) -> p t e", e=E),
                                         cum_t[:, PAD - 1:PAD + NT - 1, :], ALU.add))
            link(nc.vector.tensor_tensor(place[:, :, :], place[:, :, :], base[:, :].unsqueeze(1).to_broadcast(TE), ALU.add))
            link(nc.vector.tensor_tensor(place[:, :, :], place[:, :, :], onehot[:, :, :], ALU.mult))
            link(nc.vector.tensor_reduce(pos_f[:, :], place[:, :, :], AX.X, ALU.add))
            nc.vector.tensor_copy(T["pos"][:, :], pos_f[:, :]).then_inc(pos_ready, 1)
            link(nc.vector.tensor_tensor(below[:, :, :], ends.unsqueeze(1).to_broadcast([P, SLOTS, E]),
                                         iota_f[:, E + NT:].unsqueeze(2).to_broadcast([P, SLOTS, E]), ALU.is_le))
            link(nc.vector.tensor_reduce(slot_f[:, :], below[:, :, :], AX.X, ALU.add))
            link(nc.vector.tensor_scalar(slot_f[:, :], slot_f[:, :], float(E - 1), None, ALU.min))
            link(nc.vector.tensor_copy(T["slot_e"][:, :], slot_f[:, :]))

        @block.tensor
        def _(pe):
            pe.wait_ge(w_in, 16 * N_ROUTE)

            def project(g):
                pe.wait_ge(ot_ready, KC * (g + 1))
                for t in range(g * GT, (g + 1) * GT):
                    if t >= 2:
                        pe.wait_ge(y_ready, t - 1)
                    for kc in range(KC):
                        last = nc.tensor.matmul(ps_wo[t % 2][:, 0:D], ot_all[:, kc, t * P:(t + 1) * P], wo[:, kc, :],
                                                start=kc == 0, stop=kc == KC - 1)
                    last.then_inc(wo_done, 1)

            def turn(t):
                if t >= 2:
                    pe.wait_ge(ht_ready, t - 1)
                for kc in range(KC):
                    last = nc.tensor.transpose(ps_ht[t % 2][:, kc * P:(kc + 1) * P], h_all[:, t, kc * P:(kc + 1) * P],
                                               ident[:, :])
                last.then_inc(h_turned, 1)

            def gate(g):
                pe.wait_ge(consts, 13)
                pe.wait_ge(ht_ready, GT * (g + 1))
                if g:
                    pe.wait_ge(lt_ready, g)
                for kc in range(KC):
                    for j in range(GT):
                        last = nc.tensor.matmul(ps_lt[j * EW:(j + 1) * EW, 0:P], gate_pad[:, kc, :], ht_b[:, g % 2, j, kc, :],
                                                start=kc == 0, stop=kc == KC - 1, skip_group_check=True)
                last.then_inc(gated, 1)

            def turn_logits(g):
                pe.wait_ge(lt_ready, g + 1)
                nc.tensor.transpose(ps_gate[:, g * P:(g + 1) * P], lt_b[:, :], ident[:, :]).then_inc(gate_done, 1)

            def turn_and_gate(g):
                pe.wait_ge(h_ready, g + 1)
                for t in range(g * GT, (g + 1) * GT):
                    turn(t)
                if g:
                    turn_logits(g - 1)
                gate(g)

            for g in range(NG):
                project(g)
            for g in range(NG):
                turn_and_gate(g)
            turn_logits(NG - 1)
            nc.tensor.transpose(ps_b[:, 0:E * FC], b1_rows[:, :], ident[0:E * FC, 0:E * FC]).then_inc(b1_turned, 1)
            pe.wait_ge(onehot_ready, 1)
            nc.tensor.matmul(ps_b1[:, 0:P], tri[:, :], onehot[:, :, :], start=True, stop=True)
            nc.tensor.matmul(ps_b1[:, P:2 * P], ones[:, :], onehot[:, :, :], start=True, stop=True).then_inc(counted, 1)

        @block.scalar
        def _(act):
            act.wait_ge(w_in, 16 * N_ROUTE)
            for g in range(NG):
                act.wait_ge(ot_in[g], 16 * KC)
                for kc in range(KC):
                    nc.scalar.activation(ot_all[:, kc, g * GW:(g + 1) * GW], ot_all[:, kc, g * GW:(g + 1) * GW],
                                         ACT.Identity, bias=bv_col[:, kc:kc + 1]).then_inc(ot_ready, 1)

            def normalise(g):
                act.wait_ge(nmr_ready, g + 1)
                for t in range(g * GT, (g + 1) * GT):
                    nc.scalar.activation(h_all[:, t, :], h_all[:, t, :], ACT.Identity, bias=nmr[:, t:t + 1],
                                         scale=rstd[:, t:t + 1]).then_inc(normed, 1)

            normalise(0)
            for g in range(NG):
                if g < NG - 1:
                    normalise(g + 1)
                for t in range(g * GT, (g + 1) * GT):
                    act.wait_ge(h_turned, t + 1)
                    if g >= 2:
                        act.wait_ge(gated, g - 1)
                    nc.scalar.activation(ht_b[:, g % 2, t % GT, :, :].rearrange("p a b -> p (a b)"), ps_ht[t % 2][:, 0:D],
                                         ACT.Copy).then_inc(ht_ready, 1)
                act.wait_ge(gated, g + 1)
                if g:
                    act.wait_ge(gate_done, g)
                nc.scalar.activation(lt_b[:, :], ps_lt[:, 0:P], ACT.Copy).then_inc(lt_ready, 1)
            act.wait_ge(b1_turned, 1)
            nc.scalar.activation(T["b1_t"][:, :, :].rearrange("p a b -> p (a b)"), ps_b[:, 0:E * FC], ACT.Copy).then_inc(b1_out, 1)
            act.wait_ge(less_max, 1)
            nc.scalar.activation(ex[:, :, :], ex[:, :, :], ACT.Exp).then_inc(exps_ready, 1)


def phase_experts(nc, T, dr):
    HALF = FC // 2
    with ExitStack() as ctx:
        def sb(name, shape, dt=F32):
            return ctx.enter_context(nc.sbuf_tensor(name, shape, dt))

        def ps(name):
            return ctx.enter_context(nc.psum_tensor(name, [P, 512], F32))

        def sem(name):
            return ctx.enter_context(nc.semaphore(name))

        ident, slot_e = T["ident"], T["slot_e"]
        tok = sb("tok", [P, 2, D])
        t32 = sb("t32", [P, KC * P])
        th, tl = sb("th", [P, KC * P], F16), sb("tl", [P, KC * P], F16)
        b1_b = sb("b1_b", [P, FC])
        hid = sb("hid", [P, FC, P])
        hid16 = [sb("hid_h", [P, 2, FC * P], F16), sb("hid_l", [P, 2, FC * P], F16)]
        y_b = sb("y_b_d", [P, D])
        ps_t, ps_y = ps("ps_t"), ps("ps_y")
        ps_h = [ps("ps_h0"), ps("ps_h1")]
        tok_in, y_stored = [sem("tok_in0"), sem("tok_in1")], sem("y_stored")
        turned, t32_ready, th_ready, t_split = sem("turned"), sem("t32_ready"), sem("th_ready"), sem("t_split")
        up_done, b1_ready, gelu_done = sem("up_done"), sem("b1_ready"), sem("gelu_done")
        hid_hi, hid_split, down_done, y_ready = sem("hid_hi"), sem("hid_split"), sem("down_done"), sem("y_ready")
        hid_scaled = sem("hid_scaled")
        block = ctx.enter_context(nc.Block())

        def expert(eng, s):
            slot = slot_e[0:1, s:s + 1] if isinstance(s, int) else slot_e[0:1, bass.ds(s, 1)]
            return eng.value_load(slot, min_val=0, max_val=E - 1)

        def over_slots(eng, step):
            EARLY, BODY = 3, 4
            TURNS = (SLOTS - EARLY - 1) // BODY
            e = None
            for s in range(EARLY):
                e = step(s, s % 2, e)
            with eng.Fori(0, TURNS) as b:
                e = None
                for n in range(EARLY, EARLY + BODY):
                    e = step(b * BODY + n, n % 2, e)
            e = None
            for s in range(EARLY + TURNS * BODY, SLOTS):
                e = step(s, s % 2, e)
            return e

        def first(s):
            return isinstance(s, int) and s == 0

        def final(s):
            return isinstance(s, int) and s == SLOTS - 1

        @block.sync
        def _(sp):
            def load(s, par):
                if not (isinstance(s, int) and s < 2):
                    sp.wait_ge(turned, s - 1)
                sp.dma_start(tok[:, par, :], dr["hs"][bass.ds(s * P, P), :]).then_inc(tok_in[par], 16)

            def store(s):
                sp.wait_ge(y_ready, s + 1)
                sp.dma_start(dr["ys"][bass.ds(s * P, P), :], y_b[:, :]).then_inc(y_stored, 16)

            def step(s, par, _):
                if not (isinstance(s, int) and s + 2 >= SLOTS):
                    load(s + 2, par)
                if not first(s):
                    store(s - 1)

            load(0, 0)
            load(1, 1)
            over_slots(sp, step)
            store(SLOTS - 1)
            sp.wait_ge(y_stored, 16 * SLOTS)

        @block.tensor
        def _(pe):
            def turn_tokens(s, par):
                pe.wait_ge(tok_in[par], s * 8 + (16 - 8 * par))
                if not first(s):
                    pe.wait_ge(t32_ready, s)
                for kc in range(KC):
                    last = nc.tensor.transpose(ps_t[:, kc * P:(kc + 1) * P], tok[:, par, kc * P:(kc + 1) * P], ident[:, :])
                last.then_inc(turned, 1)

            def up(s, e, half):
                if not first(s):
                    pe.wait_ge(gelu_done, s * 2 + (half - 1))
                products = [(w, x, kc) for w, x in (("w1h", th), ("w1h", tl), ("w1l", th)) for kc in range(KC)]
                for f in range(half * HALF, (half + 1) * HALF):
                    for n, (w, x, kc) in enumerate(products):
                        last = nc.tensor.matmul(ps_h[half][:, (f % HALF) * P:(f % HALF + 1) * P],
                                                T[w][:, bass.ds(e, 1), kc, f * P:(f + 1) * P].rearrange("p a f -> p (a f)"),
                                                x[:, kc * P:(kc + 1) * P], start=n == 0, stop=n == len(products) - 1)
                last.then_inc(up_done, 1)

            def down(s, par, e):
                pe.wait_ge(hid_split, s * 2 + 2)
                if not first(s):
                    pe.wait_ge(y_ready, s)
                n = 0
                for f in range(FC):
                    for x, w in ((0, "w2h"), (0, "w2l"), (1, "w2h")):
                        last = nc.tensor.matmul(ps_y[:, 0:D], hid16[x][:, par, f * P:(f + 1) * P],
                                                T[w][:, bass.ds(e, 1), f, :].rearrange("p a d -> p (a d)"),
                                                start=n == 0, stop=n == 3 * FC - 1)
                        n += 1
                last.then_inc(down_done, 1)

            def step(s, par, last_e):
                if last_e is None and not first(s):
                    last_e = expert(pe, s - 1)
                e = expert(pe, s)
                pe.wait_ge(t_split, s + 1)
                up(s, e, 0)
                if not final(s):
                    turn_tokens(s + 1, 1 - par)
                up(s, e, 1)
                if not first(s):
                    down(s - 1, 1 - par, last_e)
                return e

            turn_tokens(0, 0)
            e = over_slots(pe, step)
            down(SLOTS - 1, (SLOTS - 1) % 2, e)

        @block.scalar
        def _(act):
            def tokens(s):
                act.wait_ge(turned, s + 1)
                if not first(s):
                    act.wait_ge(t_split, s)
                nc.scalar.activation(t32[:, :], ps_t[:, 0:D], ACT.Copy, scale=TS).then_inc(t32_ready, 1)

            def step(s, par, _):
                act.wait_ge(b1_ready, s + 1)
                for half in range(2):
                    act.wait_ge(up_done, s * 2 + (half + 1))
                    if not first(s):
                        act.wait_ge(hid_split, s * 2 + (half - 1))
                    for f in range(half * HALF, (half + 1) * HALF):
                        last = nc.scalar.activation(hid[:, f, :], ps_h[half][:, (f % HALF) * P:(f % HALF + 1) * P],
                                                    ACT.Gelu_apprx_tanh, bias=b1_b[:, f:f + 1], scale=1.0 / (TS * WS))
                    last.then_inc(gelu_done, 1)
                    if half == 0 and not final(s):
                        tokens(s + 1)

            tokens(0)
            over_slots(act, step)

        @block.vector
        def _(dve):
            def split_tokens(s):
                dve.wait_ge(t32_ready, s + 1)
                if not first(s):
                    dve.wait_ge(up_done, s * 2)
                nc.vector.tensor_copy(th[:, :], t32[:, :]).then_inc(th_ready, 1)
                dve.wait_ge(th_ready, s + 1)
                nc.vector.tensor_tensor(tl[:, :], t32[:, :], th[:, :], ALU.subtract).then_inc(t_split, 1)

            def bias(s, e):
                if not first(s):
                    dve.wait_ge(gelu_done, s * 2)
                nc.vector.tensor_copy(b1_b[:, :], T["b1_t"][:, bass.ds(e, 1), :].rearrange("p a f -> p (a f)")).then_inc(b1_ready, 1)

            def split_hidden(s, par, half):
                dve.wait_ge(gelu_done, s * 2 + (half + 1))
                if not (isinstance(s, int) and s < 2):
                    if half == 0:
                        dve.wait_ge(down_done, s - 1)
                raw = hid[:, half * HALF:(half + 1) * HALF, :].rearrange("p f q -> p (f q)")
                hi, lo = (x[:, par, half * HALF * P:(half + 1) * HALF * P] for x in hid16)
                nc.vector.tensor_scalar(raw, raw, TS, None, ALU.mult).then_inc(hid_scaled, 1)
                dve.wait_ge(hid_scaled, s * 2 + (half + 1))
                nc.vector.tensor_copy(hi, raw).then_inc(hid_hi, 1)
                dve.wait_ge(hid_hi, s * 2 + (half + 1))
                nc.vector.tensor_tensor(lo, raw, hi, ALU.subtract).then_inc(hid_split, 1)

            def output(s, e):
                dve.wait_ge(down_done, s + 1)
                if not first(s):
                    dve.wait_ge(y_stored, s * 16)
                nc.vector.scalar_tensor_tensor(y_b[:, :], ps_y[:, 0:D], 1.0 / (TS * WS),
                                               T["b2_bc"][:, bass.ds(e, 1), :].rearrange("p a d -> p (a d)"),
                                               ALU.mult, ALU.add).then_inc(y_ready, 1)

            def step(s, par, last_e):
                if last_e is None and not first(s):
                    last_e = expert(dve, s - 1)
                e = expert(dve, s)
                bias(s, e)
                split_hidden(s, par, 0)
                if not final(s):
                    split_tokens(s + 1)
                split_hidden(s, par, 1)
                if not first(s):
                    output(s - 1, last_e)
                return e

            split_tokens(0)
            e = over_slots(dve, step)
            output(SLOTS - 1, e)


def phase_return(nc, T, dr):
    with ExitStack() as ctx:
        def sb(name, shape, dt=F32):
            return ctx.enter_context(nc.sbuf_tensor(name, shape, dt))

        def sem(name):
            return ctx.enter_context(nc.semaphore(name))

        y_all, x1_all = sb("y_all", [P, NT, D]), sb("x1_all", [P, NT, D])
        x1_in, y_in, summed, stored = sem("x1_in"), [sem(f"y_in{g}") for g in range(NG)], sem("summed"), sem("stored")
        block = ctx.enter_context(nc.Block())

        @block.gpsimd
        def _(pool):
            for t in range(NT):
                pool.indirect_dma_start(y_all[:, t, :], None, dr["ys"],
                                        bass.IndirectOffsetOnAxis(ap=T["pos"][:, t:t + 1], axis=0)).then_inc(y_in[t // GT], 16)

        @block.vector
        def _(dve):
            dve.wait_ge(x1_in, 16)
            for t in range(NT):
                if t % GT == 0:
                    dve.wait_ge(y_in[t // GT], 16 * GT)
                last = nc.vector.scalar_tensor_tensor(y_all[:, t, :], y_all[:, t, :], T["gw"][:, t:t + 1], x1_all[:, t, :],
                                                      ALU.mult, ALU.add).then_inc(summed, 1)

        @block.sync
        def _(sp):
            sp.dma_start(x1_all[:, :, :], dr["x1"].rearrange("(t p) d -> p t d", p=P)).then_inc(x1_in, 16)
            for g in range(NG):
                sp.wait_ge(summed, GT * (g + 1))
                sp.dma_start(dr["out"][g * GW:(g + 1) * GW, :].rearrange("(t p) d -> p t d", p=P),
                             y_all[:, g * GT:(g + 1) * GT, :]).then_inc(stored, 16)
            sp.wait_ge(stored, 16 * NG)


def phase_rest(nc, T, dr, phases):
    with ExitStack() as ctx:
        def sb(name, shape, dt=F32):
            return ctx.enter_context(nc.sbuf_tensor(name, shape, dt))

        for w in ("w1h", "w1l"):
            T[w] = sb(w, [P, E, KC, FF], F16)
        for w in ("w2h", "w2l"):
            T[w] = sb(w, [P, E, FC, D], F16)
        T["pos"] = sb("pos", [P, NT], U32)
        T["gw"] = sb("gw", [P, NT])
        T["slot_e"] = sb("slot_e", [P, SLOTS], I32)
        T["b1_t"] = sb("b1_t", [P, E, FC])
        with ExitStack() as inner:
            for name in ("o_stored", "w_in"):
                T[name] = inner.enter_context(nc.semaphore(name))
            for name, shape in (("bv_col", [P, KC]), ("wo", [P, KC, D]), ("gate_w", [P, KC, E]), ("gate_b", [P, E]),
                                ("b1_rows", [E * FC, P]), ("o_unit", [P, P])):
                T[name] = inner.enter_context(nc.sbuf_tensor(name + "_t", shape, F32))
            T["rows"] = {n: inner.enter_context(nc.sbuf_tensor("row_" + n, [P, D], F32)) for n in ("bo", "ln_g", "ln_b")}
            phase_attend(nc, T, dr)
            if "C" in phases:
                T["b2_bc"] = inner.enter_context(nc.sbuf_tensor("b2_bc", [P, E, D], F32))
                phase_route(nc, T, dr)
            if "D" in phases:
                phase_experts(nc, T, dr)
        if "E" in phases:
            phase_return(nc, T, dr)


def build(nc, a, out, phases="ABCDE"):
    with ExitStack() as ctx:
        def sb(name, shape, dt=F32):
            return ctx.enter_context(nc.sbuf_tensor(name, shape, dt))

        dr = dict(a)
        dr["out"] = out
        for name, shape, dt in (("x1", (N, D), F32), ("xn2", (N, D), F32), ("qh", (2, D, N), F16), ("kh", (2, D, N), F16), ("ot", (NG, GT, D, P), F32),
                                ("hs", (SLOTS * P, D), F32), ("ys", (SLOTS * P, D), F32)):
            dr[name] = nc.dram_tensor(name + "_scratch", shape, dt).ap()
        T = {"ident": sb("ident", [P, P]), "v_all": sb("v_all", [P, NT, H, HD]),
             "minus_half": sb("minus_half", [P, NT]),
             "hs_cleared": ctx.enter_context(nc.semaphore("hs_cleared"))}
        phase_project(nc, T, dr)
        if "B" in phases:
            phase_rest(nc, T, dr, phases)


_INS = {"x": "x", "adj": "adj", "L0_gnn_w_self": "w_self", "L0_gnn_w_neigh": "w_neigh", "L0_ffn_ln1_g": "ln_g",
        "L0_ffn_ln1_b": "ln_b", "L0_ffn_Wq": "Wq", "L0_ffn_bq": "bq", "L0_ffn_Wk": "Wk", "L0_ffn_bk": "bk",
        "L0_ffn_Wv": "Wv", "L0_ffn_bv": "bv", "L0_ffn_Wo": "Wo", "L0_ffn_bo": "bo", "L0_ffn_gate_W": "gate_W",
        "L0_ffn_gate_b": "gate_b", "L0_ffn_W1": "W1", "L0_ffn_b1": "b1", "L0_ffn_W2": "W2", "L0_ffn_b2": "b2"}


def kernel(**inputs):
    import numpy as np
    import concourse.bacc as bacc
    from concourse.bass_utils import run_bass_kernel_spmd

    nc = bacc.Bacc("TRN2", target_bir_lowering=False, num_devices=1)
    arrays, aps = {}, {}
    for name, short in _INS.items():
        arr = np.ascontiguousarray(inputs[name])
        arrays["in_" + short] = arr
        aps[short] = nc.dram_tensor("in_" + short, arr.shape, mybir.dt.from_np(arr.dtype), kind="ExternalInput").ap()
    out = nc.dram_tensor("out", (N, D), F32, kind="ExternalOutput").ap()
    build(nc, aps, out)
    r = run_bass_kernel_spmd(nc, [arrays], core_ids=[0])
    return r.results[0]["out"]
```
